# Optimizing a Trainium2 kernel written in Bass

```python
import numpy as np
import jax
import jax.numpy as jnp

def _softmax(x, axis=-1):
    return jax.nn.softmax(x, axis=axis)

def _gelu(x):
    return jax.nn.gelu(x, approximate=True)

def _silu(x):
    return jax.nn.silu(x)

def _sigmoid(x):
    return jax.nn.sigmoid(x)

def _layernorm(x, axis=-1, eps=1e-05):
    m = jnp.mean(x, axis=axis, keepdims=True)
    v = jnp.var(x, axis=axis, keepdims=True)
    return (x - m) / jnp.sqrt(v + eps)

def _scatter_add(tgt, idx, src, axis=0):
    return tgt.at[idx].add(src)

def _segment_sum(src, seg, n):
    return jax.ops.segment_sum(src, seg, n)
kernel_name = 'mk_decoder_preln_d2_seqx_r8_c05b1f'

def setup_inputs(seed: int=0):
    np.random.seed(seed)
    _w = jnp.asarray

    def _rec_inputs():
        import jax
        import jax.numpy as jnp
        _rk = jax.random.key(seed)
        x = 0.5 + 0.2887 * jax.random.normal(jax.random.fold_in(_rk, 1), (4, 256, 256), jnp.float32)
        _lenS = 256 - jax.random.randint(jax.random.fold_in(_rk, 7), (4,), 0, max(1, 256 // 4) + 1, jnp.int32)
        _lenS2 = 256 - jax.random.randint(jax.random.fold_in(_rk, 8), (4,), 0, max(1, 256 // 4) + 1, jnp.int32)
        _ctx_512P = jax.random.normal(jax.random.fold_in(_rk, 11), (4, 16, 64), jnp.float32)
        _ctx_512c = jax.random.dirichlet(jax.random.fold_in(_rk, 511), 0.3 * jnp.ones((16,), jnp.float32), (4, 256))
        _ctx_512t = jnp.einsum('bsk,bkd->bsd', _ctx_512c, _ctx_512P)
        _ctx_512t = _ctx_512t * jax.lax.rsqrt(jnp.mean(jnp.square(_ctx_512t)) + 1e-12) * 0.953939
        ctx_512 = 7.22013e-05 + 1.00017 * (_ctx_512t + 0.3 * jax.random.normal(jax.random.fold_in(_rk, 611), (4, 256, 64), jnp.float32))
        return (x, ctx_512)
    x, ctx_512 = _rec_inputs()

    def _L0_attn_setup():
        import jax, jax.numpy as jnp
        import numpy as np
        EPS = 1e-05
        CHUNK = 128

        def lightning_attn(q, k, v, ld, chunk=CHUNK):
            b, n, h, d = q.shape
            nc = n // chunk
            idx = jnp.arange(chunk)
            diff = idx[:, None] - idx[None, :]
            mask = diff >= 0
            D = jnp.exp(ld[:, None, None] * jnp.where(mask, diff, 0)) * mask
            q_decay = jnp.exp(ld[None, :] * (idx + 1)[:, None])
            k_decay = jnp.exp(ld[None, :] * (chunk - 1 - idx)[:, None])
            chunk_decay = jnp.exp(ld * chunk)
            qc = jnp.moveaxis(q.reshape(b, nc, chunk, h, d), 1, 0)
            kc = jnp.moveaxis(k.reshape(b, nc, chunk, h, d), 1, 0)
            vc = jnp.moveaxis(v.reshape(b, nc, chunk, h, d), 1, 0)

            def step(S, inp):
                qb, kb, vb = inp
                scores = jnp.einsum('bchd,bshd->bhcs', qb, kb) * D[None]
                o_intra = jnp.einsum('bhcs,bshd->bchd', scores, vb)
                o_inter = jnp.einsum('bchd,bhde->bche', qb, S) * q_decay[None, :, :, None]
                S_new = chunk_decay[None, :, None, None] * S + jnp.einsum('bshd,bshe->bhde', kb * k_decay[None, :, :, None], vb)
                return (S_new, o_intra + o_inter)
            S0 = jnp.zeros((b, h, d, d), dtype=q.dtype)
            S_final, oc = jax.lax.scan(step, S0, (qc, kc, vc))
            out = jnp.moveaxis(oc, 0, 1).reshape(b, n, h, d)
            return (out, S_final)

        def group_rmsnorm_fused_gate(o, gate, w, num_heads):
            b, n, d = o.shape
            hd = d // num_heads
            o = o * jax.nn.sigmoid(gate)
            og = o.reshape(b, n, num_heads, hd)
            og = og * jax.lax.rsqrt(jnp.mean(og * og, axis=-1, keepdims=True) + EPS)
            return og.reshape(b, n, d) * w
        key = jax.random.key(seed)
        ks = jax.random.split(key, 10)
        B, N, D, H = (2, 512, 256, 16)
        HD = D // H
        s = 1.0 / np.sqrt(D)
        x = jax.random.normal(ks[0], (B, N, D), dtype=jnp.float32)
        log_decay = -jax.random.uniform(ks[1], (H,), dtype=jnp.float32, minval=0.01, maxval=1.0)
        Wq = jax.random.normal(ks[2], (D, D), dtype=jnp.float32) * s
        Wk = jax.random.normal(ks[3], (D, D), dtype=jnp.float32) * s
        Wv = jax.random.normal(ks[4], (D, D), dtype=jnp.float32) * s
        Wo = jax.random.normal(ks[5], (D, D), dtype=jnp.float32) * s
        Wg1 = jax.random.normal(ks[6], (D, HD), dtype=jnp.float32) * s
        Wg2 = jax.random.normal(ks[7], (HD, D), dtype=jnp.float32) / np.sqrt(HD)
        norm_w = jnp.ones((D,), dtype=jnp.float32)
        return {'x': x, 'log_decay': log_decay, 'Wq': Wq, 'Wk': Wk, 'Wv': Wv, 'Wo': Wo, 'Wg1': Wg1, 'Wg2': Wg2, 'norm_w': norm_w}
    _L0_attn_all = _L0_attn_setup()
    _L0_attn_in = {k: v for k, v in _L0_attn_all.items() if k in ('log_decay', 'Wq', 'Wk', 'Wv', 'Wo', 'Wg1', 'Wg2', 'norm_w')}
    del _L0_attn_all

    def _L0_xattn_setup():
        import jax, jax.numpy as jnp
        import numpy as np
        P_ASEM = 0.6
        key = jax.random.key(seed)
        k1, k2, k3 = jax.random.split(key, 3)
        B, N, D = (8, 256, 64)
        x = jax.random.normal(k1, (B, N, D), dtype=jnp.float32)
        adj = jax.random.uniform(k2, (B, N, N), dtype=jnp.float32)
        bound = 1.0 / np.sqrt(2 * D)
        W = jax.random.uniform(k3, (1, 2 * D), dtype=jnp.float32, minval=-bound, maxval=bound)
        b = jnp.zeros((1,), dtype=jnp.float32)
        return {'x': x, 'adj': adj, 'W': W, 'b': b}
    _L0_xattn_all = _L0_xattn_setup()
    _L0_xattn_in = {k: v for k, v in _L0_xattn_all.items() if k in ('W', 'b')}
    del _L0_xattn_all

    def _L0_ffn_setup():
        import jax, jax.numpy as jnp
        import numpy as np
        H, I, E, TOP_K = (256, 176, 16, 6)
        IS = 352
        NORM_TOPK_PROB = False

        def _silu_and_mul(gate_up):
            d = gate_up.shape[-1] // 2
            g, u = (gate_up[..., :d], gate_up[..., d:])
            return jax.nn.silu(g) * u
        key = jax.random.key(seed)
        ks = jax.random.split(key, 6)
        s = 0.02
        return {'x': jax.random.normal(ks[0], (1, 256, H), jnp.float32), 'gate_w': jax.random.normal(ks[1], (E, H), jnp.float32) * s, 'w1': jax.random.normal(ks[2], (E, 2 * I, H), jnp.float32) * s, 'w2': jax.random.normal(ks[3], (E, H, I), jnp.float32) * s, 'shared_w1': jax.random.normal(ks[4], (2 * IS, H), jnp.float32) * s, 'shared_w2': jax.random.normal(ks[5], (H, IS), jnp.float32) * s}
    _L0_ffn_all = _L0_ffn_setup()
    _L0_ffn_in = {k: v for k, v in _L0_ffn_all.items() if k in ('gate_w', 'w1', 'w2', 'shared_w1', 'shared_w2')}
    del _L0_ffn_all

    def _L1_attn_setup():
        import jax, jax.numpy as jnp
        import numpy as np
        D_MODEL = 256
        NUM_HEADS = 16
        D_K = D_MODEL // NUM_HEADS
        SEQ = 256
        BATCH = 2
        THETA = 10000.0

        def _rope_tables(seq_len, d_k, theta, dtype):
            pos = jnp.arange(seq_len, dtype=dtype)[:, None]
            inv = theta ** (-(jnp.arange(0, d_k, 2, dtype=dtype) / d_k))
            ang = pos * inv
            sin = jnp.repeat(jnp.sin(ang), 2, axis=1)
            cos = jnp.repeat(jnp.cos(ang), 2, axis=1)
            return (sin, cos)

        def _apply_rope(x, sin, cos):
            xp = x.reshape(x.shape[:-1] + (x.shape[-1] // 2, 2))
            swapped = jnp.stack((-xp[..., 1], xp[..., 0]), axis=-1).reshape(x.shape)
            return x * cos + swapped * sin
        key = jax.random.key(seed)
        ks = jax.random.split(key, 5)
        s = 1.0 / np.sqrt(D_MODEL)
        return {'x': jax.random.normal(ks[0], (BATCH, SEQ, D_MODEL), jnp.float32), 'wq': jax.random.normal(ks[1], (D_MODEL, D_MODEL), jnp.float32) * s, 'wk': jax.random.normal(ks[2], (D_MODEL, D_MODEL), jnp.float32) * s, 'wv': jax.random.normal(ks[3], (D_MODEL, D_MODEL), jnp.float32) * s, 'wo': jax.random.normal(ks[4], (D_MODEL, D_MODEL), jnp.float32) * s}
    _L1_attn_all = _L1_attn_setup()
    _L1_attn_in = {k: v for k, v in _L1_attn_all.items() if k in ('wq', 'wk', 'wv', 'wo')}
    del _L1_attn_all

    def _L1_xattn_setup():
        import jax, jax.numpy as jnp
        import numpy as np
        B, S, L = (2, 128, 128)
        DIM_Q, H, K, D_C, D_CQ, R = (256, 16, 128, 64, 192, 64)

        def _rope_tables(length, dim):
            inv = 1.0 / 10000.0 ** (jnp.arange(0, dim, 2, dtype=jnp.float32) / dim)
            f = jnp.arange(length, dtype=jnp.float32)[:, None] * inv[None, :]
            sin = jnp.repeat(jnp.sin(f), 2, axis=-1)
            cos = jnp.repeat(jnp.cos(f), 2, axis=-1)
            return (sin, cos)

        def _rotate_half(x):
            half = x.shape[-1] // 2
            return jnp.concatenate([-x[..., half:], x[..., :half]], axis=-1)

        def _apply_rope(x, sin, cos):
            return x * cos + _rotate_half(x) * sin
        key = jax.random.key(seed)
        ks = jax.random.split(key, 8)
        return {'hidden_q': jax.random.normal(ks[0], (B, S, DIM_Q), jnp.float32), 'kv_c': jax.random.normal(ks[1], (B, L, D_C), jnp.float32), 'Wq': jax.random.normal(ks[2], (H * K, DIM_Q), jnp.float32) / np.sqrt(DIM_Q).astype(np.float32), 'w_kc_q': jax.random.normal(ks[3], (H, K, D_CQ), jnp.float32) / np.sqrt(K).astype(np.float32), 'w_kc_kv': jax.random.normal(ks[4], (H, K, D_C), jnp.float32) / np.sqrt(K).astype(np.float32), 'W_qr': jax.random.normal(ks[5], (H, D_CQ, R), jnp.float32) / np.float32(np.sqrt(D_CQ) * np.sqrt(R)), 'W_kr': jax.random.normal(ks[6], (H, D_C, R), jnp.float32) / np.sqrt(D_C).astype(np.float32), 'Wo': jax.random.normal(ks[7], (DIM_Q, H * K), jnp.float32) / np.sqrt(H * K).astype(np.float32)}
    _L1_xattn_all = _L1_xattn_setup()
    _L1_xattn_in = {k: v for k, v in _L1_xattn_all.items() if k in ('Wq', 'w_kc_q', 'w_kc_kv', 'W_qr', 'W_kr', 'Wo')}
    del _L1_xattn_all

    def _L1_ffn_setup():
        import jax, jax.numpy as jnp
        import numpy as np
        from jax import lax
        H = 256
        I = 176
        E = 16
        TOP_K = 6
        IS = 2 * I

        def _swiglu(x, w13_, w2_):
            gu = x @ w13_.T
            g, u = jnp.split(gu, 2, axis=-1)
            return jax.nn.silu(g) * u @ w2_.T
        key = jax.random.key(seed)
        ks = jax.random.split(key, 6)
        return {'hidden_states': jax.random.normal(ks[0], (1, 256, H), jnp.float32), 'gate_w': jax.random.normal(ks[1], (E, H), jnp.float32) * 0.02, 'w13': jax.random.normal(ks[2], (E, 2 * I, H), jnp.float32) * 0.02, 'w2': jax.random.normal(ks[3], (E, H, I), jnp.float32) * 0.02, 'sw13': jax.random.normal(ks[4], (2 * IS, H), jnp.float32) * 0.02, 'sw2': jax.random.normal(ks[5], (H, IS), jnp.float32) * 0.02}
    _L1_ffn_all = _L1_ffn_setup()
    _L1_ffn_in = {k: v for k, v in _L1_ffn_all.items() if k in ('gate_w', 'w13', 'w2', 'sw13', 'sw2')}
    del _L1_ffn_all
    return {'x': x, 'ctx_512': ctx_512, 'L0_attn_log_decay': _L0_attn_in['log_decay'], 'L0_attn_Wq': _L0_attn_in['Wq'], 'L0_attn_Wk': _L0_attn_in['Wk'], 'L0_attn_Wv': _L0_attn_in['Wv'], 'L0_attn_Wo': _L0_attn_in['Wo'], 'L0_attn_Wg1': _L0_attn_in['Wg1'], 'L0_attn_Wg2': _L0_attn_in['Wg2'], 'L0_attn_norm_w': _L0_attn_in['norm_w'], 'L0_xattn_W': _L0_xattn_in['W'], 'L0_xattn_b': _L0_xattn_in['b'], 'L0_ffn_gate_w': _L0_ffn_in['gate_w'], 'L0_ffn_w1': _L0_ffn_in['w1'], 'L0_ffn_w2': _L0_ffn_in['w2'], 'L0_ffn_shared_w1': _L0_ffn_in['shared_w1'], 'L0_ffn_shared_w2': _L0_ffn_in['shared_w2'], 'L1_attn_wq': _L1_attn_in['wq'], 'L1_attn_wk': _L1_attn_in['wk'], 'L1_attn_wv': _L1_attn_in['wv'], 'L1_attn_wo': _L1_attn_in['wo'], 'L1_xattn_Wq': _L1_xattn_in['Wq'], 'L1_xattn_w_kc_q': _L1_xattn_in['w_kc_q'], 'L1_xattn_w_kc_kv': _L1_xattn_in['w_kc_kv'], 'L1_xattn_W_qr': _L1_xattn_in['W_qr'], 'L1_xattn_W_kr': _L1_xattn_in['W_kr'], 'L1_xattn_Wo': _L1_xattn_in['Wo'], 'L1_ffn_gate_w': _L1_ffn_in['gate_w'], 'L1_ffn_w13': _L1_ffn_in['w13'], 'L1_ffn_w2': _L1_ffn_in['w2'], 'L1_ffn_sw13': _L1_ffn_in['sw13'], 'L1_ffn_sw2': _L1_ffn_in['sw2']}

def reference(x, ctx_512, L0_attn_log_decay, L0_attn_Wq, L0_attn_Wk, L0_attn_Wv, L0_attn_Wo, L0_attn_Wg1, L0_attn_Wg2, L0_attn_norm_w, L0_xattn_W, L0_xattn_b, L0_ffn_gate_w, L0_ffn_w1, L0_ffn_w2, L0_ffn_shared_w1, L0_ffn_shared_w2, L1_attn_wq, L1_attn_wk, L1_attn_wv, L1_attn_wo, L1_xattn_Wq, L1_xattn_w_kc_q, L1_xattn_w_kc_kv, L1_xattn_W_qr, L1_xattn_W_kr, L1_xattn_Wo, L1_ffn_gate_w, L1_ffn_w13, L1_ffn_w2, L1_ffn_sw13, L1_ffn_sw2):
    import jax
    import jax.numpy as jnp

    def _L0_attn_ref(x, log_decay, Wq, Wk, Wv, Wo, Wg1, Wg2, norm_w):
        import jax, jax.numpy as jnp
        import numpy as np
        EPS = 1e-05
        CHUNK = 128

        def lightning_attn(q, k, v, ld, chunk=CHUNK):
            b, n, h, d = q.shape
            nc = n // chunk
            idx = jnp.arange(chunk)
            diff = idx[:, None] - idx[None, :]
            mask = diff >= 0
            D = jnp.exp(ld[:, None, None] * jnp.where(mask, diff, 0)) * mask
            q_decay = jnp.exp(ld[None, :] * (idx + 1)[:, None])
            k_decay = jnp.exp(ld[None, :] * (chunk - 1 - idx)[:, None])
            chunk_decay = jnp.exp(ld * chunk)
            qc = jnp.moveaxis(q.reshape(b, nc, chunk, h, d), 1, 0)
            kc = jnp.moveaxis(k.reshape(b, nc, chunk, h, d), 1, 0)
            vc = jnp.moveaxis(v.reshape(b, nc, chunk, h, d), 1, 0)

            def step(S, inp):
                qb, kb, vb = inp
                scores = jnp.einsum('bchd,bshd->bhcs', qb, kb) * D[None]
                o_intra = jnp.einsum('bhcs,bshd->bchd', scores, vb)
                o_inter = jnp.einsum('bchd,bhde->bche', qb, S) * q_decay[None, :, :, None]
                S_new = chunk_decay[None, :, None, None] * S + jnp.einsum('bshd,bshe->bhde', kb * k_decay[None, :, :, None], vb)
                return (S_new, o_intra + o_inter)
            S0 = jnp.zeros((b, h, d, d), dtype=q.dtype)
            S_final, oc = jax.lax.scan(step, S0, (qc, kc, vc))
            out = jnp.moveaxis(oc, 0, 1).reshape(b, n, h, d)
            return (out, S_final)

        def group_rmsnorm_fused_gate(o, gate, w, num_heads):
            b, n, d = o.shape
            hd = d // num_heads
            o = o * jax.nn.sigmoid(gate)
            og = o.reshape(b, n, num_heads, hd)
            og = og * jax.lax.rsqrt(jnp.mean(og * og, axis=-1, keepdims=True) + EPS)
            return og.reshape(b, n, d) * w
        b, n, d = x.shape
        H = log_decay.shape[0]
        hd = d // H
        q = jax.nn.silu(jnp.einsum('bnd,de->bne', x, Wq).reshape(b, n, H, hd))
        k = jax.nn.silu(jnp.einsum('bnd,de->bne', x, Wk).reshape(b, n, H, hd))
        v = jax.nn.silu(jnp.einsum('bnd,de->bne', x, Wv).reshape(b, n, H, hd))
        o, _ = lightning_attn(q, k, v, log_decay)
        o = o.reshape(b, n, d)
        gate = jnp.einsum('bnk,kd->bnd', jnp.einsum('bnd,dk->bnk', x, Wg1), Wg2)
        o = group_rmsnorm_fused_gate(o, gate, norm_w, H)
        return jnp.einsum('bnd,de->bne', o, Wo)

    def _L0_xattn_ref(x, adj, W, b):
        import jax, jax.numpy as jnp
        import numpy as np
        P_ASEM = 0.6
        D = x.shape[-1]
        Wi = W[:, :D]
        Wj = W[:, D:]
        si = jnp.einsum('bnd,d->bn', x, Wi[0])
        sj = jnp.einsum('bnd,d->bn', x, Wj[0])
        xij = jax.nn.sigmoid(si[:, :, None] + sj[:, None, :] + b[0])
        return P_ASEM * xij + (1.0 - P_ASEM) * adj

    def _L0_ffn_ref(x, gate_w, w1, w2, shared_w1, shared_w2):
        import jax, jax.numpy as jnp
        import numpy as np
        H, I, E, TOP_K = (256, 176, 16, 6)
        IS = 352
        NORM_TOPK_PROB = False

        def _silu_and_mul(gate_up):
            d = gate_up.shape[-1] // 2
            g, u = (gate_up[..., :d], gate_up[..., d:])
            return jax.nn.silu(g) * u
        B, S, Hd = x.shape
        xf = x.reshape(-1, Hd)
        T = xf.shape[0]
        shared_out = _silu_and_mul(xf @ shared_w1.T) @ shared_w2.T
        logits = xf @ gate_w.T
        probs = jax.nn.softmax(logits.astype(jnp.float32), axis=-1)
        routing_weights, selected = jax.lax.top_k(probs, TOP_K)
        if NORM_TOPK_PROB:
            routing_weights = routing_weights / routing_weights.sum(-1, keepdims=True)
        combine = jnp.zeros((T, E), jnp.float32).at[jnp.arange(T)[:, None], selected].add(routing_weights).astype(x.dtype)
        gate_up = jnp.einsum('th,eoh->teo', xf, w1)
        act = _silu_and_mul(gate_up)
        moe_out = jnp.einsum('te,tei,ehi->th', combine, act, w2)
        return (moe_out + shared_out).reshape(B, S, Hd)

    def _L1_attn_ref(x, wq, wk, wv, wo):
        import jax, jax.numpy as jnp
        import numpy as np
        D_MODEL = 256
        NUM_HEADS = 16
        D_K = D_MODEL // NUM_HEADS
        SEQ = 256
        BATCH = 2
        THETA = 10000.0

        def _rope_tables(seq_len, d_k, theta, dtype):
            pos = jnp.arange(seq_len, dtype=dtype)[:, None]
            inv = theta ** (-(jnp.arange(0, d_k, 2, dtype=dtype) / d_k))
            ang = pos * inv
            sin = jnp.repeat(jnp.sin(ang), 2, axis=1)
            cos = jnp.repeat(jnp.cos(ang), 2, axis=1)
            return (sin, cos)

        def _apply_rope(x, sin, cos):
            xp = x.reshape(x.shape[:-1] + (x.shape[-1] // 2, 2))
            swapped = jnp.stack((-xp[..., 1], xp[..., 0]), axis=-1).reshape(x.shape)
            return x * cos + swapped * sin
        B, S, D = x.shape
        H, dk = (NUM_HEADS, D_K)
        q = jnp.einsum('bsd,hkd->bhsk', x, wq.reshape(H, dk, D))
        k = jnp.einsum('bsd,hkd->bhsk', x, wk.reshape(H, dk, D))
        v = jnp.einsum('bsd,hkd->bhsk', x, wv.reshape(H, dk, D))
        sin, cos = _rope_tables(S, dk, THETA, x.dtype)
        q = _apply_rope(q, sin, cos)
        k = _apply_rope(k, sin, cos)
        scores = jnp.einsum('bhqk,bhsk->bhqs', q, k) / jnp.sqrt(jnp.asarray(dk, x.dtype))
        causal = jnp.triu(jnp.ones((S, S), dtype=bool), k=1)
        scores = jnp.where(causal, -jnp.inf, scores)
        attn = jax.nn.softmax(scores, axis=-1)
        out = jnp.einsum('bhqs,bhsv->bqhv', attn, v).reshape(B, S, H * dk)
        return jnp.einsum('bsf,df->bsd', out, wo)

    def _L1_xattn_ref(hidden_q, kv_c, Wq, w_kc_q, w_kc_kv, W_qr, W_kr, Wo):
        import jax, jax.numpy as jnp
        import numpy as np
        B, S, L = (2, 128, 128)
        DIM_Q, H, K, D_C, D_CQ, R = (256, 16, 128, 64, 192, 64)

        def _rope_tables(length, dim):
            inv = 1.0 / 10000.0 ** (jnp.arange(0, dim, 2, dtype=jnp.float32) / dim)
            f = jnp.arange(length, dtype=jnp.float32)[:, None] * inv[None, :]
            sin = jnp.repeat(jnp.sin(f), 2, axis=-1)
            cos = jnp.repeat(jnp.cos(f), 2, axis=-1)
            return (sin, cos)

        def _rotate_half(x):
            half = x.shape[-1] // 2
            return jnp.concatenate([-x[..., half:], x[..., :half]], axis=-1)

        def _apply_rope(x, sin, cos):
            return x * cos + _rotate_half(x) * sin
        Bv, Sv, _ = hidden_q.shape
        _, Lv, _ = kv_c.shape
        q_hk = (hidden_q @ Wq.T).reshape(Bv, Sv, H, K)
        q_big = jnp.einsum('bshk,hkq->bshq', q_hk, w_kc_q)
        sin_q, cos_q = _rope_tables(Sv, D_CQ)
        q_big = _apply_rope(q_big, sin_q[None, :, None, :], cos_q[None, :, None, :])
        sin_k, cos_k = _rope_tables(Lv, D_C)
        kv_r = _apply_rope(kv_c, sin_k[None], cos_k[None])
        q_r = jnp.einsum('bshq,hqr->bhsr', q_big, W_qr)
        k_r = jnp.einsum('bld,hdr->bhlr', kv_r, W_kr)
        scores = jnp.einsum('bhsr,bhlr->bhsl', q_r, k_r)
        attn = jax.nn.softmax(scores, axis=-1)
        ctx_c = jnp.einsum('bhsl,bld->bhsd', attn, kv_r)
        ctx_lat = jnp.einsum('bhsd,hkd->bhsk', ctx_c, w_kc_kv)
        ctx = ctx_lat.transpose(0, 2, 1, 3).reshape(Bv, Sv, H * K)
        return ctx @ Wo.T

    def _L1_ffn_ref(hidden_states, gate_w, w13, w2, sw13, sw2):
        import jax, jax.numpy as jnp
        import numpy as np
        from jax import lax
        H = 256
        I = 176
        E = 16
        TOP_K = 6
        IS = 2 * I

        def _swiglu(x, w13_, w2_):
            gu = x @ w13_.T
            g, u = jnp.split(gu, 2, axis=-1)
            return jax.nn.silu(g) * u @ w2_.T
        B, S, Hd = hidden_states.shape
        x = hidden_states.reshape(-1, Hd)
        T = x.shape[0]
        scores = jax.nn.softmax(x @ gate_w.T, axis=-1)
        topk_w, topk_ids = lax.top_k(scores, TOP_K)
        topk_w = topk_w / (topk_w.sum(-1, keepdims=True) + 1e-20)
        combine = jnp.einsum('tk,tke->te', topk_w, jax.nn.one_hot(topk_ids, E, dtype=topk_w.dtype))

        def body(acc, ew):
            w13_e, w2_e, c_e = ew
            y = _swiglu(x, w13_e, w2_e)
            return (acc + c_e[:, None] * y, None)
        out, _ = lax.scan(body, jnp.zeros_like(x), (w13, w2, combine.T))
        out = out + _swiglu(x, sw13, sw2)
        return out.reshape(B, S, Hd)
    x = x + _L0_attn_ref(_layernorm(x, axis=-1), L0_attn_log_decay, L0_attn_Wq, L0_attn_Wk, L0_attn_Wv, L0_attn_Wo, L0_attn_Wg1, L0_attn_Wg2, L0_attn_norm_w)
    x = x + _L0_xattn_ref(ctx_512, _layernorm(x, axis=-1), L0_xattn_W, L0_xattn_b)
    x = x + _L0_ffn_ref(_layernorm(x, axis=-1), L0_ffn_gate_w, L0_ffn_w1, L0_ffn_w2, L0_ffn_shared_w1, L0_ffn_shared_w2)
    x = x + _L1_attn_ref(_layernorm(x, axis=-1), L1_attn_wq, L1_attn_wk, L1_attn_wv, L1_attn_wo)
    x = x + _L1_xattn_ref(_layernorm(x, axis=-1), ctx_512, L1_xattn_Wq, L1_xattn_w_kc_q, L1_xattn_w_kc_kv, L1_xattn_W_qr, L1_xattn_W_kr, L1_xattn_Wo)
    x = x + _L1_ffn_ref(_layernorm(x, axis=-1), L1_ffn_gate_w, L1_ffn_w13, L1_ffn_w2, L1_ffn_sw13, L1_ffn_sw2)
    return x

_drawn_inputs = setup_inputs


def setup_inputs(seed=0):
    import zlib

    import numpy as np

    out = dict(_drawn_inputs(seed))
    spreads = {'L0_attn_norm_w': (1.0, 0.2)}
    factors = {'L0_ffn_gate_w': 8.0,
     'L0_ffn_w1': 8.0,
     'L0_ffn_w2': 8.0,
     'L0_ffn_shared_w1': 4.947,
     'L0_ffn_shared_w2': 4.905,
     'L1_ffn_gate_w': 8.0,
     'L1_ffn_w13': 8.0,
     'L1_ffn_w2': 8.0,
     'L1_ffn_sw13': 5.158,
     'L1_ffn_sw2': 5.158}
    for name, (base, spread) in spreads.items():
        noise = np.random.default_rng([zlib.crc32(name.encode()), seed]).standard_normal(out[name].shape)
        drawn = base * np.exp(spread * noise) if base else spread * noise
        out[name] = jnp.asarray(drawn.astype(out[name].dtype))
    for name, factor in factors.items():
        out[name] = (out[name] * factor).astype(out[name].dtype)
    return out
```

```python
from contextlib import ExitStack

import numpy as np

import concourse.bass as bass
from concourse import mybir

F32 = mybir.dt.float32
F32R = mybir.dt.float32r
BF16 = mybir.dt.bfloat16
ALU = mybir.AluOpType
ACT = mybir.ActivationFunctionType
AX = mybir.AxisListType.X

P = 128
D = 256
NB, SEQ = 4, 256
TILES = NB * SEQ // P
KD = D // P
HEADS, HD = 16, 16
EPS = 1e-5
NEG = -1e30
HALF = 512

E, TOP_K, INNER, SHARED = 16, 6, 176, 352
CHUNKS = -(-(E * INNER + SHARED) // P)
PACK = 4 * 128 + 256 + 128
RING = 5

XH, XK, XQ, XR, XC = 16, 128, 192, 64, 64
GROUPS = XH // 4
LO = XQ // 2

def pack_layout():
    at, n = {}, 0
    for name, width in (("wq", 4 * D), ("kcq", 4 * XQ), ("qrT", 2 * 4 * LO), ("krT", 4 * XC), ("kckv", 4 * XC), ("woT", 4 * D)):
        at[name] = (n, n + width)
        n += width
    return at, n


XP, XPACK = pack_layout()


def cx_layout():
    at, n = {}, 0
    for name, width in (("cosq", 3 * 2 * SEQ), ("sinq", 3 * 2 * SEQ), ("coskv", SEQ), ("sinkv", SEQ), ("gmask", 6), ("slot2", 2)):
        at[name] = (n, n + width)
        n += width
    return at, n


CX, CX_W = cx_layout()

STAGES = 6


def const_layout():
    at, n = {}, 0
    for name, width in (("ident", 128), ("dist", SEQ), ("causal", SEQ), ("neg_qs", 128), ("neg_sq", 128),
                        ("even", 1), ("odd", 1), ("slot", 4), ("block_ones", 128), ("pick16", 128), ("ones", 128),
                        ("cos", SEQ), ("sin", SEQ)):
        at[name] = (n, n + width)
        n += width
    return at, n


CONST, CONST_W = const_layout()


def build(nc, d, out, stages):
    with ExitStack() as ctx:
        def sb(name, shape, dt=F32, c=ctx):
            return c.enter_context(nc.sbuf_tensor(name, shape, dt))

        def sem(name):
            return ctx.enter_context(nc.semaphore(name))

        ps = ctx.enter_context(nc.psum_tensor("ps", [P, 8, 512], F32))

        X = sb("X", [P, TILES, D])
        xn = sb("xn", [P, TILES, D])
        cst = sb("cst", [P, CONST_W])
        stats = sb("stats", [P, TILES, 6])
        mv = sb("mv", [P, TILES, 2])
        sd = sb("sd", [P, TILES])
        rstd = sb("rstd", [P, TILES])
        epsc = sb("epsc", [P, 1])

        def k(name):
            a, b = CONST[name]
            return cst[:, a:b]

        ident = k("ident")

        a_ctx = ctx.enter_context(ExitStack())
        xT = sb("xT", [P, KD, SEQ])
        wqkv0 = sb("wqkv0", [P, 3, KD, D])
        wg1 = sb("wg1", [P, KD, HD])
        wg2 = sb("wg2", [HD, 4, 128])
        wo_gap = sb("wo_gap", [P, 2, 4, D])
        normw = sb("normw", [P, 4])
        ld_bc = sb("ld_bc", [P, HEADS])
        xT4 = sb("xT4", [P, KD, NB, SEQ])
        xb_l, xb_r = xT4[:, 0], xT4[:, 1]
        xb_b = sb("xb_b", [P, 1])
        wqkv1 = sb("wqkv1", [P, 5, KD, D])

        phase = ExitStack()
        with phase:
            DT = sb("DT", [P, HEADS, SEQ], c=phase)
            P0 = sb("P0", [P, 2, 4, 2, 256], c=phase)
            P1 = sb("P1", [P, 2, 4, 2, 128], c=phase)
            sg = sb("sg", [P, 4, 512], c=phase)
            qT = sb("qT", [P, 2, SEQ], c=phase)
            kT = sb("kT", [P, 2, SEQ], c=phase)
            kE = sb("kE", [P, 2, SEQ], c=phase)
            kO = sb("kO", [P, 2, SEQ], c=phase)
            vpad = sb("vpad", [P, 2, HEADS, 32], c=phase)
            g1S = sb("g1S", [HD, SEQ], c=phase)
            sgate = sb("sgate", [P, 2, 512], c=phase)
            og = sb("og", [P, 2, 512], c=phase)
            sq = sb("sq", [P, 2, 512], c=phase)
            rms = sb("rms", [P, 2, 512], c=phase)
            rrec = sb("rrec", [P, 2, 512], c=phase)
            on = sb("on", [P, 4, SEQ], c=phase)
            nm = sb("nm", [P, 2, 4, 32], c=phase)
            BD = sb("BD", [P, 4, SEQ], F32R, c=phase)
            onesr = sb("onesr", [P, 128], F32R, c=phase)
            identb = sb("identb", [P, 128], BF16, c=phase)
            negqs = sb("negqs", [P, 128], BF16, c=phase)
            negsq = sb("negsq", [P, 128], BF16, c=phase)
            xsig = sb("xsig", [P, 2, 256], c=phase)
        phase = ExitStack()
        with phase:
            xTh = sb("xTh", [P, KD, 2, HALF], F32R, c=phase)
            xTl = sb("xTl", [P, KD, 2, HALF], F32R, c=phase)
            raw = sb("raw", [P, RING, PACK], c=phase)
            whi = sb("whi", [P, RING, PACK], F32R, c=phase)
            wlo = sb("wlo", [P, RING, PACK - 128], F32R, c=phase)
            sl = sb("sl", [P, 2, HALF], c=phase)
            h1 = sb("h1", [P, 2, HALF], c=phase)
            h2 = sb("h2", [P, 2, HALF], c=phase)
            ahi = sb("ahi", [P, 2, HALF], F32R, c=phase)
            alo = sb("alo", [P, 2, HALF], F32R, c=phase)
            CT = sb("CT", [64, 2, HALF], F32R, c=phase)
            gwr = sb("gwr", [P, KD, E], c=phase)
            gwh = sb("gwh", [P, KD, E], F32R, c=phase)
            gwl = sb("gwl", [P, KD, E], F32R, c=phase)
            lgT = sb("lgT", [E, 2, HALF], c=phase)
            nmx = sb("nmx", [P, TILES], c=phase)
            lgs = sb("lgs", [P, TILES, E], c=phase)
            ex = sb("ex", [P, TILES, E], c=phase)
            den = sb("den", [P, 2, TILES], c=phase)
            prob = sb("prob", [P, TILES, 18], c=phase)
            v8 = sb("v8", [P, TILES, 8], c=phase)
            left = sb("left", [P, TILES, 18], c=phase)
            comb = sb("comb", [P, TILES, 17], c=phase)
            zeros = sb("zeros", [P, HALF], F32R, c=phase)
            yS = sb("yS", [P, 2, 2, HALF], c=phase)

        phase = ExitStack()
        with phase:
            Aw = sb("Aw", [P, GROUPS, KD, 2, 4 * LO], c=phase)
            Gm = sb("Gm", [P, GROUPS, 2, 4, 128], c=phase)
            MM = sb("MM", [P, GROUPS, 2, D], c=phase)
            cx = sb("cx", [P, CX_W], c=phase)
            rr = sb("rr", [P, 2 * 3 * 512], c=phase)
            kvT = sb("kvT", [P, NB, SEQ], c=phase)
            kvaug = sb("kvaug", [P, TILES, 2, 128], c=phase)
            r1, r2 = (rr[:, 1536 * n:1536 * n + 1536].rearrange("p (j s) -> p j s", j=3) for n in range(2))
            kvc = rr[:, 0:2 * NB * SEQ].rearrange("p (a b s) -> p a b s", a=2, b=NB)
            qr = sb("qr", [P, 3, 2, SEQ], c=phase)
            tS = sb("tS", [P, 2, SEQ], c=phase)
            nmq = sb("nmq", [P, 2, 2, 64], c=phase)
            BDx = sb("BDx", [P, 2, SEQ], F32R, c=phase)
            onesx = sb("onesx", [P, 128], F32R, c=phase)
            Px = sb("Px", [P, 2, 2, 512], c=phase)
            recx = sb("recx", [P, 512], c=phase)
            ctxS = sb("ctxS", [P, 2, SEQ], c=phase)
            wx = sb("wx", [P, 2, XPACK], c=phase)

        def kx(name):
            a, b = CX[name]
            return cx[:, a:b]

        x_loaded = [sem(f"x_loaded{b}") for b in range(NB)]
        const_loaded = sem("const_loaded")
        w_loaded = sem("w_loaded")
        x_done = sem("x_done")
        norm_stats, norm_var, norm_sd, norm_rstd, norm_done = map(sem, ("norm_stats", "norm_var", "norm_sd", "norm_rstd", "norm_done"))
        eps_ready = sem("eps_ready")
        setup_v = sem("setup_v")
        dt_exp = sem("dt_exp")
        dt_ready = sem("dt_ready")
        pe_xt, xt_ready, pe_q, pe_k, pe_v, pe_g1 = map(sem, ("pe_xt", "xt_ready", "pe_q", "pe_k", "pe_v", "pe_g1"))
        sig_done, g1_ready, q_ready, k_ready, v_ready = map(sem, ("sig_done", "g1_ready", "q_ready", "k_ready", "v_ready"))
        pe_gate, gate_ready, pe_s, p_done, pe_o = map(sem, ("pe_gate", "gate_ready", "pe_s", "p_done", "pe_o"))
        og_ready, sq_ready, pe_ss, rms_ready, rec_ready, on_ready, pe_out = map(
            sem, ("og_ready", "sq_ready", "pe_ss", "rms_ready", "rec_ready", "on_ready", "pe_out"))
        rope_done, k_sum, pe_m, max_done, pe_nmt, bd_ready = map(sem, ("rope_done", "k_sum", "pe_m", "max_done", "pe_nmt", "bd_ready"))
        pe_xb, xsig_ready, xb_part = map(sem, ("pe_xb", "xsig_ready", "xb_part"))
        out_done = sem("out_done")
        wx_in = [sem(f"wx_in{u}") for u in range(2)]
        cx_in, kvc_in = sem("cx_in"), sem("kvc_in")
        (x_zero, x_kvm, x_kv, x_pekv, x_kvt, x_pea, x_a, x_peg, x_g, x_pem, x_mm, x_q, x_r, x_qr, x_t, x_ts, x_m, x_max, x_nmt,
         x_bd, x_s, x_p, x_c, x_rec, x_ctx, x_o) = map(sem, (
            "x_zero", "x_kvm", "x_kv", "x_pekv", "x_kvt", "x_pea", "x_a", "x_peg", "x_g", "x_pem", "x_mm", "x_q", "x_r", "x_qr", "x_t",
            "x_ts", "x_m", "x_max", "x_nmt", "x_bd", "x_s", "x_p", "x_c", "x_rec", "x_ctx", "x_o"))
        ld_loaded = sem("ld_loaded")
        pad_ready = sem("pad_ready")
        f_pe_xt, f_hi, f_lo, f_lgT, f_lgTs, f_lg, f_d, f_ex, f_v, f_combT, f_cth, f_ctl = map(
            sem, ("f_pe_xt", "f_hi", "f_lo", "f_lgT", "f_lgTs", "f_lg", "f_d", "f_ex", "f_v", "f_combT", "f_cth", "f_ctl"))
        f_gw, f_gwh, f_gwl = map(sem, ("f_gw", "f_gwh", "f_gwl"))
        f_ones = sem("f_ones")
        raw_in = [[sem(f"raw_in{l}_{u}") for u in range(RING)] for l in range(2)]
        w_hi, w_lo = [[sem(f"{n}{l}") for l in range(2)] for n in ("w_hi", "w_lo")]
        s_g, s_u, s_c, s_silu, s_t2, s_t3, s_ahi, s_alo, s_y = [
            [sem(f"{n}{l}") for l in range(2)] for n in ("s_g", "s_u", "s_c", "s_silu", "s_t2", "s_t3", "s_ahi", "s_alo", "s_y")]
        f_ys, f_yt = sem("f_ys"), sem("f_yt")

        block = ctx.enter_context(nc.Block())

        N_FV = 24
        UNITS = NB * GROUPS

        def blocks(eng):
            with eng.Fori(0, CHUNKS // RING - 1) as i:
                yield i, False
            yield CHUNKS // RING - 1, True

        @block.sync
        def _(sp):
            xf = d["x"].rearrange("b n d -> (b n) d").rearrange("(t p) d -> p t d", p=P)
            for b in range(NB):
                sp.dma_start(X[:, 2 * b:2 * b + 2, :], xf[:, 2 * b:2 * b + 2, :]).then_inc(x_loaded[b], 16)
            sp.dma_start(cst[:, :], d["const"]).then_inc(const_loaded, 16)
            sp.dma_start(wqkv0[:, :, :, :], d["wqkv0"]).then_inc(w_loaded, 16)
            sp.dma_start(wg1[:, :, :], d["wg1"]).then_inc(w_loaded, 16)
            sp.dma_start(wg2[:, :, :], d["wg2"]).then_inc(w_loaded, 16)
            sp.dma_start(wo_gap[:, :, :, :], d["wo_gap"]).then_inc(w_loaded, 16)
            sp.dma_start(normw[:, :], d["normw"]).then_inc(w_loaded, 16)
            sp.dma_start(xb_l[:, :, :], d["xb_l"]).then_inc(w_loaded, 16)
            sp.dma_start(xb_r[:, :, :], d["xb_r"]).then_inc(w_loaded, 16)
            sp.dma_start(xb_b[:, :], d["xb_b"]).then_inc(w_loaded, 16)
            sp.dma_start(wqkv1[:, :, :, :], d["wqkv1"]).then_inc(w_loaded, 16)
            for l in range(2):
                stage = 2 + 3 * l
                if stage >= stages:
                    break
                W = d[f"ffn{l}"]
                sp.wait_ge(x_done, 8 * stage)
                sp.dma_start(gwr[:, :, :], d[f"gate{l}"]).then_inc(f_gw, 16)
                for c in range(RING):
                    sp.dma_start(raw[:, c, :], W[c, :, :]).then_inc(raw_in[l][c], 16)
                with sp.Fori(0, CHUNKS // RING - 1) as i:
                    for u in range(RING):
                        c = i * RING + u
                        sp.wait_ge(w_lo[l], c + 1)
                        sp.dma_start(raw[:, u, :], W[bass.ds(c + RING, 1), :, :].rearrange("a p n -> p (a n)")).then_inc(raw_in[l][u], 16)
                if l == 0 and stages >= 5:
                    sp.wait_ge(x_done, 8 * 3)
                    for hg in range(2):
                        sp.dma_start(wx[:, hg, :], d["wx"][hg, :, :]).then_inc(wx_in[hg], 16)
                    sp.wait_ge(x_done, 8 * 4)
                    sp.dma_start(kvc[:, :, :, :], d["kvc"]).then_inc(kvc_in, 16)
                    sp.dma_start(cx[:, :], d["cx"]).then_inc(cx_in, 16)
                    for hg in range(2, GROUPS):
                        sp.wait_ge(x_mm, hg - 1)
                        sp.dma_start(wx[:, hg % 2, :], d["wx"][hg, :, :]).then_inc(wx_in[hg % 2], 16)
            of = out.rearrange("b n d -> (b n) d").rearrange("(t p) d -> p t d", p=P)
            for b in range(NB):
                sp.wait_ge(x_done, 8 * (stages - 1) + 2 * b + 2)
                sp.dma_start(of[:, 2 * b:2 * b + 2, :], X[:, 2 * b:2 * b + 2, :]).then_inc(out_done, 16)
            sp.wait_ge(out_done, 16 * NB)

        @block.vector
        def _(v):
            def norm(n):
                for t in range(TILES):
                    if n == 0:
                        v.wait_ge(x_loaded[t // 2], 16)
                    else:
                        v.wait_ge(x_done, 8 * (n - 1) + t + 1)
                    v.bn_stats(stats[:, t, :], X[:, t, :]).then_inc(norm_stats, 1)
                for t in range(TILES):
                    v.wait_ge(norm_stats, 8 * n + t + 1)
                    v.bn_aggr(mv[:, t, :], stats[:, t, :]).then_inc(norm_var, 1)
                v.wait_ge(norm_sd, n + 1)
                v.reciprocal(rstd[:, :], sd[:, :]).then_inc(norm_rstd, 1)
                v.wait_ge(norm_rstd, n + 1)
                for t in range(TILES):
                    v.tensor_scalar(xn[:, t, :], X[:, t, :], mv[:, t, 0:1], rstd[:, t:t + 1],
                                    ALU.subtract, ALU.mult).then_inc(norm_done, 1)

            def attention(l, b):
                i = 4 * l + b
                stage = 3 * l
                if l == 0:
                    v.wait_ge(sig_done, 3 * b + 1)
                    v.tensor_tensor(qT[:, :, :].rearrange("p m s -> p (m s)"), ps[:, 1, :], sg[:, 0, :], ALU.mult).then_inc(q_ready, 1)
                    v.wait_ge(sig_done, 3 * b + 2)
                    v.scalar_tensor_tensor(kE[:, :, :].rearrange("p m s -> p (m s)"), ps[:, 2, :], k("even"), sg[:, 1, :], ALU.mult, ALU.mult).then_inc(k_ready, 1)
                    v.scalar_tensor_tensor(kO[:, :, :].rearrange("p m s -> p (m s)"), ps[:, 2, :], k("odd"), sg[:, 1, :], ALU.mult, ALU.mult).then_inc(k_ready, 1)
                    v.wait_ge(sig_done, 3 * b + 3)
                    v.wait_ge(pad_ready, 1)
                    if b >= 1:
                        v.wait_ge(pe_o, 2 * i)
                    for st in range(2):
                        v.tensor_tensor(vpad[:, st, :, 0:HD], ps[:, 3, 256 * st:256 * st + 256].rearrange("p (h e) -> p h e", h=HEADS),
                                        sg[:, 2, 256 * st:256 * st + 256].rearrange("p (h e) -> p h e", h=HEADS), ALU.mult).then_inc(v_ready, 1)
                    if b == 0:
                        v.wait_ge(dt_ready, 1)
                    for m in range(2):
                        if b >= 1:
                            v.wait_ge(pe_o, 2 * (i - 1) + m + 1)
                        for st in range(2):
                            for g in range(4):
                                u = 16 * i + 8 * m + 4 * st + g
                                v.wait_ge(pe_s, u + 1)
                                n = 256 if st == 0 else 128
                                h = 8 * m + 2 * g
                                dst = (P0 if st == 0 else P1)[:, m, g, :, :]
                                v.tensor_tensor(dst, ps[:, 4 + g, 0:2 * n].rearrange("p (e q) -> p e q", e=2), DT[:, h:h + 2, 0:n],
                                                ALU.mult).then_inc(p_done, 1)
                    v.wait_ge(gate_ready, b + 1)
                    for m in range(2):
                        v.wait_ge(pe_o, 2 * i + m + 1)
                        v.tensor_tensor(og[:, m, :], ps[:, 1 + m, :], sgate[:, m, :], ALU.mult).then_inc(og_ready, 1)
                    for m in range(2):
                        v.wait_ge(rms_ready, 2 * b + m + 1)
                        v.reciprocal(rrec[:, m, :], rms[:, m, :]).then_inc(rec_ready, 1)
                        v.wait_ge(rec_ready, 2 * i + m + 1)
                        for e in range(2):
                            grp = 2 * m + e
                            v.scalar_tensor_tensor(on[:, grp, :], og[:, m, 256 * e:256 * e + 256], normw[:, grp:grp + 1],
                                                   rrec[:, m, 256 * e:256 * e + 256], ALU.mult, ALU.mult).then_inc(on_ready, 1)
                else:
                    for j, (bank, tab) in enumerate(((1, "cos"), (2, "sin"), (3, "cos"), (4, "sin"))):
                        v.wait_ge(pe_q, 4 + 4 * b + j + 1)
                        v.tensor_tensor(sg[:, j, :].rearrange("p (m s) -> p m s", m=2), ps[:, bank, :].rearrange("p (m s) -> p m s", m=2),
                                        k(tab).unsqueeze(1).to_broadcast([P, 2, SEQ]), ALU.mult).then_inc(rope_done, 1)
                    for qt in range(2):
                        for m in range(2):
                            for g in range(4):
                                u = 16 * b + 8 * qt + 4 * m + g
                                v.wait_ge(pe_m, u + 1)
                                n = 128 * (qt + 1)
                                v.tensor_reduce(nm[:, qt, g, 2 * m:2 * m + 2], ps[:, 4 + g, 0:2 * n].rearrange("p (e s) -> p e s", e=2),
                                                AX, ALU.max, negate=True).then_inc(max_done, 1)
                    v.wait_ge(pe_nmt, b + 1)
                    v.tensor_tensor(BD[:, :, :], ps[:, 3, 0:SEQ].unsqueeze(1).to_broadcast([P, 4, SEQ]),
                                    k("slot").unsqueeze(2).to_broadcast([P, 4, SEQ]), ALU.mult).then_inc(bd_ready, 1)
                    for m in range(2):
                        v.wait_ge(pe_ss, 2 * i + m + 1)
                        v.reciprocal(rrec[:, m, :], ps[:, 1 + m, :]).then_inc(rec_ready, 1)
                        v.wait_ge(rec_ready, 2 * i + m + 1)
                        for e in range(2):
                            v.tensor_tensor(on[:, 2 * m + e, :], og[:, m, 256 * e:256 * e + 256],
                                            rrec[:, m, 256 * e:256 * e + 256], ALU.mult).then_inc(on_ready, 1)
                v.wait_ge(pe_out, i + 1)
                for t in range(2):
                    v.tensor_tensor(X[:, 2 * b + t, :], X[:, 2 * b + t, :], ps[:, 3, 256 * t:256 * t + 256], ALU.add).then_inc(x_done, 1)

            def experts(l):
                for kk in range(KD):
                    for hf in range(2):
                        n = 2 * kk + hf
                        v.wait_ge(f_hi, 4 * l + n + 1)
                        v.tensor_tensor(xTl[:, kk, hf, :], ps[:, n, :], xTh[:, kk, hf, :].bitcast(F32), ALU.subtract).then_inc(f_lo, 1)
                v.wait_ge(f_gwh, l + 1)
                v.tensor_tensor(gwl[:, :, :], gwr[:, :, :], gwh[:, :, :].bitcast(F32), ALU.subtract).then_inc(f_gwl, 1)
                for c in range(2):
                    split_lo(l, c, c)
                v.wait_ge(f_lg, l + 1)
                lg = ps[:, 6, 0:TILES * E].rearrange("p (t e) -> p t e", t=TILES)
                v.tensor_reduce(nmx[:, :], lg, AX, ALU.max, negate=True).then_inc(f_v, 1)
                base = N_FV * l
                v.wait_ge(f_v, base + 1)
                v.tensor_tensor(lgs[:, :, :], lg, nmx[:, :].unsqueeze(2).to_broadcast([P, TILES, E]), ALU.add).then_inc(f_d, 1)
                v.wait_ge(f_ex, l + 1)
                v.tensor_reduce(den[:, 0, :], ex[:, :, :], AX, ALU.add).then_inc(f_v, 1)
                v.memset(prob[:, :, E:18], -1.0).then_inc(f_v, 1)
                v.memset(comb[:, :, E:17], 1.0).then_inc(f_v, 1)
                v.wait_ge(f_v, base + 4)
                v.reciprocal(den[:, 1, :], den[:, 0, :]).then_inc(f_v, 1)
                v.wait_ge(f_v, base + 5)
                v.tensor_tensor(prob[:, :, 0:E], ex[:, :, :], den[:, 1, :].unsqueeze(2).to_broadcast([P, TILES, E]), ALU.mult).then_inc(f_v, 1)
                v.wait_ge(f_v, base + 6)
                for t in range(TILES):
                    v.max(v8[:, t, :], prob[:, t, 0:E]).then_inc(f_v, 1)
                v.wait_ge(f_v, base + 14)
                v.memset(v8[:, :, TOP_K:8], -1.0).then_inc(f_v, 1)
                v.wait_ge(f_v, base + 15)
                for t in range(TILES):
                    v.match_replace(left[:, t, :], v8[:, t, :], prob[:, t, :], 0.0).then_inc(f_v, 1)
                v.wait_ge(f_v, base + 23)
                v.tensor_tensor(comb[:, :, 0:E], prob[:, :, 0:E], left[:, :, 0:E], ALU.subtract).then_inc(f_v, 1)
                v.wait_ge(f_v, base + 24)
                if l == 1:
                    v.tensor_reduce(den[:, 0, :], comb[:, :, 0:E], AX, ALU.add).then_inc(f_v, 1)
                    v.wait_ge(f_v, base + 25)
                    v.tensor_scalar(den[:, 0, :], den[:, 0, :], 1e-20, None, ALU.add).then_inc(f_v, 1)
                    v.wait_ge(f_v, base + 26)
                    v.reciprocal(den[:, 1, :], den[:, 0, :]).then_inc(f_v, 1)
                    v.wait_ge(f_v, base + 27)
                    v.tensor_tensor(comb[:, :, 0:E], comb[:, :, 0:E], den[:, 1, :].unsqueeze(2).to_broadcast([P, TILES, E]), ALU.mult).then_inc(f_v, 1)
                for hf in range(2):
                    v.wait_ge(f_cth, 2 * l + hf + 1)
                    v.tensor_tensor(CT[32:49, hf, :], ps[0:17, 6 + hf, :], CT[0:17, hf, :].bitcast(F32), ALU.subtract).then_inc(f_ctl, 1)
                for i, last in blocks(v):
                    for u in range(2 * RING):
                        n = i * (2 * RING) + u
                        c = i * RING + u // 2
                        v.wait_ge(s_silu[l], n + 1)
                        v.wait_ge(s_u[l], n + 1)
                        v.tensor_tensor(h1[:, u % 2, :], ps[:, 5, :], sl[:, u % 2, :], ALU.mult).then_inc(s_t2[l], 1)
                        v.wait_ge(s_c[l], n + 1)
                        v.wait_ge(s_t2[l], n + 1)
                        v.tensor_tensor(h2[:, u % 2, :], ps[:, 6, :], h1[:, u % 2, :], ALU.mult).then_inc(s_t3[l], 1)
                        v.wait_ge(s_ahi[l], n + 1)
                        v.tensor_tensor(alo[:, u % 2, :], h2[:, u % 2, :], ahi[:, u % 2, :].bitcast(F32), ALU.subtract).then_inc(s_alo[l], 1)
                        if u % 2 == 0 and not (last and u // 2 + 2 >= RING):
                            split_lo(l, c + 2, (u // 2 + 2) % RING)
                for t in range(TILES):
                    v.wait_ge(f_yt, 4 * l + t // 2 + 1)
                    v.tensor_tensor(X[:, t, :], X[:, t, :], ps[:, 4 + t // 2, 256 * (t % 2):256 * (t % 2) + 256], ALU.add).then_inc(x_done, 1)

            def split_lo(l, c, slot):
                v.wait_ge(w_hi[l], c + 1)
                v.tensor_tensor(wlo[:, slot, :], raw[:, slot, 0:PACK - 128], whi[:, slot, 0:PACK - 128].bitcast(F32), ALU.subtract).then_inc(w_lo[l], 1)

            def cross():
                v.wait_ge(norm_done, 8 * 5)
                v.memset(Gm[:, :, :, :, :], 0.0).then_inc(x_zero, 1)
                v.memset(nmq[:, :, :, :], 0.0).then_inc(x_zero, 1)
                v.memset(kvaug[:, :, :, :], 1.0).then_inc(x_zero, 1)
                v.tensor_copy(onesx[:, :], k("ones")).then_inc(x_zero, 1)
                v.wait_ge(kvc_in, 16)
                v.wait_ge(cx_in, 16)
                for j, tab in enumerate(("coskv", "sinkv")):
                    v.tensor_tensor(kvc[:, j, :, :], kvc[:, j, :, :], kx(tab).unsqueeze(1).to_broadcast([P, NB, SEQ]), ALU.mult).then_inc(x_kvm, 1)
                v.wait_ge(x_kvm, 2)
                v.tensor_tensor(kvT[:, :, :], kvc[:, 0, :, :], kvc[:, 1, :, :], ALU.add).then_inc(x_kv, 1)
                v.wait_ge(x_pekv, 1)
                v.wait_ge(x_zero, 4)
                kv_tok = ps[:, 7, :].rearrange("p (t c) -> p t c", t=TILES)
                v.tensor_copy(kvaug[:, :, 0, 0:XC], kv_tok).then_inc(x_kvt, 1)
                v.tensor_copy(kvaug[:, :, 1, XC:128], kv_tok).then_inc(x_kvt, 1)
                gm = kx("gmask").rearrange("p (j e) -> p j e", j=3)
                for hg in range(GROUPS):
                    for part in range(2):
                        v.wait_ge(x_peg, 2 * hg + part + 1)
                        for piece, j, e in ((0, 0, 0), (0, 0, 1), (1, 1, 0), (2, 1, 1), (3, 2, 0), (3, 2, 1)):
                            col = XC * ((j + e) % 2)
                            v.tensor_scalar(Gm[:, hg, part, piece, col:col + XC], ps[:, 4 + part, 128 * j + XC * e:128 * j + XC * e + XC],
                                            gm[:, j, e:e + 1], None, ALU.mult).then_inc(x_g, 1)

                def rope(w, j):
                    n = 3 * w + j
                    v.wait_ge(x_q, n + 1)
                    if w >= 1:
                        v.wait_ge(x_qr, 2 * (n - 3) + 2)
                    v.tensor_tensor(r1[:, j, :], ps[:, n % 2, :], kx("cosq")[:, 512 * j:512 * j + 512], ALU.mult).then_inc(x_r, 1)
                    v.tensor_tensor(r2[:, j, :], ps[:, n % 2, :], kx("sinq")[:, 512 * j:512 * j + 512], ALU.mult).then_inc(x_r, 1)

                def row_max(w, n):
                    v.wait_ge(x_m, 4 * w + n + 1)
                    v.tensor_reduce(nmq[:, n // 2, n % 2, 0:2], ps[:, 3 + n % 2, :].rearrange("p (e s) -> p e s", e=2),
                                    AX, ALU.max, negate=True).then_inc(x_max, 1)

                def contexts(w):
                    for ab in range(2):
                        mine, other = slice(64 * ab, 64 * ab + 64), slice(64 - 64 * ab, 128 - 64 * ab)
                        v.wait_ge(x_c, 2 * w + ab + 1)
                        v.reciprocal(recx[mine, :], ps[other, 5 + ab, :]).then_inc(x_rec, 1)
                        v.wait_ge(x_rec, 2 * w + ab + 1)
                        if w >= 1:
                            v.wait_ge(x_o, w)
                        v.tensor_tensor(ctxS[mine, :, :].rearrange("p e s -> p (e s)"), ps[mine, 5 + ab, :], recx[mine, :], ALU.mult).then_inc(x_ctx, 1)

                def add_output(b):
                    v.wait_ge(x_o, GROUPS * (b + 1))
                    for t in range(2):
                        v.tensor_tensor(X[:, 2 * b + t, :], X[:, 2 * b + t, :], ps[:, 7, 256 * t:256 * t + 256], ALU.add).then_inc(x_done, 1)

                for j in range(3):
                    rope(0, j)
                for w in range(UNITS):
                    more = w + 1 < UNITS
                    if w >= 1:
                        contexts(w - 1)
                    if more:
                        rope(w + 1, 0)
                    row_max(w, 0)
                    row_max(w, 1)
                    if more:
                        rope(w + 1, 1)
                    row_max(w, 2)
                    row_max(w, 3)
                    v.wait_ge(x_nmt, w + 1)
                    v.tensor_tensor(BDx[:, :, :], ps[:, 2, 0:SEQ].unsqueeze(1).to_broadcast([P, 2, SEQ]),
                                    kx("slot2").unsqueeze(2).to_broadcast([P, 2, SEQ]), ALU.mult).then_inc(x_bd, 1)
                    if more:
                        rope(w + 1, 2)
                    if w % GROUPS == 0 and w:
                        add_output(w // GROUPS - 1)
                contexts(UNITS - 1)
                add_output(NB - 1)

            v.memset(epsc[:, :], EPS).then_inc(eps_ready, 1)
            norm(0)
            v.wait_ge(dt_exp, HEADS)
            v.tensor_tensor(DT[:, :, :], DT[:, :, :], k("causal").unsqueeze(1).to_broadcast([P, HEADS, SEQ]), ALU.mult).then_inc(dt_ready, 1)
            for b in range(NB):
                attention(0, b)
            if stages >= 2:
                norm(1)
                for t in range(TILES):
                    v.wait_ge(xsig_ready, t + 1)
                    v.scalar_tensor_tensor(X[:, t, :], xsig[:, t % 2, :], 0.6, X[:, t, :], ALU.mult, ALU.add).then_inc(xb_part, 1)
                    v.wait_ge(xb_part, t + 1)
                    v.wait_ge(norm_done, 8 + t + 1)
                    v.scalar_tensor_tensor(X[:, t, :], xn[:, t, :], 1.0 - 0.6, X[:, t, :], ALU.mult, ALU.add).then_inc(x_done, 1)
            if stages >= 3:
                norm(2)
                experts(0)
            if stages >= 4:
                norm(3)
                v.tensor_copy(onesr[:, :], k("ones")).then_inc(setup_v, 1)
                v.tensor_copy(identb[:, :], ident).then_inc(setup_v, 1)
                v.tensor_copy(negqs[:, :], k("neg_qs")).then_inc(setup_v, 1)
                v.tensor_copy(negsq[:, :], k("neg_sq")).then_inc(setup_v, 1)
                v.memset(nm[:, :, :, :], 0.0).then_inc(setup_v, 1)
                v.wait_ge(setup_v, 5)
                for b in range(NB):
                    attention(1, b)
            if stages >= 5:
                norm(4)
                cross()
            if stages >= 6:
                norm(5)
                experts(1)

        @block.scalar
        def _(a):
            def norm(n):
                if n == 0:
                    a.wait_ge(eps_ready, 1)
                a.wait_ge(norm_var, 8 * (n + 1))
                a.activation(sd[:, :], mv[:, :, 1], ACT.Sqrt, bias=epsc[:, 0:1]).then_inc(norm_sd, 1)

            def attention(l, b):
                i = 4 * l + b
                a.wait_ge(pe_xt, i + 1)
                a.activation(xT[:, :, :].rearrange("p k s -> p (k s)"), ps[:, 0, :], ACT.Copy).then_inc(xt_ready, 1)
                if l == 0:
                    for j, s in enumerate((pe_q, pe_k, pe_v)):
                        a.wait_ge(s, b + 1)
                        a.activation(sg[:, j, :], ps[:, 1 + j, :], ACT.Sigmoid).then_inc(sig_done, 1)
                    a.wait_ge(pe_g1, b + 1)
                    a.activation(g1S[:, :], ps[0:HD, 0, 0:SEQ], ACT.Copy).then_inc(g1_ready, 1)
                    a.wait_ge(pe_gate, b + 1)
                    a.activation(sgate[:, :, :], ps[:, 4:6, :], ACT.Sigmoid).then_inc(gate_ready, 1)
                    for m in range(2):
                        a.wait_ge(og_ready, 2 * b + m + 1)
                        a.activation(sq[:, m, :], og[:, m, :], ACT.Square).then_inc(sq_ready, 1)
                    for m in range(2):
                        a.wait_ge(pe_ss, 2 * i + m + 1)
                        a.activation(rms[:, m, :], ps[:, 1 + m, :], ACT.Sqrt, bias=epsc[:, 0:1], scale=1.0 / HD).then_inc(rms_ready, 1)
                else:
                    a.wait_ge(pe_v, i + 1)
                    a.wait_ge(pad_ready, 3)
                    for st in range(2):
                        a.activation(vpad[:, st, :, 0:HD], ps[:, 5, 256 * st:256 * st + 256].rearrange("p (h e) -> p h e", h=HEADS),
                                     ACT.Copy).then_inc(v_ready, 1)
                    for m in range(2):
                        if b >= 1:
                            a.wait_ge(pe_o, 2 * (i - 1) + m + 1)
                        for st in range(2):
                            for g in range(4):
                                u = 16 * i + 8 * m + 4 * st + g
                                a.wait_ge(pe_s, u + 1)
                                n = 256 if st == 0 else 128
                                dst = (P0 if st == 0 else P1)[:, m, g, :, :]
                                a.activation(dst, ps[:, 4 + g, 0:2 * n].rearrange("p (e q) -> p e q", e=2), ACT.Exp,
                                             scale=1.0 / HD ** 0.5).then_inc(p_done, 1)
                    for m in range(2):
                        a.wait_ge(pe_o, 2 * i + m + 1)
                        a.activation(og[:, m, :], ps[:, 1 + m, :], ACT.Copy).then_inc(og_ready, 1)

            def split_hi(l, c, slot, turn):
                a.wait_ge(raw_in[l][slot], 16 * (turn + 1))
                a.activation(whi[:, slot, :], raw[:, slot, :], ACT.Copy).then_inc(w_hi[l], 1)

            def experts(l):
                for kk in range(KD):
                    for hf in range(2):
                        n = 2 * kk + hf
                        a.wait_ge(f_pe_xt, 4 * l + n + 1)
                        a.activation(xTh[:, kk, hf, :], ps[:, n, :], ACT.Copy).then_inc(f_hi, 1)
                a.wait_ge(f_gw, 16 * (l + 1))
                a.activation(gwh[:, :, :], gwr[:, :, :], ACT.Copy).then_inc(f_gwh, 1)
                for c in range(2):
                    split_hi(l, c, c, 0)
                for hf in range(2):
                    a.wait_ge(f_lgT, 2 * l + hf + 1)
                    a.activation(lgT[:, hf, :], ps[0:E, 4 + hf, :], ACT.Copy).then_inc(f_lgTs, 1)
                a.wait_ge(f_d, l + 1)
                a.activation(ex[:, :, :], lgs[:, :, :], ACT.Exp).then_inc(f_ex, 1)
                for hf in range(2):
                    a.wait_ge(f_combT, 2 * l + hf + 1)
                    a.wait_ge(f_ones, 2 * (l + 1))
                    a.activation(CT[0:17, hf, :], ps[0:17, 6 + hf, :], ACT.Copy).then_inc(f_cth, 1)
                for i, last in blocks(a):
                    for u in range(2 * RING):
                        n = i * (2 * RING) + u
                        c = i * RING + u // 2
                        a.wait_ge(s_g[l], n + 1)
                        a.activation(sl[:, u % 2, :], ps[:, 4, :], ACT.Silu).then_inc(s_silu[l], 1)
                        a.wait_ge(s_t3[l], n + 1)
                        a.activation(ahi[:, u % 2, :], h2[:, u % 2, :], ACT.Copy).then_inc(s_ahi[l], 1)
                        if u % 2 == 0 and not (last and u // 2 + 2 >= RING):
                            split_hi(l, c + 2, (u // 2 + 2) % RING, i + (u // 2 + 2) // RING)
                for mt in range(2):
                    for hf in range(2):
                        a.wait_ge(s_y[l], 2 * CHUNKS + 1)
                        a.activation(yS[:, mt, hf, :], ps[:, 2 * mt + hf, :], ACT.Copy).then_inc(f_ys, 1)

            def cross():
                for hg in range(GROUPS):
                    for jj in range(4):
                        a.wait_ge(x_pea, 4 * hg + jj + 1)
                        a.activation(Aw[:, hg, :, :, LO * jj:LO * jj + LO], ps[:, jj, 0:2 * XQ].rearrange("p (k h f) -> p k h f", k=KD, h=2),
                                     ACT.Copy).then_inc(x_a, 1)
                    a.wait_ge(x_pem, hg + 1)
                    a.activation(MM[:, hg, :, :].rearrange("p e n -> p (e n)"), ps[:, 6, :], ACT.Copy).then_inc(x_mm, 1)
                    a.wait_ge(pe_xt, 8 + hg + 1)
                    a.activation(xT4[:, :, hg, :], ps[:, 7, :].rearrange("p (k s) -> p k s", k=KD), ACT.Copy).then_inc(xt_ready, 1)
                for w in range(UNITS):
                    a.wait_ge(x_t, w + 1)
                    a.activation(tS[:, :, :].rearrange("p e s -> p (e s)"), ps[:, 2, :], ACT.Copy).then_inc(x_ts, 1)
                    for n in range(4):
                        a.wait_ge(x_s, 4 * w + n + 1)
                        a.activation(Px[:, n // 2, n % 2, :], ps[:, 3 + n % 2, :], ACT.Exp).then_inc(x_p, 1)

            norm(0)
            a.wait_ge(const_loaded, 16)
            a.wait_ge(ld_loaded, 16)
            for h in range(HEADS):
                a.activation(DT[:, h, :], k("dist"), ACT.Exp, scale=ld_bc[:, h:h + 1]).then_inc(dt_exp, 1)
            for b in range(NB):
                attention(0, b)
            if stages >= 2:
                norm(1)
                for t in range(TILES):
                    a.wait_ge(pe_xb, t + 1)
                    if t >= 2:
                        a.wait_ge(xb_part, t - 1)
                    a.activation(xsig[:, t % 2, :], ps[:, t % 4, 0:SEQ], ACT.Sigmoid, bias=xb_b[:, 0:1]).then_inc(xsig_ready, 1)
            if stages >= 3:
                norm(2)
                experts(0)
            if stages >= 4:
                norm(3)
                for b in range(NB):
                    attention(1, b)
            if stages >= 5:
                norm(4)
                cross()
            if stages >= 6:
                norm(5)
                experts(1)

        @block.gpsimd
        def _(g):
            g.dma_start(ld_bc[:, :], d["ld"]).then_inc(ld_loaded, 16)
            g.memset(vpad[:, :, :, :], 0.0).then_inc(pad_ready, 1)

            def zero_fill(l):
                g.wait_ge(x_done, 8 * (2 + 3 * l))
                g.memset(CT[:, :, :].bitcast(F32), 0.0).then_inc(f_ones, 1)
                g.memset(zeros[:, :].bitcast(F32), 0.0).then_inc(f_ones, 1)

            if stages >= 3:
                zero_fill(0)
            if stages >= 4:
                g.wait_ge(x_done, 8 * 3)
                g.memset(vpad[:, :, :, :], 0.0).then_inc(pad_ready, 1)
                g.wait_ge(pad_ready, 2)
                g.memset(vpad[:, :, :, HD:HD + 1], 1.0).then_inc(pad_ready, 1)
                for b in range(NB):
                    g.wait_ge(rope_done, 4 * b + 2)
                    if b >= 1:
                        g.wait_ge(pe_o, 2 * (4 + b - 1) + 2)
                    g.tensor_tensor(qT[:, :, :].rearrange("p m s -> p (m s)"), sg[:, 0, :], sg[:, 1, :], ALU.add).then_inc(q_ready, 1)
                    g.wait_ge(rope_done, 4 * b + 4)
                    g.tensor_tensor(kT[:, :, :].rearrange("p m s -> p (m s)"), sg[:, 2, :], sg[:, 3, :], ALU.add).then_inc(k_sum, 1)
                    g.wait_ge(k_sum, b + 1)
                    g.tensor_scalar(kE[:, :, :], kT[:, :, :], k("even"), None, ALU.mult).then_inc(k_ready, 1)
                    g.tensor_scalar(kO[:, :, :], kT[:, :, :], k("odd"), None, ALU.mult).then_inc(k_ready, 1)
            if stages >= 5:
                for w in range(NB * GROUPS):
                    for j in range(3):
                        g.wait_ge(x_r, 6 * w + 2 * j + 2)
                        if w >= 1:
                            g.wait_ge(x_t, w)
                        for part in range(2):
                            g.tensor_tensor(qr[:, j, part, :], r1[:, j, 256 * part:256 * part + 256], r2[:, j, 256 - 256 * part:512 - 256 * part],
                                            ALU.add).then_inc(x_qr, 1)
            if stages >= 6:
                zero_fill(1)

        @block.tensor
        def _(pe):
            def mm(o, l, r, start, stop):
                return pe.matmul(o, l, r, start=start, stop=stop, skip_group_check=True)

            def attention(l, b):
                i = 4 * l + b
                stage = 3 * l
                if b == 0 and l == 0:
                    pe.wait_ge(const_loaded, 16)
                pe.wait_ge(norm_done, 8 * stage + 2 * b + 2)
                if l == 0 and b >= 1:
                    pe.wait_ge(g1_ready, b)
                for kk in range(KD):
                    for t in range(2):
                        last = pe.transpose(ps[:, 0, 256 * kk + 128 * t:256 * kk + 128 * t + 128], xn[:, 2 * b + t, 128 * kk:128 * kk + 128], ident)
                last.then_inc(pe_xt, 1)
                if l == 0 and b == 0:
                    pe.wait_ge(w_loaded, 16 * 9)
                pe.wait_ge(xt_ready, i + 1)
                if l == 1 or b >= 1:
                    pe.wait_ge(rec_ready, 2 * i)
                w = wqkv0 if l == 0 else wqkv1

                def features(bank, j):
                    for m in range(2):
                        for kk in range(KD):
                            last = mm(ps[:, bank, 256 * m:256 * m + 256], w[:, j, kk, 128 * m:128 * m + 128], xT[:, kk, :], kk == 0, kk == KD - 1)
                    return last

                def tokens(bank, j):
                    for st in range(2):
                        for kk in range(KD):
                            last = mm(ps[:, bank, 256 * st:256 * st + 256], xT[:, kk, 128 * st:128 * st + 128], w[:, j, kk, :], kk == 0, kk == KD - 1)
                    return last

                if l == 0:
                    features(1, 0).then_inc(pe_q, 1)
                    features(2, 1).then_inc(pe_k, 1)
                    pe.wait_ge(x_done, 2 * b)
                    tokens(3, 2).then_inc(pe_v, 1)
                    for kk in range(KD):
                        last = mm(ps[0:HD, 0, 0:SEQ], wg1[:, kk, :], xT[:, kk, :], kk == 0, kk == KD - 1)
                    last.then_inc(pe_g1, 1)
                    pe.wait_ge(g1_ready, b + 1)
                    pe.wait_ge(p_done, 16 * i)
                    for grp in range(4):
                        last = mm(ps[:, 4 + grp // 2, 256 * (grp % 2):256 * (grp % 2) + 256], wg2[:, grp, :], g1S[:, :], True, True)
                    last.then_inc(pe_gate, 1)
                    pe.wait_ge(gate_ready, b + 1)
                    pe.wait_ge(pad_ready, 1)
                else:
                    features(1, 0).then_inc(pe_q, 1)
                    features(2, 1).then_inc(pe_q, 1)
                    pe.wait_ge(x_done, 8 * 3 + 2 * b)
                    features(3, 2).then_inc(pe_q, 1)
                    pe.wait_ge(p_done, 16 * i)
                    features(4, 3).then_inc(pe_q, 1)
                    tokens(5, 4).then_inc(pe_v, 1)
                    pe.wait_ge(pad_ready, 3)
                pe.wait_ge(q_ready, i + 1)
                pe.wait_ge(k_ready, 2 * i + 2)
                pe.wait_ge(v_ready, 2 * i + 2)
                if l == 1:
                    pe.wait_ge(setup_v, 5)
                    for qt in range(2):
                        for m in range(2):
                            for g in range(4):
                                u = 16 * b + 8 * qt + 4 * m + g
                                n = 128 * (qt + 1)
                                if 8 * qt + 4 * m + g >= 4:
                                    pe.wait_ge(max_done, u - 3)
                                bank = ps[:, 4 + g, 0:2 * n].rearrange("p (e s) -> p e s", e=2)
                                mm(bank[:, :, n - 128:n], identb[:, :], negqs[:, :].unsqueeze(1).to_broadcast([P, 2, 128]), True, False)
                                r = slice(32 * g, 32 * g + 32)
                                for e, kk in enumerate((kE, kO)):
                                    last = mm(bank[:, e, :], qT[r, m, 128 * qt:128 * qt + 128], kk[r, m, 0:n], False, e == 1)
                                last.then_inc(pe_m, 1)
                    pe.wait_ge(max_done, 16 * (b + 1))
                    for qt in range(2):
                        last = pe.transpose(ps[:, 3, 128 * qt:128 * qt + 128], nm[:, qt, :, :].rearrange("p g s -> p (g s)"), ident)
                    last.then_inc(pe_nmt, 1)
                    pe.wait_ge(bd_ready, b + 1)
                for m in range(2):
                    for st in range(2):
                        n = 256 if st == 0 else 128
                        for g in range(4):
                            u = 16 * i + 8 * m + 4 * st + g
                            if 8 * m + 4 * st + g >= 4:
                                pe.wait_ge(p_done, u - 3)
                            bank = ps[:, 4 + g, 0:2 * n].rearrange("p (e q) -> p e q", e=2)
                            r = slice(32 * g, 32 * g + 32)
                            if l == 1:
                                mm(bank[:, :, 0:128], identb[:, :], negsq[:, :].unsqueeze(1).to_broadcast([P, 2, 128]), True, False)
                                mm(bank, onesr[r, :], BD[r, 2 * m:2 * m + 2, SEQ - n:SEQ], False, False)
                            for e, kk in enumerate((kE, kO)):
                                last = mm(bank[:, e, :], kk[r, m, 128 * st:128 * st + 128], qT[r, m, SEQ - n:SEQ], l == 0, True)
                            last.then_inc(pe_s, 1)
                    pe.wait_ge(p_done, 16 * i + 8 * m + 8)
                    for g in range(4):
                        for st in range(2):
                            for e in range(2):
                                h = 8 * m + 2 * g + e
                                last = mm(ps[32 * g:32 * g + 32, 1 + m, 256 * e + 128 * st:256 * e + 256], vpad[:, st, h, :],
                                          (P0 if st == 0 else P1)[:, m, g, e, :], e == 0 and st == 0, st == 1)
                    last.then_inc(pe_o, 1)
                for m in range(2):
                    if l == 0:
                        pe.wait_ge(sq_ready, 2 * b + m + 1)
                        mm(ps[:, 1 + m, :], k("block_ones"), sq[:, m, :], True, True).then_inc(pe_ss, 1)
                    else:
                        pe.wait_ge(og_ready, 2 * i + m + 1)
                        mm(ps[:, 1 + m, :], k("pick16"), og[:, m, :], True, True).then_inc(pe_ss, 1)
                pe.wait_ge(on_ready, 4 * i + 4)
                for t in range(2):
                    for grp in range(4):
                        last = mm(ps[:, 3, 256 * t:256 * t + 256], on[:, grp, 128 * t:128 * t + 128], wo_gap[:, l, grp, :], grp == 0, grp == 3)
                last.then_inc(pe_out, 1)

            def experts(l):
                stage = 2 + 3 * l
                for kk in range(KD):
                    for hf in range(2):
                        for t in range(4):
                            pe.wait_ge(norm_done, 8 * stage + 4 * hf + t + 1)
                            last = pe.transpose(ps[:, 2 * kk + hf, 128 * t:128 * t + 128], xn[:, 4 * hf + t, 128 * kk:128 * kk + 128], ident)
                        last.then_inc(f_pe_xt, 1)
                pe.wait_ge(f_lo, 4 * (l + 1))
                pe.wait_ge(f_gwl, l + 1)
                for hf in range(2):
                    pairs = ((gwh, xTh), (gwl, xTh), (gwh, xTl))
                    for j, (w, x) in enumerate(pairs):
                        for kk in range(KD):
                            last = mm(ps[0:E, 4 + hf, :], w[:, kk, :], x[:, kk, hf, :], j + kk == 0, j == 2 and kk == 1)
                    last.then_inc(f_lgT, 1)
                pe.wait_ge(f_lgTs, 2 * (l + 1))
                for t in range(TILES):
                    last = pe.transpose(ps[:, 6, E * t:E * t + E], lgT[:, t // 4, 128 * (t % 4):128 * (t % 4) + 128], ident[0:E, 0:E])
                last.then_inc(f_lg, 1)
                pe.wait_ge(f_ones, 2 * (l + 1))
                for bank in range(4):
                    last = mm(ps[:, bank, :], zeros[:, 0:128], zeros[:, :], True, False)
                last.then_inc(s_y[l], 1)

                def gate_up(n, u):
                    slot, hf = u // 2 % RING, u % 2
                    pe.wait_ge(w_lo[l], nchunk(n, u) + 1)
                    pe.wait_ge(s_silu[l], n)
                    three(4, whi, wlo, slot, 0, hf).then_inc(s_g[l], 1)
                    pe.wait_ge(s_t2[l], n)
                    three(5, whi, wlo, slot, 256, hf).then_inc(s_u[l], 1)

                def three(bank, hi, lo, slot, col, hf):
                    first = True
                    for w, x in ((hi, xTh), (lo, xTh), (hi, xTl)):
                        for kk in range(KD):
                            last = mm(ps[:, bank, :], w[:, slot, col + 128 * kk:col + 128 * kk + 128], x[:, kk, hf, :], first, False)
                            first = False
                    return last

                def weights_of_experts(n, u):
                    pe.wait_ge(s_t3[l], n)
                    mm(ps[:, 6, :], whi[0:64, u // 2 % RING, PACK - 128:PACK], CT[:, u % 2, :], True, True).then_inc(s_c[l], 1)

                def down(n, u):
                    slot, hf = u // 2 % RING, u % 2
                    pe.wait_ge(s_alo[l], n + 1)
                    for mt in range(2):
                        for w, x in ((whi, ahi), (wlo, ahi), (whi, alo)):
                            last = mm(ps[:, 2 * mt + hf, :], w[:, slot, 512 + 128 * mt:640 + 128 * mt], x[:, u % 2, :], False, False)
                    last.then_inc(s_y[l], 1)

                def nchunk(n, u):
                    return cur[0] * RING + u // 2

                cur = [0]
                gate_up(0, 0)
                for t in range(TILES):
                    if t == 0:
                        pe.wait_ge(f_v, 24 if l == 0 else 24 + 28)
                    last = pe.transpose(ps[0:17, 6 + t // 4, 128 * (t % 4):128 * (t % 4) + 128], comb[:, t, :], ident)
                    if t % 4 == 3:
                        last.then_inc(f_combT, 1)
                pe.wait_ge(f_ctl, 2 * (l + 1))
                weights_of_experts(0, 0)
                for i, last in blocks(pe):
                    cur[0] = i
                    for u in range(2 * RING):
                        n = i * (2 * RING) + u
                        if not (last and u == 2 * RING - 1):
                            gate_up(n + 1, u + 1)
                            weights_of_experts(n + 1, u + 1)
                        down(n, u)
                pe.wait_ge(f_ys, 4 * (l + 1))
                for t in range(TILES):
                    for mt in range(2):
                        last = pe.transpose(ps[:, 4 + t // 2, 256 * (t % 2) + 128 * mt:256 * (t % 2) + 128 * mt + 128],
                                            yS[:, mt, t // 4, 128 * (t % 4):128 * (t % 4) + 128], ident)
                    if t % 2:
                        last.then_inc(f_yt, 1)

            def cross():
                def part_of(slot, name, rows=P):
                    a, b = XP[name]
                    return wx[0:rows, slot, a:b]

                pe.wait_ge(x_done, 8 * 4)
                pe.wait_ge(x_kv, 1)
                for t in range(TILES):
                    last = pe.transpose(ps[:, 7, XC * t:XC * t + XC], kvT[0:XC, t // 2, 128 * (t % 2):128 * (t % 2) + 128], ident[0:XC, 0:XC])
                last.then_inc(x_pekv, 1)
                for hg in range(GROUPS):
                    slot = hg % 2
                    pe.wait_ge(wx_in[slot], 16 * (hg // 2 + 1))
                    wq = part_of(slot, "wq").rearrange("p (h d) -> p h d", h=4)
                    kcq = part_of(slot, "kcq").rearrange("p (h q) -> p h q", h=4)
                    qrT = part_of(slot, "qrT", XR).rearrange("p (h f) -> p h f", h=2)
                    krT = part_of(slot, "krT", XR)
                    kckv = part_of(slot, "kckv").rearrange("p (h c) -> p h c", h=4)
                    woT = part_of(slot, "woT").rearrange("p (h n) -> p h n", h=4)
                    for jj in range(4):
                        if hg >= 1:
                            pe.wait_ge(x_a, 4 * (hg - 1) + jj + 1)
                        for kk in range(KD):
                            last = mm(ps[:, jj, XQ * kk:XQ * kk + XQ], wq[:, jj, 128 * kk:128 * kk + 128], kcq[:, jj, :], True, True)
                        last.then_inc(x_pea, 1)
                    for part in range(2):
                        if hg >= 1:
                            pe.wait_ge(x_g, 12 * (hg - 1) + 6 * part + 6)
                        for j in range(3):
                            last = mm(ps[:, 4 + part, 128 * j:128 * j + 128], qrT[:, part, 128 * j:128 * j + 128], krT[:, XC * j:XC * j + 2 * XC], True, True)
                        last.then_inc(x_peg, 1)
                    if hg >= 1:
                        pe.wait_ge(x_mm, hg)
                    for jj in range(4):
                        last = mm(ps[64 * (jj % 2):64 * (jj % 2) + 64, 6, 256 * (jj // 2):256 * (jj // 2) + 256], kckv[:, jj, :], woT[:, jj, :], True, True)
                    last.then_inc(x_pem, 1)
                    b = hg
                    if b == 0:
                        pe.wait_ge(x_kvt, 2)
                    else:
                        pe.wait_ge(xt_ready, 8 + b)
                    pe.wait_ge(norm_done, 8 * 4 + 2 * b + 2)
                    for kk in range(KD):
                        for t in range(2):
                            last = pe.transpose(ps[:, 7, 256 * kk + 128 * t:256 * kk + 128 * t + 128], xn[:, 2 * b + t, 128 * kk:128 * kk + 128], ident)
                    last.then_inc(pe_xt, 1)
                pe.wait_ge(x_a, 4 * GROUPS)
                pe.wait_ge(x_mm, GROUPS)
                pe.wait_ge(x_g, 12 * GROUPS)
                pe.wait_ge(xt_ready, 8 + NB)

                def latent_queries(w, j):
                    b, hg, n = w // GROUPS, w % GROUPS, 3 * w + j
                    if n >= 2:
                        pe.wait_ge(x_r, 2 * (n - 2) + 2)
                    for part in range(2):
                        for kk in range(KD):
                            last = mm(ps[:, n % 2, 256 * part:256 * part + 256], Aw[:, hg, kk, part, 128 * j:128 * j + 128], xT4[:, kk, b, :], kk == 0, kk == 1)
                    last.then_inc(x_q, 1)

                def query_side(w):
                    pe.wait_ge(x_qr, 6 * w + 6)
                    if w >= 1:
                        pe.wait_ge(x_bd, w)
                    for pair in range(2):
                        n = 0
                        for piece in (2 * pair, 2 * pair + 1):
                            j = pair + piece % 2
                            for part in range(2):
                                last = mm(ps[:, 2, 256 * pair:256 * pair + 256], Gm[:, w % GROUPS, part, piece, :], qr[:, j, part, :], n == 0, n == 3)
                                n += 1
                    last.then_inc(x_t, 1)

                def max_scores(w, n):
                    st, ab = n // 2, n % 2
                    r = slice(64 * ab, 64 * ab + 64)
                    if n == 0:
                        pe.wait_ge(x_ts, w + 1)
                    if n >= 2:
                        pe.wait_ge(x_max, 4 * w + n - 1)
                    elif w >= 1:
                        pe.wait_ge(x_p, 4 * w + n - 1)
                    for pair in range(2):
                        last = mm(ps[:, 3 + ab, 256 * pair:256 * pair + 256], tS[r, pair, 128 * st:128 * st + 128], kvT[r, w // GROUPS, :], True, True)
                    last.then_inc(x_m, 1)

                def transposed_maxima(w):
                    pe.wait_ge(x_max, 4 * w + 4)
                    for st in range(2):
                        last = pe.transpose(ps[:, 2, 128 * st:128 * st + 128], nmq[:, st, :, :].rearrange("p a n -> p (a n)"), ident)
                    last.then_inc(x_nmt, 1)

                def scores(w):
                    pe.wait_ge(x_bd, w + 1)
                    for n in range(4):
                        lt, ab = n // 2, n % 2
                        r = slice(64 * ab, 64 * ab + 64)
                        if n >= 2:
                            pe.wait_ge(x_p, 4 * w + n - 1)
                        mm(ps[:, 3 + ab, :], kvT[r, w // GROUPS, 128 * lt:128 * lt + 128], tS[r, :, :].rearrange("p e s -> p (e s)"), True, False)
                        mm(ps[:, 3 + ab, :], onesx[r, :], BDx[r, :, :].rearrange("p e s -> p (e s)"), False, True).then_inc(x_s, 1)

                def weighted_contexts(w):
                    for ab in range(2):
                        for lt in range(2):
                            pe.wait_ge(x_p, 4 * w + 2 * lt + ab + 1)
                            last = mm(ps[:, 5 + ab, :], kvaug[:, 2 * (w // GROUPS) + lt, ab, :], Px[:, lt, ab, :], lt == 0, lt == 1)
                        last.then_inc(x_c, 1)

                def output(w):
                    b, hg = w // GROUPS, w % GROUPS
                    pe.wait_ge(x_ctx, 2 * w + 2)
                    if hg == 0:
                        pe.wait_ge(x_done, 8 * 4 + 2 * b)
                    for t in range(2):
                        for pair in range(2):
                            last = mm(ps[:, 7, 256 * t:256 * t + 256], ctxS[:, pair, 128 * t:128 * t + 128], MM[:, hg, pair, :],
                                      hg + t + pair == 0, hg == 3 and pair == 1)
                    last.then_inc(x_o, 1)

                for j in range(3):
                    latent_queries(0, j)
                for w in range(UNITS):
                    more = w + 1 < UNITS
                    query_side(w)
                    if more:
                        latent_queries(w + 1, 0)
                    max_scores(w, 0)
                    max_scores(w, 1)
                    if more:
                        latent_queries(w + 1, 1)
                    max_scores(w, 2)
                    max_scores(w, 3)
                    if more:
                        latent_queries(w + 1, 2)
                    transposed_maxima(w)
                    if w >= 1:
                        output(w - 1)
                    scores(w)
                    weighted_contexts(w)
                output(UNITS - 1)

            for b in range(NB):
                attention(0, b)
            if stages >= 2:
                for t in range(TILES):
                    b = t // 2
                    if t >= 4:
                        pe.wait_ge(xsig_ready, t - 3)
                    else:
                        pe.wait_ge(x_done, 8)
                    mm(ps[:, t % 4, 0:SEQ], xb_l[:, b, 128 * (t % 2):128 * (t % 2) + 128], xb_r[:, b, :], True, True).then_inc(pe_xb, 1)
            if stages >= 3:
                experts(0)
            if stages >= 4:
                for b in range(NB):
                    attention(1, b)
            if stages >= 5:
                cross()
            if stages >= 6:
                experts(1)


def constants():
    c = np.zeros((P, CONST_W), np.float32)
    p = np.arange(P)

    def put(name, a):
        lo, hi = CONST[name]
        c[:, lo:hi] = np.asarray(a, np.float32).reshape(P, hi - lo)

    put("ident", np.eye(P))
    q = np.arange(SEQ)
    put("dist", np.maximum(q[None] - p[:, None], 0))
    put("causal", q[None] >= p[:, None])
    put("neg_qs", np.where(p[None] > p[:, None], NEG, 0.0))
    put("neg_sq", np.where(p[:, None] > p[None], NEG, 0.0))
    put("even", (p // HD) % 2 == 0)
    put("odd", (p // HD) % 2 == 1)
    put("slot", (p % 32)[:, None] == np.arange(4)[None])
    same = (p[:, None] // 32) == (p[None] // 32)
    put("block_ones", same & (p[:, None] % 32 < HD))
    put("pick16", same & (p[:, None] % 32 == HD))
    put("ones", np.ones((P, 128)))
    dd = p % HD
    inv = np.float32(10000.0) ** (-(np.arange(0, HD, 2, dtype=np.float32) / np.float32(HD)))
    ang = (q.astype(np.float32)[None] * inv[dd // 2][:, None]).astype(np.float32)
    put("cos", np.cos(ang))
    put("sin", np.where(dd[:, None] % 2 == 0, -1.0, 1.0) * np.sin(ang))
    return c


def cross_constants():
    c = np.zeros((P, CX_W), np.float32)
    p = np.arange(P)
    pos = np.arange(SEQ, dtype=np.float32)

    def put(name, a):
        lo, hi = CX[name]
        c[:, lo:hi] = np.asarray(a, np.float32).reshape(P, hi - lo)

    def angles(dim, feature):
        inv = np.float32(1.0) / np.float32(10000.0) ** (np.arange(0, dim, 2, dtype=np.float32) / np.float32(dim))
        return (pos * inv[feature // 2][..., None]).astype(np.float32)

    f = (np.arange(3)[None] * P + p[:, None]) % LO
    lo, hi = angles(XQ, f), angles(XQ, f + LO)
    put("cosq", np.stack([np.cos(lo), np.cos(hi)], axis=2))
    put("sinq", np.stack([np.sin(hi), -np.sin(lo)], axis=2))
    g = angles(XC, p % XC)
    put("coskv", np.cos(g))
    put("sinkv", np.where((p % XC < XC // 2)[:, None], -1.0, 1.0) * np.sin(g))
    head = (np.arange(3)[None] * P + p[:, None]) // LO
    put("gmask", head[:, :, None] == np.arange(3)[None, :, None] + np.arange(2)[None, None, :])
    put("slot2", (p % 64)[:, None] == np.arange(2)[None])
    return c


def cross_pack(i):
    o = np.zeros((GROUPS, P, XPACK), np.float32)

    def put(name, a):
        lo, hi = XP[name]
        o[:, 0:a.shape[1], lo:hi] = a.reshape(GROUPS, a.shape[1], hi - lo)

    def by_group(a, *axes):
        return a.reshape((GROUPS, 4) + a.shape[1:]).transpose(axes)

    put("wq", by_group(i["L1_xattn_Wq"].reshape(XH, XK, D), 0, 2, 1, 3))
    put("kcq", by_group(i["L1_xattn_w_kc_q"], 0, 2, 1, 3))
    put("qrT", by_group(i["L1_xattn_W_qr"].reshape(XH, 2, LO, XR), 0, 4, 2, 1, 3))
    put("krT", by_group(i["L1_xattn_W_kr"], 0, 3, 1, 2))
    put("kckv", by_group(i["L1_xattn_w_kc_kv"], 0, 2, 1, 3))
    put("woT", by_group(i["L1_xattn_Wo"].T.reshape(XH, XK, D), 0, 2, 1, 3))
    return o


def rows_to_lhs(w):
    return w.reshape(KD, P, -1).transpose(1, 0, 2)


def gap_rows(w):
    n = w.shape[1]
    o = np.zeros((4, 32, 4, n), w.dtype)
    w = w.reshape(2, 4, 2, HD, n)
    for m in range(2):
        for e in range(2):
            o[:, 0:HD, 2 * m + e] = w[m, :, e]
    return o.reshape(P, 4, n)


def expert_pack(w13, w2, s13, s2):
    total = CHUNKS * P
    flat = E * INNER

    def rows(experts, shared):
        o = np.zeros((total, D), np.float32)
        o[:flat] = experts.reshape(flat, D)
        o[flat:flat + SHARED] = shared
        return o

    g = rows(w13[:, :INNER], s13[:SHARED]).reshape(CHUNKS, P, KD, P)
    u = rows(w13[:, INNER:], s13[SHARED:]).reshape(CHUNKS, P, KD, P)
    dn = rows(w2.transpose(0, 2, 1), s2.T).reshape(CHUNKS, P, D)
    sel = np.zeros((total, P), np.float32)
    r = np.arange(total)
    e = np.where(r < flat, r // INNER, E)
    sel[r, e] = 1
    sel[r, 32 + e] = 1
    sel = sel.reshape(CHUNKS, P, P).transpose(0, 2, 1)
    g = g.transpose(0, 3, 2, 1).reshape(CHUNKS, P, 2 * P)
    u = u.transpose(0, 3, 2, 1).reshape(CHUNKS, P, 2 * P)
    return np.concatenate([g, u, dn, sel], axis=2)


def lay_out(i):
    i = {k: np.asarray(v) for k, v in i.items()}
    ctxT = i["ctx_512"].transpose(2, 0, 1)
    xw = i["L0_xattn_W"][0]
    half = (64, NB, SEQ)
    swap = np.arange(D) ^ 1
    turn = np.arange(XC) ^ (XC // 2)
    wq, wk, wv = (i[f"L1_attn_w{c}"] for c in "qkv")
    return {
        "x": i["x"],
        "const": constants(),
        "ld": np.broadcast_to(i["L0_attn_log_decay"], (P, HEADS)),
        "wqkv0": np.stack([rows_to_lhs(i[f"L0_attn_W{c}"]) for c in "qkv"], axis=1),
        "wg1": rows_to_lhs(i["L0_attn_Wg1"]),
        "wg2": gap_rows(i["L0_attn_Wg2"].T).transpose(2, 1, 0),
        "wo_gap": np.stack([gap_rows(i["L0_attn_Wo"]), gap_rows(i["L1_attn_wo"].T)], axis=1),
        "normw": gap_rows(i["L0_attn_norm_w"].reshape(D, 1))[:, :, 0],
        "xb_l": np.concatenate([ctxT, np.broadcast_to(xw[64:, None, None], half)]),
        "xb_r": np.concatenate([np.broadcast_to(xw[:64, None, None], half), ctxT]),
        "xb_b": np.broadcast_to(i["L0_xattn_b"].reshape(1, 1), (P, 1)),
        "wqkv1": np.stack([rows_to_lhs(w.T) for w in (wq, wq[swap], wk, wk[swap], wv)], axis=1),
        "gate0": rows_to_lhs(i["L0_ffn_gate_w"].T),
        "gate1": rows_to_lhs(i["L1_ffn_gate_w"].T),
        "wx": cross_pack(i),
        "cx": cross_constants(),
        "kvc": np.stack([np.concatenate([ctxT, ctxT]), np.concatenate([ctxT[turn], ctxT[turn]])], axis=1),
        "ffn0": expert_pack(i["L0_ffn_w1"], i["L0_ffn_w2"], i["L0_ffn_shared_w1"], i["L0_ffn_shared_w2"]),
        "ffn1": expert_pack(i["L1_ffn_w13"], i["L1_ffn_w2"], i["L1_ffn_sw13"], i["L1_ffn_sw2"]),
    }


def kernel(**inputs):
    import numpy as _np
    import concourse.bacc as _bacc
    from concourse import mybir as _mybir
    from concourse.bass_utils import run_bass_kernel_spmd as _run

    nc = _bacc.Bacc("TRN2", target_bir_lowering=False, num_devices=1)
    arrays, aps = {}, {}
    for name, a in lay_out(inputs).items():
        a = _np.ascontiguousarray(a)
        arrays[f"in_{name}"] = a
        aps[name] = nc.dram_tensor(f"in_{name}", a.shape, _mybir.dt.from_np(a.dtype), kind="ExternalInput").ap()
    out = nc.dram_tensor("out", (NB, SEQ, D), F32, kind="ExternalOutput").ap()
    build(nc, aps, out, STAGES)
    r = _run(nc, [arrays], core_ids=[0])
    return r.results[0]["out"]
```

```python
from contextlib import ExitStack

import numpy as np

import concourse.bass as bass
from concourse import mybir

F32 = mybir.dt.float32
F32R = mybir.dt.float32r
BF16 = mybir.dt.bfloat16
ALU = mybir.AluOpType
ACT = mybir.ActivationFunctionType
AX = mybir.AxisListType.X

P = 128
D = 256
NB, SEQ = 4, 256
TILES = NB * SEQ // P
KD = D // P
HEADS, HD = 16, 16
EPS = 1e-5
NEG = -1e30
HALF = 512

E, TOP_K, INNER, SHARED = 16, 6, 176, 352
CHUNKS = -(-(E * INNER + SHARED) // P)
PACK = 4 * 128 + 256 + 128
RING = 5

XH, XK, XQ, XR, XC = 16, 128, 192, 64, 64
GROUPS = XH // 4
LO = XQ // 2

def pack_layout():
    at, n = {}, 0
    for name, width in (("wq", 4 * D), ("kcq", 4 * XQ), ("qrT", 2 * 4 * LO), ("krT", 4 * XC), ("kckv", 4 * XC), ("woT", 4 * D)):
        at[name] = (n, n + width)
        n += width
    return at, n


XP, XPACK = pack_layout()


def cx_layout():
    at, n = {}, 0
    for name, width in (("cosq", 3 * 2 * SEQ), ("sinq", 3 * 2 * SEQ), ("coskv", SEQ), ("sinkv", SEQ), ("gmask", 6), ("slot2", 2)):
        at[name] = (n, n + width)
        n += width
    return at, n


CX, CX_W = cx_layout()

STAGES = 6


def const_layout():
    at, n = {}, 0
    for name, width in (("ident", 128), ("dist", SEQ), ("causal", SEQ), ("neg_qs", 128),
                        ("even", 1), ("odd", 1), ("even_s", 1), ("odd_s", 1), ("block_ones", 128), ("pick16", 128), ("ones", 128),
                        ("cos", SEQ), ("sin", SEQ)):
        at[name] = (n, n + width)
        n += width
    return at, n


CONST, CONST_W = const_layout()


def build(nc, d, out, stages):
    with ExitStack() as ctx:
        def sb(name, shape, dt=F32, c=ctx):
            return c.enter_context(nc.sbuf_tensor(name, shape, dt))

        def sem(name):
            return ctx.enter_context(nc.semaphore(name))

        ps = ctx.enter_context(nc.psum_tensor("ps", [P, 8, 512], F32))

        X = sb("X", [P, TILES, D])
        xn = sb("xn", [P, TILES, D])
        cst = sb("cst", [P, CONST_W])
        stats = sb("stats", [P, TILES, 6])
        mv = sb("mv", [P, TILES, 2])
        sd = sb("sd", [P, TILES])
        rstd = sb("rstd", [P, TILES])
        epsc = sb("epsc", [P, 1])
        identb = sb("identb", [P, 128], BF16)
        negqs = sb("negqs", [P, 128], BF16)

        def k(name):
            a, b = CONST[name]
            return cst[:, a:b]

        ident = k("ident")

        a_ctx = ctx.enter_context(ExitStack())
        wqkv0 = sb("wqkv0", [P, 3, KD, D])
        wg1 = sb("wg1", [P, KD, HD])
        wg2 = sb("wg2", [HD, 4, 128])
        wo_gap = sb("wo_gap", [P, 2, 4, D])
        normw = sb("normw", [P, 4])
        ld_bc = sb("ld_bc", [P, HEADS])
        xT4 = sb("xT4", [P, KD, NB, SEQ])
        xb_l, xb_r = xT4[:, 0], xT4[:, 1]
        xb_b = sb("xb_b", [P, 1])
        kT = sb("kT", [P, 2, SEQ])
        wqkv1 = sb("wqkv1", [P, 5, KD, D])

        phase = ExitStack()
        with phase:
            qT = sb("qT", [P, NB, 2, SEQ], c=phase)
            kE = sb("kE", [P, NB, 2, SEQ], c=phase)
            kO = sb("kO", [P, NB, 2, SEQ], c=phase)
            vpad = sb("vpad", [P, TILES, HEADS, 32], c=phase)
            P0 = sb("P0", [P, 2, 4, 2, 256], c=phase)
            P1 = sb("P1", [P, 2, 4, 2, 128], c=phase)
            sg = sb("sg", [P, 4, 512], c=phase)
            og = sb("og", [P, 2, 512], c=phase)
            rrec = sb("rrec", [P, 2, 512], c=phase)
            on = sb("on", [P, 4, SEQ], c=phase)
            with ExitStack() as layer0:
                DT = sb("DT", [P, HEADS, SEQ], c=layer0)
                g1S = sb("g1S", [HD, NB, SEQ], c=layer0)
                sgate = sb("sgate", [P, NB, 2, 512], c=layer0)
                sq = sb("sq", [P, 2, 512], c=layer0)
                rms = sb("rms", [P, 2, 512], c=layer0)
                xsig = sb("xsig", [P, 2, 256], c=layer0)
            with ExitStack() as layer1:
                nm = sb("nm", [P, 2, 2, 4, 2], c=layer1)
                Q0 = sb("Q0", [P, 2, 4, 2, 128], c=layer1)
                Q1 = sb("Q1", [P, 2, 4, 2, 256], c=layer1)
        phase = ExitStack()
        with phase:
            xTh = sb("xTh", [P, KD, 2, HALF], F32R, c=phase)
            xTl = sb("xTl", [P, KD, 2, HALF], F32R, c=phase)
            raw = sb("raw", [P, RING, PACK], c=phase)
            whi = sb("whi", [P, RING, PACK], F32R, c=phase)
            wlo = sb("wlo", [P, RING, PACK - 128], F32R, c=phase)
            sl = sb("sl", [P, 2, HALF], c=phase)
            h1 = sb("h1", [P, 2, HALF], c=phase)
            h2 = sb("h2", [P, 2, HALF], c=phase)
            ahi = sb("ahi", [P, 2, HALF], F32R, c=phase)
            alo = sb("alo", [P, 2, HALF], F32R, c=phase)
            CT = sb("CT", [64, 2, HALF], F32R, c=phase)
            gwr = sb("gwr", [P, KD, E], c=phase)
            gwh = sb("gwh", [P, KD, E], F32R, c=phase)
            gwl = sb("gwl", [P, KD, E], F32R, c=phase)
            lgT = sb("lgT", [E, 2, HALF], c=phase)
            nmx = sb("nmx", [P, TILES], c=phase)
            lgs = sb("lgs", [P, TILES, E], c=phase)
            ex = sb("ex", [P, TILES, E], c=phase)
            den = sb("den", [P, 2, TILES], c=phase)
            prob = sb("prob", [P, TILES, 18], c=phase)
            v8 = sb("v8", [P, TILES, 8], c=phase)
            left = sb("left", [P, TILES, 18], c=phase)
            comb = sb("comb", [P, TILES, 17], c=phase)
            zeros = sb("zeros", [P, HALF], F32R, c=phase)
            yS = sb("yS", [P, 2, 2, HALF], c=phase)

        phase = ExitStack()
        with phase:
            Aw = sb("Aw", [P, GROUPS, KD, 2, 4 * LO], c=phase)
            Gm = sb("Gm", [P, GROUPS, 2, 4, 128], c=phase)
            MM = sb("MM", [P, GROUPS, 2, D], c=phase)
            cx = sb("cx", [P, CX_W], c=phase)
            rr = sb("rr", [P, 2 * 3 * 512], c=phase)
            kvT = sb("kvT", [P, NB, SEQ], c=phase)
            kvaug = sb("kvaug", [P, TILES, 2, 128], c=phase)
            r1, r2 = (rr[:, 1536 * n:1536 * n + 1536].rearrange("p (j s) -> p j s", j=3) for n in range(2))
            kvc = rr[:, 0:2 * NB * SEQ].rearrange("p (a b s) -> p a b s", a=2, b=NB)
            qr = sb("qr", [P, 3, 2, SEQ], c=phase)
            tS = sb("tS", [P, 2, SEQ], c=phase)
            nmq = sb("nmq", [P, 2, 2, 64], c=phase)
            BDx = sb("BDx", [P, 2, SEQ], F32R, c=phase)
            onesx = sb("onesx", [P, 128], F32R, c=phase)
            Px = sb("Px", [P, 2, 2, 512], c=phase)
            recx = sb("recx", [P, 512], c=phase)
            ctxS = sb("ctxS", [P, 2, SEQ], c=phase)
            wx = sb("wx", [P, 2, XPACK], c=phase)

        def kx(name):
            a, b = CX[name]
            return cx[:, a:b]

        x_loaded = [sem(f"x_loaded{b}") for b in range(NB)]
        const_loaded = sem("const_loaded")
        w0_loaded, w1_loaded, xb_loaded = map(sem, ("w0_loaded", "w1_loaded", "xb_loaded"))
        x_done = sem("x_done")
        norm_stats, norm_var, norm_sd, norm_rstd, norm_done = map(sem, ("norm_stats", "norm_var", "norm_sd", "norm_rstd", "norm_done"))
        eps_ready = sem("eps_ready")
        setup_v = sem("setup_v")
        dt_exp = sem("dt_exp")
        dt_ready = sem("dt_ready")
        pe_xt, xt_ready, pe_q, pe_k, pe_v, pe_g1, pe_gate, pe_f = map(sem, ("pe_xt", "xt_ready", "pe_q", "pe_k", "pe_v", "pe_g1", "pe_gate", "pe_f"))
        sig_done, g1_ready, gate_ready, q_ready, k_ready, v_ready = map(sem, ("sig_done", "g1_ready", "gate_ready", "q_ready", "k_ready", "v_ready"))
        rope_done, k_sum = map(sem, ("rope_done", "k_sum"))
        pe_s, p_done, max_done, pe_ta, ta_copied, pe_tb, tb_copied = map(
            sem, ("pe_s", "p_done", "max_done", "pe_ta", "ta_copied", "pe_tb", "tb_copied"))
        pe_o, og_ready, sq_ready, pe_ss, rms_ready, rec_ready, on_ready, pe_out = map(
            sem, ("pe_o", "og_ready", "sq_ready", "pe_ss", "rms_ready", "rec_ready", "on_ready", "pe_out"))
        pe_xb, xsig_ready, xb_part = map(sem, ("pe_xb", "xsig_ready", "xb_part"))
        out_done = sem("out_done")
        wx_in = [sem(f"wx_in{u}") for u in range(2)]
        cx_in, kvc_in = sem("cx_in"), sem("kvc_in")
        (x_zero, x_kvm, x_kv, x_pekv, x_kvt, x_pea, x_a, x_peg, x_g, x_pem, x_mm, x_q, x_r, x_qr, x_t, x_ts, x_m, x_max, x_nmt,
         x_bd, x_s, x_p, x_c, x_rec, x_ctx, x_o) = map(sem, (
            "x_zero", "x_kvm", "x_kv", "x_pekv", "x_kvt", "x_pea", "x_a", "x_peg", "x_g", "x_pem", "x_mm", "x_q", "x_r", "x_qr", "x_t",
            "x_ts", "x_m", "x_max", "x_nmt", "x_bd", "x_s", "x_p", "x_c", "x_rec", "x_ctx", "x_o"))
        ld_loaded = sem("ld_loaded")
        pad_ready = sem("pad_ready")
        f_pe_xt, f_hi, f_lo, f_lgT, f_lgTs, f_lg, f_d, f_ex, f_v, f_combT, f_cth, f_ctl = map(
            sem, ("f_pe_xt", "f_hi", "f_lo", "f_lgT", "f_lgTs", "f_lg", "f_d", "f_ex", "f_v", "f_combT", "f_cth", "f_ctl"))
        f_gw, f_gwh, f_gwl = map(sem, ("f_gw", "f_gwh", "f_gwl"))
        f_ones = sem("f_ones")
        raw_in = [[sem(f"raw_in{l}_{u}") for u in range(RING)] for l in range(2)]
        w_hi, w_lo = [[sem(f"{n}{l}") for l in range(2)] for n in ("w_hi", "w_lo")]
        s_g, s_u, s_c, s_silu, s_t2, s_t3, s_ahi, s_alo, s_y = [
            [sem(f"{n}{l}") for l in range(2)] for n in ("s_g", "s_u", "s_c", "s_silu", "s_t2", "s_t3", "s_ahi", "s_alo", "s_y")]
        f_ys, f_yt = sem("f_ys"), sem("f_yt")

        block = ctx.enter_context(nc.Block())

        N_FV = 24
        HALVES = 2 * NB
        SLOTS = 6
        FIRST = (4, 4)
        TURN = (4, 3)

        def score_bank(l, n):
            return FIRST[l] + n % TURN[l]

        def value_bank(l, b, m):
            return m if l else 2 * (b % 2) + m

        def out_bank(l, b):
            return 7 if l else 2 * (b % 2) + 1
        UNITS = NB * GROUPS

        def blocks(eng):
            with eng.Fori(0, CHUNKS // RING - 1) as i:
                yield i, False
            yield CHUNKS // RING - 1, True

        @block.sync
        def _(sp):
            xf = d["x"].rearrange("b n d -> (b n) d").rearrange("(t p) d -> p t d", p=P)
            for b in range(NB):
                sp.dma_start(X[:, 2 * b:2 * b + 2, :], xf[:, 2 * b:2 * b + 2, :]).then_inc(x_loaded[b], 16)
            sp.dma_start(cst[:, :], d["const"]).then_inc(const_loaded, 16)
            sp.dma_start(wqkv0[:, :, :, :], d["wqkv0"]).then_inc(w0_loaded, 16)
            sp.dma_start(wg1[:, :, :], d["wg1"]).then_inc(w0_loaded, 16)
            sp.dma_start(wg2[:, :, :], d["wg2"]).then_inc(w0_loaded, 16)
            sp.dma_start(wo_gap[:, :, :, :], d["wo_gap"]).then_inc(w0_loaded, 16)
            sp.dma_start(normw[:, :], d["normw"]).then_inc(w0_loaded, 16)
            sp.dma_start(xb_b[:, :], d["xb_b"]).then_inc(xb_loaded, 16)
            sp.dma_start(wqkv1[:, :, :, :], d["wqkv1"]).then_inc(w1_loaded, 16)
            sp.wait_ge(pe_gate, NB)
            sp.dma_start(xb_l[:, :, :], d["xb_l"]).then_inc(xb_loaded, 16)
            sp.dma_start(xb_r[:, :, :], d["xb_r"]).then_inc(xb_loaded, 16)
            for l in range(2):
                stage = 2 + 3 * l
                if stage >= stages:
                    break
                W = d[f"ffn{l}"]
                sp.wait_ge(x_done, 8 * stage)
                sp.dma_start(gwr[:, :, :], d[f"gate{l}"]).then_inc(f_gw, 16)
                for c in range(RING):
                    sp.dma_start(raw[:, c, :], W[c, :, :]).then_inc(raw_in[l][c], 16)
                with sp.Fori(0, CHUNKS // RING - 1) as i:
                    for u in range(RING):
                        c = i * RING + u
                        sp.wait_ge(w_lo[l], c + 1)
                        sp.dma_start(raw[:, u, :], W[bass.ds(c + RING, 1), :, :].rearrange("a p n -> p (a n)")).then_inc(raw_in[l][u], 16)
                if l == 0 and stages >= 5:
                    sp.wait_ge(x_done, 8 * 3)
                    for hg in range(2):
                        sp.dma_start(wx[:, hg, :], d["wx"][hg, :, :]).then_inc(wx_in[hg], 16)
                    sp.wait_ge(x_done, 8 * 4)
                    sp.dma_start(kvc[:, :, :, :], d["kvc"]).then_inc(kvc_in, 16)
                    sp.dma_start(cx[:, :], d["cx"]).then_inc(cx_in, 16)
                    for hg in range(2, GROUPS):
                        sp.wait_ge(x_mm, hg - 1)
                        sp.dma_start(wx[:, hg % 2, :], d["wx"][hg, :, :]).then_inc(wx_in[hg % 2], 16)
            of = out.rearrange("b n d -> (b n) d").rearrange("(t p) d -> p t d", p=P)
            for b in range(NB):
                sp.wait_ge(x_done, 8 * (stages - 1) + 2 * b + 2)
                sp.dma_start(of[:, 2 * b:2 * b + 2, :], X[:, 2 * b:2 * b + 2, :]).then_inc(out_done, 16)
            sp.wait_ge(out_done, 16 * NB)

        @block.vector
        def _(v):
            def norm(n):
                for t in range(TILES):
                    if n == 0:
                        v.wait_ge(x_loaded[t // 2], 16)
                    else:
                        v.wait_ge(x_done, 8 * (n - 1) + t + 1)
                    v.bn_stats(stats[:, t, :], X[:, t, :]).then_inc(norm_stats, 1)
                for t in range(TILES):
                    v.wait_ge(norm_stats, 8 * n + t + 1)
                    v.bn_aggr(mv[:, t, :], stats[:, t, :]).then_inc(norm_var, 1)
                v.wait_ge(norm_sd, n + 1)
                v.reciprocal(rstd[:, :], sd[:, :]).then_inc(norm_rstd, 1)
                v.wait_ge(norm_rstd, n + 1)
                for t in range(TILES):
                    v.tensor_scalar(xn[:, t, :], X[:, t, :], mv[:, t, 0:1], rstd[:, t:t + 1],
                                    ALU.subtract, ALU.mult).then_inc(norm_done, 1)

            def flat(x):
                return x.rearrange("p m s -> p (m s)")

            def project0(b):
                v.wait_ge(sig_done, 3 * b + 1)
                v.tensor_tensor(flat(qT[:, b]), ps[:, 0, :], sg[:, 0, :], ALU.mult).then_inc(q_ready, 1)
                v.wait_ge(sig_done, 3 * b + 2)
                v.scalar_tensor_tensor(flat(kE[:, b]), ps[:, 1, :], k("even"), sg[:, 1, :], ALU.mult, ALU.mult).then_inc(k_ready, 1)
                v.scalar_tensor_tensor(flat(kO[:, b]), ps[:, 1, :], k("odd"), sg[:, 1, :], ALU.mult, ALU.mult).then_inc(k_ready, 1)
                v.wait_ge(sig_done, 3 * b + 3)
                if b == 0:
                    v.wait_ge(pad_ready, 1)
                for st in range(2):
                    v.tensor_tensor(vpad[:, 2 * b + st, :, 0:HD], ps[:, 2, 256 * st:256 * st + 256].rearrange("p (h e) -> p h e", h=HEADS),
                                    sg[:, 2, 256 * st:256 * st + 256].rearrange("p (h e) -> p h e", h=HEADS), ALU.mult).then_inc(v_ready, 1)

            def project1(b):
                for j, tab in enumerate(("cos", "sin", "cos", "sin")):
                    v.wait_ge(pe_f, 4 * b + j + 1)
                    if b >= 1:
                        v.wait_ge(q_ready if j < 2 else k_sum, 4 + b if j < 2 else b)
                    v.tensor_tensor(sg[:, j, :].rearrange("p (m s) -> p m s", m=2), ps[:, j, :].rearrange("p (m s) -> p m s", m=2),
                                    k(tab).unsqueeze(1).to_broadcast([P, 2, SEQ]), ALU.mult).then_inc(rope_done, 1)

            def recip(l, b, m):
                if l == 0:
                    v.wait_ge(rms_ready, 2 * b + m + 1)
                    v.reciprocal(rrec[:, m, :], rms[:, m, :]).then_inc(rec_ready, 1)
                else:
                    v.wait_ge(pe_ss, HALVES + 2 * b + m + 1)
                    v.reciprocal(rrec[:, m, :], ps[:, m, :]).then_inc(rec_ready, 1)

            def scaled(l, b, m):
                v.wait_ge(rec_ready, HALVES * l + 2 * b + m + 1)
                if b >= 1:
                    v.wait_ge(pe_out, NB * l + b)
                for e in range(2):
                    c = slice(256 * e, 256 * e + 256)
                    if l == 0:
                        v.scalar_tensor_tensor(on[:, 2 * m + e, :], og[:, m, c], normw[:, 2 * m + e:2 * m + e + 1], rrec[:, m, c],
                                               ALU.mult, ALU.mult).then_inc(on_ready, 1)
                    else:
                        v.tensor_tensor(on[:, 2 * m + e, :], og[:, m, c], rrec[:, m, c], ALU.mult).then_inc(on_ready, 1)

            def add_out(l, b):
                v.wait_ge(pe_out, NB * l + b + 1)
                for t in range(2):
                    v.tensor_tensor(X[:, 2 * b + t, :], X[:, 2 * b + t, :], ps[:, out_bank(l, b), 256 * t:256 * t + 256], ALU.add).then_inc(x_done, 1)

            def decayed(u, j):
                n = SLOTS * u + j
                v.wait_ge(pe_s, n + 1)
                bank = ps[:, score_bank(0, n), :]
                if j < 4:
                    h = 8 * (j // 2) + 2 * (2 * (u % 2) + j % 2)
                    v.tensor_tensor(P0[:, u % 2, j, :, :], bank.rearrange("p (e q) -> p e q", e=2), DT[:, h:h + 2, :], ALU.mult).then_inc(p_done, 1)
                else:
                    h = 2 * (2 * (u % 2) + j - 4)
                    v.tensor_tensor(P1[:, u % 2, j - 4::2, :, :], bank.rearrange("p (m e q) -> p m e q", m=2, e=2),
                                    DT[:, :, 0:128].rearrange("p (m h) q -> p m h q", m=2)[:, :, h:h + 2, :], ALU.mult).then_inc(p_done, 1)

            def row_max(u, j):
                n = SLOTS * u + j
                v.wait_ge(pe_s, SLOTS * HALVES + n + 1)
                bank = ps[:, score_bank(1, n), :]
                if j < 2:
                    v.tensor_reduce(nm[:, u % 2, 0, j::2, :], bank.rearrange("p (m e s) -> p m e s", m=2, e=2), AX, ALU.max, negate=True).then_inc(max_done, 1)
                else:
                    v.tensor_reduce(nm[:, u % 2, 1, j - 2, :], bank.rearrange("p (e s) -> p e s", e=2), AX, ALU.max, negate=True).then_inc(max_done, 1)

            def copy_transposed(u, g):
                n = 4 * u + g
                v.wait_ge(pe_ta, n + 1)
                v.tensor_copy(P0[:, u % 2, g, :, :].rearrange("p e q -> p (e q)"), ps[:, 2 + n % 2, :]).then_inc(ta_copied, 1)

            def attention0():
                for b in range(NB):
                    project0(b)
                v.wait_ge(dt_ready, 1)
                for u in range(HALVES + 2):
                    b = u // 2 - 1
                    for j in range(SLOTS):
                        if u < HALVES:
                            decayed(u, j)
                        if b < 0:
                            continue
                        if u % 2 == 0 and j in (2, 3):
                            m = j - 2
                            v.wait_ge(pe_o, 2 * b + 2)
                            v.wait_ge(gate_ready, NB)
                            v.tensor_tensor(og[:, m, :], ps[:, value_bank(0, b, m), :], sgate[:, b, m, :], ALU.mult).then_inc(og_ready, 1)
                        if (u % 2, j) == (0, 5):
                            recip(0, b, 0)
                        if (u % 2, j) == (1, 0):
                            scaled(0, b, 0)
                        if (u % 2, j) == (1, 1):
                            recip(0, b, 1)
                        if (u % 2, j) == (1, 2):
                            scaled(0, b, 1)
                        if (u % 2, j) == (1, 5):
                            add_out(0, b)

            def attention1():
                for b in range(NB):
                    project1(b)
                for u in range(HALVES + 3):
                    for j in range(SLOTS):
                        if u < HALVES:
                            row_max(u, j)
                        if j < 4 and 1 <= u <= HALVES:
                            copy_transposed(u - 1, j)
                        b = (u - 3) // 2
                        if u >= 3 and u % 2:
                            if j in (1, 3):
                                recip(1, b, j // 2)
                            if j in (2, 4):
                                scaled(1, b, j // 2 - 1)
                        if u >= 4 and (u % 2, j) == (0, 0):
                            add_out(1, b)

            def experts(l):
                for kk in range(KD):
                    for hf in range(2):
                        n = 2 * kk + hf
                        v.wait_ge(f_hi, 4 * l + n + 1)
                        v.tensor_tensor(xTl[:, kk, hf, :], ps[:, n, :], xTh[:, kk, hf, :].bitcast(F32), ALU.subtract).then_inc(f_lo, 1)
                v.wait_ge(f_gwh, l + 1)
                v.tensor_tensor(gwl[:, :, :], gwr[:, :, :], gwh[:, :, :].bitcast(F32), ALU.subtract).then_inc(f_gwl, 1)
                for c in range(2):
                    split_lo(l, c, c)
                v.wait_ge(f_lg, l + 1)
                lg = ps[:, 6, 0:TILES * E].rearrange("p (t e) -> p t e", t=TILES)
                v.tensor_reduce(nmx[:, :], lg, AX, ALU.max, negate=True).then_inc(f_v, 1)
                base = N_FV * l
                v.wait_ge(f_v, base + 1)
                v.tensor_tensor(lgs[:, :, :], lg, nmx[:, :].unsqueeze(2).to_broadcast([P, TILES, E]), ALU.add).then_inc(f_d, 1)
                v.wait_ge(f_ex, l + 1)
                v.tensor_reduce(den[:, 0, :], ex[:, :, :], AX, ALU.add).then_inc(f_v, 1)
                v.memset(prob[:, :, E:18], -1.0).then_inc(f_v, 1)
                v.memset(comb[:, :, E:17], 1.0).then_inc(f_v, 1)
                v.wait_ge(f_v, base + 4)
                v.reciprocal(den[:, 1, :], den[:, 0, :]).then_inc(f_v, 1)
                v.wait_ge(f_v, base + 5)
                v.tensor_tensor(prob[:, :, 0:E], ex[:, :, :], den[:, 1, :].unsqueeze(2).to_broadcast([P, TILES, E]), ALU.mult).then_inc(f_v, 1)
                v.wait_ge(f_v, base + 6)
                for t in range(TILES):
                    v.max(v8[:, t, :], prob[:, t, 0:E]).then_inc(f_v, 1)
                v.wait_ge(f_v, base + 14)
                v.memset(v8[:, :, TOP_K:8], -1.0).then_inc(f_v, 1)
                v.wait_ge(f_v, base + 15)
                for t in range(TILES):
                    v.match_replace(left[:, t, :], v8[:, t, :], prob[:, t, :], 0.0).then_inc(f_v, 1)
                v.wait_ge(f_v, base + 23)
                v.tensor_tensor(comb[:, :, 0:E], prob[:, :, 0:E], left[:, :, 0:E], ALU.subtract).then_inc(f_v, 1)
                v.wait_ge(f_v, base + 24)
                if l == 1:
                    v.tensor_reduce(den[:, 0, :], comb[:, :, 0:E], AX, ALU.add).then_inc(f_v, 1)
                    v.wait_ge(f_v, base + 25)
                    v.tensor_scalar(den[:, 0, :], den[:, 0, :], 1e-20, None, ALU.add).then_inc(f_v, 1)
                    v.wait_ge(f_v, base + 26)
                    v.reciprocal(den[:, 1, :], den[:, 0, :]).then_inc(f_v, 1)
                    v.wait_ge(f_v, base + 27)
                    v.tensor_tensor(comb[:, :, 0:E], comb[:, :, 0:E], den[:, 1, :].unsqueeze(2).to_broadcast([P, TILES, E]), ALU.mult).then_inc(f_v, 1)
                for hf in range(2):
                    v.wait_ge(f_cth, 2 * l + hf + 1)
                    v.tensor_tensor(CT[32:49, hf, :], ps[0:17, 6 + hf, :], CT[0:17, hf, :].bitcast(F32), ALU.subtract).then_inc(f_ctl, 1)
                for i, last in blocks(v):
                    for u in range(2 * RING):
                        n = i * (2 * RING) + u
                        c = i * RING + u // 2
                        v.wait_ge(s_silu[l], n + 1)
                        v.wait_ge(s_u[l], n + 1)
                        v.tensor_tensor(h1[:, u % 2, :], ps[:, 5, :], sl[:, u % 2, :], ALU.mult).then_inc(s_t2[l], 1)
                        v.wait_ge(s_c[l], n + 1)
                        v.wait_ge(s_t2[l], n + 1)
                        v.tensor_tensor(h2[:, u % 2, :], ps[:, 6, :], h1[:, u % 2, :], ALU.mult).then_inc(s_t3[l], 1)
                        v.wait_ge(s_ahi[l], n + 1)
                        v.tensor_tensor(alo[:, u % 2, :], h2[:, u % 2, :], ahi[:, u % 2, :].bitcast(F32), ALU.subtract).then_inc(s_alo[l], 1)
                        if u % 2 == 0 and not (last and u // 2 + 2 >= RING):
                            split_lo(l, c + 2, (u // 2 + 2) % RING)
                for t in range(TILES):
                    v.wait_ge(f_yt, 4 * l + t // 2 + 1)
                    v.tensor_tensor(X[:, t, :], X[:, t, :], ps[:, 4 + t // 2, 256 * (t % 2):256 * (t % 2) + 256], ALU.add).then_inc(x_done, 1)

            def split_lo(l, c, slot):
                v.wait_ge(w_hi[l], c + 1)
                v.tensor_tensor(wlo[:, slot, :], raw[:, slot, 0:PACK - 128], whi[:, slot, 0:PACK - 128].bitcast(F32), ALU.subtract).then_inc(w_lo[l], 1)

            def cross():
                v.wait_ge(norm_done, 8 * 5)
                v.memset(Gm[:, :, :, :, :], 0.0).then_inc(x_zero, 1)
                v.memset(nmq[:, :, :, :], 0.0).then_inc(x_zero, 1)
                v.memset(kvaug[:, :, :, :], 1.0).then_inc(x_zero, 1)
                v.tensor_copy(onesx[:, :], k("ones")).then_inc(x_zero, 1)
                v.wait_ge(kvc_in, 16)
                v.wait_ge(cx_in, 16)
                for j, tab in enumerate(("coskv", "sinkv")):
                    v.tensor_tensor(kvc[:, j, :, :], kvc[:, j, :, :], kx(tab).unsqueeze(1).to_broadcast([P, NB, SEQ]), ALU.mult).then_inc(x_kvm, 1)
                v.wait_ge(x_kvm, 2)
                v.tensor_tensor(kvT[:, :, :], kvc[:, 0, :, :], kvc[:, 1, :, :], ALU.add).then_inc(x_kv, 1)
                v.wait_ge(x_pekv, 1)
                v.wait_ge(x_zero, 4)
                kv_tok = ps[:, 7, :].rearrange("p (t c) -> p t c", t=TILES)
                v.tensor_copy(kvaug[:, :, 0, 0:XC], kv_tok).then_inc(x_kvt, 1)
                v.tensor_copy(kvaug[:, :, 1, XC:128], kv_tok).then_inc(x_kvt, 1)
                gm = kx("gmask").rearrange("p (j e) -> p j e", j=3)
                for hg in range(GROUPS):
                    for part in range(2):
                        v.wait_ge(x_peg, 2 * hg + part + 1)
                        for piece, j, e in ((0, 0, 0), (0, 0, 1), (1, 1, 0), (2, 1, 1), (3, 2, 0), (3, 2, 1)):
                            col = XC * ((j + e) % 2)
                            v.tensor_scalar(Gm[:, hg, part, piece, col:col + XC], ps[:, 4 + part, 128 * j + XC * e:128 * j + XC * e + XC],
                                            gm[:, j, e:e + 1], None, ALU.mult).then_inc(x_g, 1)

                def rope(w, j):
                    n = 3 * w + j
                    v.wait_ge(x_q, n + 1)
                    if w >= 1:
                        v.wait_ge(x_qr, 2 * (n - 3) + 2)
                    v.tensor_tensor(r1[:, j, :], ps[:, n % 2, :], kx("cosq")[:, 512 * j:512 * j + 512], ALU.mult).then_inc(x_r, 1)
                    v.tensor_tensor(r2[:, j, :], ps[:, n % 2, :], kx("sinq")[:, 512 * j:512 * j + 512], ALU.mult).then_inc(x_r, 1)

                def row_max(w, n):
                    v.wait_ge(x_m, 4 * w + n + 1)
                    v.tensor_reduce(nmq[:, n // 2, n % 2, 0:2], ps[:, 3 + n % 2, :].rearrange("p (e s) -> p e s", e=2),
                                    AX, ALU.max, negate=True).then_inc(x_max, 1)

                def contexts(w):
                    for ab in range(2):
                        mine, other = slice(64 * ab, 64 * ab + 64), slice(64 - 64 * ab, 128 - 64 * ab)
                        v.wait_ge(x_c, 2 * w + ab + 1)
                        v.reciprocal(recx[mine, :], ps[other, 5 + ab, :]).then_inc(x_rec, 1)
                        v.wait_ge(x_rec, 2 * w + ab + 1)
                        if w >= 1:
                            v.wait_ge(x_o, w)
                        v.tensor_tensor(ctxS[mine, :, :].rearrange("p e s -> p (e s)"), ps[mine, 5 + ab, :], recx[mine, :], ALU.mult).then_inc(x_ctx, 1)

                def add_output(b):
                    v.wait_ge(x_o, GROUPS * (b + 1))
                    for t in range(2):
                        v.tensor_tensor(X[:, 2 * b + t, :], X[:, 2 * b + t, :], ps[:, 7, 256 * t:256 * t + 256], ALU.add).then_inc(x_done, 1)

                for j in range(3):
                    rope(0, j)
                for w in range(UNITS):
                    more = w + 1 < UNITS
                    if w >= 1:
                        contexts(w - 1)
                    if more:
                        rope(w + 1, 0)
                    row_max(w, 0)
                    row_max(w, 1)
                    if more:
                        rope(w + 1, 1)
                    row_max(w, 2)
                    row_max(w, 3)
                    v.wait_ge(x_nmt, w + 1)
                    v.tensor_tensor(BDx[:, :, :], ps[:, 2, 0:SEQ].unsqueeze(1).to_broadcast([P, 2, SEQ]),
                                    kx("slot2").unsqueeze(2).to_broadcast([P, 2, SEQ]), ALU.mult).then_inc(x_bd, 1)
                    if more:
                        rope(w + 1, 2)
                    if w % GROUPS == 0 and w:
                        add_output(w // GROUPS - 1)
                contexts(UNITS - 1)
                add_output(NB - 1)

            v.memset(epsc[:, :], EPS).then_inc(eps_ready, 1)
            norm(0)
            v.wait_ge(dt_exp, HEADS)
            v.tensor_tensor(DT[:, :, :], DT[:, :, :], k("causal").unsqueeze(1).to_broadcast([P, HEADS, SEQ]), ALU.mult).then_inc(dt_ready, 1)
            attention0()
            if stages >= 2:
                norm(1)
                for t in range(TILES):
                    v.wait_ge(xsig_ready, t + 1)
                    v.scalar_tensor_tensor(X[:, t, :], xsig[:, t % 2, :], 0.6, X[:, t, :], ALU.mult, ALU.add).then_inc(xb_part, 1)
                    v.wait_ge(xb_part, t + 1)
                    v.wait_ge(norm_done, 8 + t + 1)
                    v.scalar_tensor_tensor(X[:, t, :], xn[:, t, :], 1.0 - 0.6, X[:, t, :], ALU.mult, ALU.add).then_inc(x_done, 1)
            if stages >= 3:
                norm(2)
                experts(0)
            if stages >= 4:
                norm(3)
                v.tensor_copy(identb[:, :], ident).then_inc(setup_v, 1)
                v.tensor_copy(negqs[:, :], k("neg_qs")).then_inc(setup_v, 1)
                attention1()
            if stages >= 5:
                norm(4)
                cross()
            if stages >= 6:
                norm(5)
                experts(1)

        @block.scalar
        def _(a):
            def norm(n):
                if n == 0:
                    a.wait_ge(eps_ready, 1)
                a.wait_ge(norm_var, 8 * (n + 1))
                a.activation(sd[:, :], mv[:, :, 1], ACT.Sqrt, bias=epsc[:, 0:1]).then_inc(norm_sd, 1)

            def transposed_tokens(i, b):
                a.wait_ge(pe_xt, i + 1)
                a.activation(xT4[:, :, b, :], ps[:, 7, :].rearrange("p (k s) -> p k s", k=KD), ACT.Copy).then_inc(xt_ready, 1)

            def attention0():
                transposed_tokens(0, 0)
                for b in range(NB):
                    if b + 1 < NB:
                        transposed_tokens(b + 1, b + 1)
                    a.wait_ge(pe_q, b + 1)
                    a.activation(sg[:, 0, :], ps[:, 0, :], ACT.Sigmoid).then_inc(sig_done, 1)
                    if b >= 1:
                        gate(b - 1)
                    a.wait_ge(pe_k, b + 1)
                    a.activation(sg[:, 1, :], ps[:, 1, :], ACT.Sigmoid).then_inc(sig_done, 1)
                    a.wait_ge(pe_v, b + 1)
                    a.activation(sg[:, 2, :], ps[:, 2, :], ACT.Sigmoid).then_inc(sig_done, 1)
                    a.wait_ge(pe_g1, b + 1)
                    a.activation(g1S[:, b, :], ps[0:HD, 3, 0:SEQ], ACT.Copy).then_inc(g1_ready, 1)
                gate(NB - 1)
                for b in range(NB):
                    for m in range(2):
                        a.wait_ge(og_ready, 2 * b + m + 1)
                        a.activation(sq[:, m, :], og[:, m, :], ACT.Square).then_inc(sq_ready, 1)
                    for m in range(2):
                        a.wait_ge(pe_ss, 2 * b + m + 1)
                        a.activation(rms[:, m, :], ps[:, value_bank(0, b, m), :], ACT.Sqrt, bias=epsc[:, 0:1], scale=1.0 / HD).then_inc(rms_ready, 1)

            def gate(b):
                a.wait_ge(pe_gate, b + 1)
                a.activation(sgate[:, b, :, :], ps[:, 5:7, :], ACT.Sigmoid).then_inc(gate_ready, 1)

            def attention1():
                transposed_tokens(NB, 0)
                for b in range(NB):
                    if b + 1 < NB:
                        transposed_tokens(NB + b + 1, b + 1)
                    if b == 0:
                        a.wait_ge(pad_ready, 3)
                    a.wait_ge(pe_v, NB + b + 1)
                    for st in range(2):
                        a.activation(vpad[:, 2 * b + st, :, 0:HD], ps[:, 6, 256 * st:256 * st + 256].rearrange("p (h e) -> p h e", h=HEADS),
                                     ACT.Copy).then_inc(v_ready, 1)
                for u in range(HALVES + 2):
                    for j in range(SLOTS):
                        if u < HALVES:
                            probabilities(u, j)
                        if j == 0 and u >= 3 and u % 2:
                            for m in range(2):
                                a.wait_ge(pe_o, HALVES + u - 1)
                                a.activation(og[:, m, :], ps[:, value_bank(1, 0, m), :], ACT.Copy).then_inc(og_ready, 1)
                        if j in (1, 3) and 1 <= u <= HALVES:
                            n = 2 * (u - 1) + j // 2
                            a.wait_ge(pe_tb, n + 1)
                            g = 2 * (j // 2)
                            a.activation(P1[:, (u - 1) % 2, g:g + 2, :, :].rearrange("p g e q -> p (g e q)"), ps[:, 7, :], ACT.Copy).then_inc(tb_copied, 1)

            def probabilities(u, j):
                n = SLOTS * u + j
                bank = ps[:, score_bank(1, n), :]
                a.wait_ge(max_done, n + 1)
                if j < 2:
                    heads = [(Q0[:, u % 2, 2 * m + j, e, :], bank[:, 256 * m + 128 * e:256 * m + 128 * e + 128], nm[:, u % 2, 0, 2 * m + j, e:e + 1])
                             for m in range(2) for e in range(2)]
                else:
                    heads = [(Q1[:, u % 2, j - 2, e, :], bank[:, 256 * e:256 * e + 256], nm[:, u % 2, 1, j - 2, e:e + 1]) for e in range(2)]
                for dst, src, neg_max in heads:
                    last = a.activation(dst, src, ACT.Exp, bias=neg_max)
                last.then_inc(p_done, 1)

            def split_hi(l, c, slot, turn):
                a.wait_ge(raw_in[l][slot], 16 * (turn + 1))
                a.activation(whi[:, slot, :], raw[:, slot, :], ACT.Copy).then_inc(w_hi[l], 1)

            def experts(l):
                for kk in range(KD):
                    for hf in range(2):
                        n = 2 * kk + hf
                        a.wait_ge(f_pe_xt, 4 * l + n + 1)
                        a.activation(xTh[:, kk, hf, :], ps[:, n, :], ACT.Copy).then_inc(f_hi, 1)
                a.wait_ge(f_gw, 16 * (l + 1))
                a.activation(gwh[:, :, :], gwr[:, :, :], ACT.Copy).then_inc(f_gwh, 1)
                for c in range(2):
                    split_hi(l, c, c, 0)
                for hf in range(2):
                    a.wait_ge(f_lgT, 2 * l + hf + 1)
                    a.activation(lgT[:, hf, :], ps[0:E, 4 + hf, :], ACT.Copy).then_inc(f_lgTs, 1)
                a.wait_ge(f_d, l + 1)
                a.activation(ex[:, :, :], lgs[:, :, :], ACT.Exp).then_inc(f_ex, 1)
                for hf in range(2):
                    a.wait_ge(f_combT, 2 * l + hf + 1)
                    a.wait_ge(f_ones, 2 * (l + 1))
                    a.activation(CT[0:17, hf, :], ps[0:17, 6 + hf, :], ACT.Copy).then_inc(f_cth, 1)
                for i, last in blocks(a):
                    for u in range(2 * RING):
                        n = i * (2 * RING) + u
                        c = i * RING + u // 2
                        a.wait_ge(s_g[l], n + 1)
                        a.activation(sl[:, u % 2, :], ps[:, 4, :], ACT.Silu).then_inc(s_silu[l], 1)
                        a.wait_ge(s_t3[l], n + 1)
                        a.activation(ahi[:, u % 2, :], h2[:, u % 2, :], ACT.Copy).then_inc(s_ahi[l], 1)
                        if u % 2 == 0 and not (last and u // 2 + 2 >= RING):
                            split_hi(l, c + 2, (u // 2 + 2) % RING, i + (u // 2 + 2) // RING)
                for mt in range(2):
                    for hf in range(2):
                        a.wait_ge(s_y[l], 2 * CHUNKS + 1)
                        a.activation(yS[:, mt, hf, :], ps[:, 2 * mt + hf, :], ACT.Copy).then_inc(f_ys, 1)

            def cross():
                for hg in range(GROUPS):
                    for jj in range(4):
                        a.wait_ge(x_pea, 4 * hg + jj + 1)
                        a.activation(Aw[:, hg, :, :, LO * jj:LO * jj + LO], ps[:, jj, 0:2 * XQ].rearrange("p (k h f) -> p k h f", k=KD, h=2),
                                     ACT.Copy).then_inc(x_a, 1)
                    a.wait_ge(x_pem, hg + 1)
                    a.activation(MM[:, hg, :, :].rearrange("p e n -> p (e n)"), ps[:, 6, :], ACT.Copy).then_inc(x_mm, 1)
                    a.wait_ge(pe_xt, 8 + hg + 1)
                    a.activation(xT4[:, :, hg, :], ps[:, 7, :].rearrange("p (k s) -> p k s", k=KD), ACT.Copy).then_inc(xt_ready, 1)
                for w in range(UNITS):
                    a.wait_ge(x_t, w + 1)
                    a.activation(tS[:, :, :].rearrange("p e s -> p (e s)"), ps[:, 2, :], ACT.Copy).then_inc(x_ts, 1)
                    for n in range(4):
                        a.wait_ge(x_s, 4 * w + n + 1)
                        a.activation(Px[:, n // 2, n % 2, :], ps[:, 3 + n % 2, :], ACT.Exp).then_inc(x_p, 1)

            norm(0)
            a.wait_ge(const_loaded, 16)
            a.wait_ge(ld_loaded, 16)
            for h in range(HEADS):
                a.activation(DT[:, h, :], k("dist"), ACT.Exp, scale=ld_bc[:, h:h + 1]).then_inc(dt_exp, 1)
            attention0()
            if stages >= 2:
                norm(1)
                a.wait_ge(xb_loaded, 16 * 3)
                for t in range(TILES):
                    a.wait_ge(pe_xb, t + 1)
                    if t >= 2:
                        a.wait_ge(xb_part, t - 1)
                    a.activation(xsig[:, t % 2, :], ps[:, t % 4, 0:SEQ], ACT.Sigmoid, bias=xb_b[:, 0:1]).then_inc(xsig_ready, 1)
            if stages >= 3:
                norm(2)
                experts(0)
            if stages >= 4:
                norm(3)
                attention1()
            if stages >= 5:
                norm(4)
                cross()
            if stages >= 6:
                norm(5)
                experts(1)

        @block.gpsimd
        def _(g):
            g.dma_start(ld_bc[:, :], d["ld"]).then_inc(ld_loaded, 16)
            g.memset(vpad[:, :, :, :], 0.0).then_inc(pad_ready, 1)

            def zero_fill(l):
                g.wait_ge(x_done, 8 * (2 + 3 * l))
                g.memset(CT[:, :, :].bitcast(F32), 0.0).then_inc(f_ones, 1)
                g.memset(zeros[:, :].bitcast(F32), 0.0).then_inc(f_ones, 1)

            if stages >= 3:
                zero_fill(0)
            if stages >= 4:
                g.wait_ge(x_done, 8 * 3)
                g.memset(vpad[:, :, :, :], 0.0).then_inc(pad_ready, 1)
                g.wait_ge(pad_ready, 2)
                g.memset(vpad[:, :, :, HD:HD + 1], 1.0).then_inc(pad_ready, 1)
                for b in range(NB):
                    g.wait_ge(rope_done, 4 * b + 2)
                    g.tensor_tensor(qT[:, b].rearrange("p m s -> p (m s)"), sg[:, 0, :], sg[:, 1, :], ALU.add).then_inc(q_ready, 1)
                    g.wait_ge(rope_done, 4 * b + 4)
                    if b >= 1:
                        g.wait_ge(k_ready, 2 * (NB + b))
                    g.tensor_tensor(kT[:, :, :].rearrange("p m s -> p (m s)"), sg[:, 2, :], sg[:, 3, :], ALU.add).then_inc(k_sum, 1)
                    g.wait_ge(k_sum, b + 1)
                    g.tensor_scalar(kE[:, b], kT[:, :, :], k("even_s"), None, ALU.mult).then_inc(k_ready, 1)
                    g.tensor_scalar(kO[:, b], kT[:, :, :], k("odd_s"), None, ALU.mult).then_inc(k_ready, 1)
            if stages >= 5:
                for w in range(NB * GROUPS):
                    for j in range(3):
                        g.wait_ge(x_r, 6 * w + 2 * j + 2)
                        if w >= 1:
                            g.wait_ge(x_t, w)
                        for part in range(2):
                            g.tensor_tensor(qr[:, j, part, :], r1[:, j, 256 * part:256 * part + 256], r2[:, j, 256 - 256 * part:512 - 256 * part],
                                            ALU.add).then_inc(x_qr, 1)
            if stages >= 6:
                zero_fill(1)

        @block.tensor
        def _(pe):
            def mm(o, l, r, start, stop):
                return pe.matmul(o, l, r, start=start, stop=stop, skip_group_check=True)

            def transposed_tokens(l, b):
                i = NB * l + b
                pe.wait_ge(norm_done, 8 * 3 * l + 2 * b + 2)
                if b >= 1:
                    pe.wait_ge(xt_ready, i)
                for kk in range(KD):
                    for t in range(2):
                        last = pe.transpose(ps[:, 7, 256 * kk + 128 * t:256 * kk + 128 * t + 128], xn[:, 2 * b + t, 128 * kk:128 * kk + 128], ident)
                last.then_inc(pe_xt, 1)

            def features(l, bank, j, b):
                w = (wqkv0, wqkv1)[l]
                for m in range(2):
                    for kk in range(KD):
                        last = mm(ps[:, bank, 256 * m:256 * m + 256], w[:, j, kk, 128 * m:128 * m + 128], xT4[:, kk, b, :], kk == 0, kk == KD - 1)
                return last

            def tokens(l, bank, j, b):
                w = (wqkv0, wqkv1)[l]
                for st in range(2):
                    for kk in range(KD):
                        last = mm(ps[:, bank, 256 * st:256 * st + 256], xT4[:, kk, b, 128 * st:128 * st + 128], w[:, j, kk, :], kk == 0, kk == KD - 1)
                return last

            def gate(b):
                pe.wait_ge(g1_ready, b + 1)
                if b >= 1:
                    pe.wait_ge(gate_ready, b)
                for grp in range(4):
                    last = mm(ps[:, 5 + grp // 2, 256 * (grp % 2):256 * (grp % 2) + 256], wg2[:, grp, :], g1S[:, b, :], True, True)
                last.then_inc(pe_gate, 1)

            def mixed_values(l, u):
                b = u // 2
                for st in range(2):
                    for m in range(2):
                        for e in range(2):
                            for gi in range(2):
                                g = 2 * (u % 2) + gi
                                last = mm(ps[32 * g:32 * g + 32, value_bank(l, b, m), 256 * e + 128 * st:256 * e + 256], vpad[:, 2 * b + st, 8 * m + 2 * g + e, :],
                                          (P0 if st == 0 else P1)[:, u % 2, 2 * m + gi, e, :], st == 0 and e == 0, st == 1)
                last.then_inc(pe_o, 1)

            def output(l, b):
                pe.wait_ge(on_ready, 4 * (NB * l + b) + 4)
                for t in range(2):
                    for grp in range(4):
                        last = mm(ps[:, out_bank(l, b), 256 * t:256 * t + 256], on[:, grp, 128 * t:128 * t + 128], wo_gap[:, l, grp, :], grp == 0, grp == 3)
                last.then_inc(pe_out, 1)

            def scores_by_key(u, j):
                n, b = SLOTS * u + j, u // 2
                if n >= TURN[0]:
                    pe.wait_ge(p_done, n - TURN[0] + 1)
                bank = ps[:, score_bank(0, n), :]
                g = 2 * (u % 2) + j % 2
                r = slice(32 * g, 32 * g + 32)
                for m in ((j // 2,) if j < 4 else (0, 1)):
                    for e, kk in enumerate((kE, kO)):
                        if j < 4:
                            last = mm(bank[:, 256 * e:256 * e + 256], kk[r, b, m, 0:128], qT[r, b, m, :], True, True)
                        else:
                            c = 256 * m + 128 * e
                            last = mm(bank[:, c:c + 128], kk[r, b, m, 128:256], qT[r, b, m, 128:256], True, True)
                last.then_inc(pe_s, 1)

            def scores_by_query(u, j):
                n, b = SLOTS * u + j, u // 2
                if n >= TURN[1]:
                    pe.wait_ge(p_done, SLOTS * HALVES + n - TURN[1] + 1)
                bank = ps[:, score_bank(1, n), :]
                if j < 2:
                    mm(bank.rearrange("p (e s) -> p e s", e=4), identb[:, :], negqs[:, :].unsqueeze(1).to_broadcast([P, 4, 128]), True, False)
                else:
                    mm(bank.rearrange("p (e s) -> p e s", e=2)[:, :, 128:256], identb[:, :], negqs[:, :].unsqueeze(1).to_broadcast([P, 2, 128]), True, False)
                g = 2 * (u % 2) + j % 2
                r = slice(32 * g, 32 * g + 32)
                for m in ((0, 1) if j < 2 else (j // 2 - 1,)):
                    for e, kk in enumerate((kE, kO)):
                        if j < 2:
                            c = 256 * m + 128 * e
                            last = mm(bank[:, c:c + 128], qT[r, b, m, 0:128], kk[r, b, m, 0:128], False, True)
                        else:
                            last = mm(bank[:, 256 * e:256 * e + 256], qT[r, b, m, 128:256], kk[r, b, m, :], False, True)
                last.then_inc(pe_s, 1)

            def transpose_a(u, g):
                n, par = 4 * u + g, u % 2
                pe.wait_ge(p_done, SLOTS * (HALVES + u) + 3 + g)
                if n >= 2:
                    pe.wait_ge(ta_copied, n - 1)
                for e in range(2):
                    pe.transpose(ps[:, 2 + n % 2, 256 * e:256 * e + 128], Q0[:, par, g, e, :], ident)
                    last = pe.transpose(ps[:, 2 + n % 2, 256 * e + 128:256 * e + 256], Q1[:, par, g, e, 0:128], ident)
                last.then_inc(pe_ta, 1)

            def transpose_b(u, half):
                n, par = 2 * u + half, u % 2
                if n >= 1:
                    pe.wait_ge(tb_copied, n)
                if half == 0 and u >= 3 and u % 2:
                    pe.wait_ge(x_done, 8 * 3 + 2 * ((u - 3) // 2) + 2)
                for c in range(4):
                    last = pe.transpose(ps[:, 7, 128 * c:128 * c + 128], Q1[:, par, 2 * half + c // 2, c % 2, 128:256], ident)
                last.then_inc(pe_tb, 1)

            def attention0():
                pe.wait_ge(const_loaded, 16)
                transposed_tokens(0, 0)
                pe.wait_ge(w0_loaded, 16 * 5)
                for b in range(NB):
                    if b + 1 < NB:
                        transposed_tokens(0, b + 1)
                    pe.wait_ge(xt_ready, b + 1)
                    if b >= 1:
                        pe.wait_ge(q_ready, b)
                    features(0, 0, 0, b).then_inc(pe_q, 1)
                    if b >= 1:
                        gate(b - 1)
                        pe.wait_ge(k_ready, 2 * b)
                    features(0, 1, 1, b).then_inc(pe_k, 1)
                    if b >= 1:
                        pe.wait_ge(v_ready, 2 * b)
                    tokens(0, 2, 2, b).then_inc(pe_v, 1)
                    for kk in range(KD):
                        last = mm(ps[0:HD, 3, 0:SEQ], wg1[:, kk, :], xT4[:, kk, b, :], kk == 0, kk == KD - 1)
                    last.then_inc(pe_g1, 1)
                gate(NB - 1)
                for u in range(HALVES + 2):
                    for j in range(SLOTS):
                        if u < HALVES:
                            if j == 0 and u % 2 == 0:
                                pe.wait_ge(q_ready, u // 2 + 1)
                                pe.wait_ge(k_ready, 2 * (u // 2) + 2)
                            if u == 0 and j == 1:
                                pe.wait_ge(gate_ready, NB)
                            scores_by_key(u, j)
                        if j == 1 and 1 <= u <= HALVES:
                            w = u - 1
                            pe.wait_ge(v_ready, 2 * (w // 2) + 2)
                            if w == 0:
                                pe.wait_ge(k_ready, 2 * NB)
                            if w == 4:
                                pe.wait_ge(x_done, 2)
                            if w == 6:
                                pe.wait_ge(x_done, 4)
                            pe.wait_ge(p_done, SLOTS * w + 6)
                            mixed_values(0, w)
                        b = u // 2 - 1
                        if b >= 0 and (u % 2, j) == (0, 4):
                            for m in range(2):
                                pe.wait_ge(sq_ready, 2 * b + m + 1)
                                mm(ps[:, value_bank(0, b, m), :], k("block_ones"), sq[:, m, :], True, True).then_inc(pe_ss, 1)
                        if b >= 0 and (u % 2, j) == (1, 4):
                            output(0, b)

            def attention1():
                pe.wait_ge(w1_loaded, 16)
                transposed_tokens(1, 0)
                for b in range(NB):
                    if b + 1 < NB:
                        transposed_tokens(1, b + 1)
                    pe.wait_ge(xt_ready, NB + b + 1)
                    if b == 0:
                        pe.wait_ge(x_done, 8 * 3)
                    else:
                        pe.wait_ge(v_ready, 2 * (NB + b))
                    tokens(1, 6, 4, b).then_inc(pe_v, 1)
                    for j in range(4):
                        if b >= 1:
                            pe.wait_ge(rope_done, 4 * (b - 1) + j + 1)
                        features(1, j, j, b).then_inc(pe_f, 1)
                pe.wait_ge(setup_v, 2)
                for u in range(HALVES + 3):
                    for j in range(SLOTS):
                        if u < HALVES:
                            if j == 0 and u % 2 == 0:
                                pe.wait_ge(q_ready, NB + u // 2 + 1)
                                pe.wait_ge(k_ready, 2 * (NB + u // 2) + 2)
                            if u == 0 and j == 2:
                                pe.wait_ge(v_ready, 4 * NB)
                            scores_by_query(u, j)
                        if j < 4 and 1 <= u <= HALVES:
                            if u == 1 and j == 0:
                                pe.wait_ge(rope_done, 4 * NB)
                            transpose_a(u - 1, j)
                            if j % 2:
                                transpose_b(u - 1, j // 2)
                        b = (u - 3) // 2
                        if u >= 3 and u % 2 and j == 1:
                            for m in range(2):
                                pe.wait_ge(og_ready, HALVES + 2 * b + m + 1)
                                mm(ps[:, value_bank(1, b, m), :], k("pick16"), og[:, m, :], True, True).then_inc(pe_ss, 1)
                        if u >= 3 and u % 2 and j == 5:
                            pe.wait_ge(tb_copied, min(2 * u, 2 * HALVES))
                            output(1, b)
                        if j == 5 and 1 <= u <= HALVES:
                            w = u - 1
                            pe.wait_ge(ta_copied, 4 * w + 4)
                            pe.wait_ge(tb_copied, 2 * w + 2)
                            if w >= 2 and w % 2 == 0:
                                pe.wait_ge(rec_ready, HALVES + w)
                            mixed_values(1, w)

            def experts(l):
                stage = 2 + 3 * l
                for kk in range(KD):
                    for hf in range(2):
                        for t in range(4):
                            pe.wait_ge(norm_done, 8 * stage + 4 * hf + t + 1)
                            last = pe.transpose(ps[:, 2 * kk + hf, 128 * t:128 * t + 128], xn[:, 4 * hf + t, 128 * kk:128 * kk + 128], ident)
                        last.then_inc(f_pe_xt, 1)
                pe.wait_ge(f_lo, 4 * (l + 1))
                pe.wait_ge(f_gwl, l + 1)
                for hf in range(2):
                    pairs = ((gwh, xTh), (gwl, xTh), (gwh, xTl))
                    for j, (w, x) in enumerate(pairs):
                        for kk in range(KD):
                            last = mm(ps[0:E, 4 + hf, :], w[:, kk, :], x[:, kk, hf, :], j + kk == 0, j == 2 and kk == 1)
                    last.then_inc(f_lgT, 1)
                pe.wait_ge(f_lgTs, 2 * (l + 1))
                for t in range(TILES):
                    last = pe.transpose(ps[:, 6, E * t:E * t + E], lgT[:, t // 4, 128 * (t % 4):128 * (t % 4) + 128], ident[0:E, 0:E])
                last.then_inc(f_lg, 1)
                pe.wait_ge(f_ones, 2 * (l + 1))
                for bank in range(4):
                    last = mm(ps[:, bank, :], zeros[:, 0:128], zeros[:, :], True, False)
                last.then_inc(s_y[l], 1)

                def gate_up(n, u):
                    slot, hf = u // 2 % RING, u % 2
                    pe.wait_ge(w_lo[l], nchunk(n, u) + 1)
                    pe.wait_ge(s_silu[l], n)
                    three(4, whi, wlo, slot, 0, hf).then_inc(s_g[l], 1)
                    pe.wait_ge(s_t2[l], n)
                    three(5, whi, wlo, slot, 256, hf).then_inc(s_u[l], 1)

                def three(bank, hi, lo, slot, col, hf):
                    first = True
                    for w, x in ((hi, xTh), (lo, xTh), (hi, xTl)):
                        for kk in range(KD):
                            last = mm(ps[:, bank, :], w[:, slot, col + 128 * kk:col + 128 * kk + 128], x[:, kk, hf, :], first, False)
                            first = False
                    return last

                def weights_of_experts(n, u):
                    pe.wait_ge(s_t3[l], n)
                    mm(ps[:, 6, :], whi[0:64, u // 2 % RING, PACK - 128:PACK], CT[:, u % 2, :], True, True).then_inc(s_c[l], 1)

                def down(n, u):
                    slot, hf = u // 2 % RING, u % 2
                    pe.wait_ge(s_alo[l], n + 1)
                    for mt in range(2):
                        for w, x in ((whi, ahi), (wlo, ahi), (whi, alo)):
                            last = mm(ps[:, 2 * mt + hf, :], w[:, slot, 512 + 128 * mt:640 + 128 * mt], x[:, u % 2, :], False, False)
                    last.then_inc(s_y[l], 1)

                def nchunk(n, u):
                    return cur[0] * RING + u // 2

                cur = [0]
                gate_up(0, 0)
                for t in range(TILES):
                    if t == 0:
                        pe.wait_ge(f_v, 24 if l == 0 else 24 + 28)
                    last = pe.transpose(ps[0:17, 6 + t // 4, 128 * (t % 4):128 * (t % 4) + 128], comb[:, t, :], ident)
                    if t % 4 == 3:
                        last.then_inc(f_combT, 1)
                pe.wait_ge(f_ctl, 2 * (l + 1))
                weights_of_experts(0, 0)
                for i, last in blocks(pe):
                    cur[0] = i
                    for u in range(2 * RING):
                        n = i * (2 * RING) + u
                        if not (last and u == 2 * RING - 1):
                            gate_up(n + 1, u + 1)
                            weights_of_experts(n + 1, u + 1)
                        down(n, u)
                pe.wait_ge(f_ys, 4 * (l + 1))
                for t in range(TILES):
                    for mt in range(2):
                        last = pe.transpose(ps[:, 4 + t // 2, 256 * (t % 2) + 128 * mt:256 * (t % 2) + 128 * mt + 128],
                                            yS[:, mt, t // 4, 128 * (t % 4):128 * (t % 4) + 128], ident)
                    if t % 2:
                        last.then_inc(f_yt, 1)

            def cross():
                def part_of(slot, name, rows=P):
                    a, b = XP[name]
                    return wx[0:rows, slot, a:b]

                pe.wait_ge(x_done, 8 * 4)
                pe.wait_ge(x_kv, 1)
                for t in range(TILES):
                    last = pe.transpose(ps[:, 7, XC * t:XC * t + XC], kvT[0:XC, t // 2, 128 * (t % 2):128 * (t % 2) + 128], ident[0:XC, 0:XC])
                last.then_inc(x_pekv, 1)
                for hg in range(GROUPS):
                    slot = hg % 2
                    pe.wait_ge(wx_in[slot], 16 * (hg // 2 + 1))
                    wq = part_of(slot, "wq").rearrange("p (h d) -> p h d", h=4)
                    kcq = part_of(slot, "kcq").rearrange("p (h q) -> p h q", h=4)
                    qrT = part_of(slot, "qrT", XR).rearrange("p (h f) -> p h f", h=2)
                    krT = part_of(slot, "krT", XR)
                    kckv = part_of(slot, "kckv").rearrange("p (h c) -> p h c", h=4)
                    woT = part_of(slot, "woT").rearrange("p (h n) -> p h n", h=4)
                    for jj in range(4):
                        if hg >= 1:
                            pe.wait_ge(x_a, 4 * (hg - 1) + jj + 1)
                        for kk in range(KD):
                            last = mm(ps[:, jj, XQ * kk:XQ * kk + XQ], wq[:, jj, 128 * kk:128 * kk + 128], kcq[:, jj, :], True, True)
                        last.then_inc(x_pea, 1)
                    for part in range(2):
                        if hg >= 1:
                            pe.wait_ge(x_g, 12 * (hg - 1) + 6 * part + 6)
                        for j in range(3):
                            last = mm(ps[:, 4 + part, 128 * j:128 * j + 128], qrT[:, part, 128 * j:128 * j + 128], krT[:, XC * j:XC * j + 2 * XC], True, True)
                        last.then_inc(x_peg, 1)
                    if hg >= 1:
                        pe.wait_ge(x_mm, hg)
                    for jj in range(4):
                        last = mm(ps[64 * (jj % 2):64 * (jj % 2) + 64, 6, 256 * (jj // 2):256 * (jj // 2) + 256], kckv[:, jj, :], woT[:, jj, :], True, True)
                    last.then_inc(x_pem, 1)
                    b = hg
                    if b == 0:
                        pe.wait_ge(x_kvt, 2)
                    else:
                        pe.wait_ge(xt_ready, 8 + b)
                    pe.wait_ge(norm_done, 8 * 4 + 2 * b + 2)
                    for kk in range(KD):
                        for t in range(2):
                            last = pe.transpose(ps[:, 7, 256 * kk + 128 * t:256 * kk + 128 * t + 128], xn[:, 2 * b + t, 128 * kk:128 * kk + 128], ident)
                    last.then_inc(pe_xt, 1)
                pe.wait_ge(x_a, 4 * GROUPS)
                pe.wait_ge(x_mm, GROUPS)
                pe.wait_ge(x_g, 12 * GROUPS)
                pe.wait_ge(xt_ready, 8 + NB)

                def latent_queries(w, j):
                    b, hg, n = w // GROUPS, w % GROUPS, 3 * w + j
                    if n >= 2:
                        pe.wait_ge(x_r, 2 * (n - 2) + 2)
                    for part in range(2):
                        for kk in range(KD):
                            last = mm(ps[:, n % 2, 256 * part:256 * part + 256], Aw[:, hg, kk, part, 128 * j:128 * j + 128], xT4[:, kk, b, :], kk == 0, kk == 1)
                    last.then_inc(x_q, 1)

                def query_side(w):
                    pe.wait_ge(x_qr, 6 * w + 6)
                    if w >= 1:
                        pe.wait_ge(x_bd, w)
                    for pair in range(2):
                        n = 0
                        for piece in (2 * pair, 2 * pair + 1):
                            j = pair + piece % 2
                            for part in range(2):
                                last = mm(ps[:, 2, 256 * pair:256 * pair + 256], Gm[:, w % GROUPS, part, piece, :], qr[:, j, part, :], n == 0, n == 3)
                                n += 1
                    last.then_inc(x_t, 1)

                def max_scores(w, n):
                    st, ab = n // 2, n % 2
                    r = slice(64 * ab, 64 * ab + 64)
                    if n == 0:
                        pe.wait_ge(x_ts, w + 1)
                    if n >= 2:
                        pe.wait_ge(x_max, 4 * w + n - 1)
                    elif w >= 1:
                        pe.wait_ge(x_p, 4 * w + n - 1)
                    for pair in range(2):
                        last = mm(ps[:, 3 + ab, 256 * pair:256 * pair + 256], tS[r, pair, 128 * st:128 * st + 128], kvT[r, w // GROUPS, :], True, True)
                    last.then_inc(x_m, 1)

                def transposed_maxima(w):
                    pe.wait_ge(x_max, 4 * w + 4)
                    for st in range(2):
                        last = pe.transpose(ps[:, 2, 128 * st:128 * st + 128], nmq[:, st, :, :].rearrange("p a n -> p (a n)"), ident)
                    last.then_inc(x_nmt, 1)

                def scores(w):
                    pe.wait_ge(x_bd, w + 1)
                    for n in range(4):
                        lt, ab = n // 2, n % 2
                        r = slice(64 * ab, 64 * ab + 64)
                        if n >= 2:
                            pe.wait_ge(x_p, 4 * w + n - 1)
                        mm(ps[:, 3 + ab, :], kvT[r, w // GROUPS, 128 * lt:128 * lt + 128], tS[r, :, :].rearrange("p e s -> p (e s)"), True, False)
                        mm(ps[:, 3 + ab, :], onesx[r, :], BDx[r, :, :].rearrange("p e s -> p (e s)"), False, True).then_inc(x_s, 1)

                def weighted_contexts(w):
                    for ab in range(2):
                        for lt in range(2):
                            pe.wait_ge(x_p, 4 * w + 2 * lt + ab + 1)
                            last = mm(ps[:, 5 + ab, :], kvaug[:, 2 * (w // GROUPS) + lt, ab, :], Px[:, lt, ab, :], lt == 0, lt == 1)
                        last.then_inc(x_c, 1)

                def output(w):
                    b, hg = w // GROUPS, w % GROUPS
                    pe.wait_ge(x_ctx, 2 * w + 2)
                    if hg == 0:
                        pe.wait_ge(x_done, 8 * 4 + 2 * b)
                    for t in range(2):
                        for pair in range(2):
                            last = mm(ps[:, 7, 256 * t:256 * t + 256], ctxS[:, pair, 128 * t:128 * t + 128], MM[:, hg, pair, :],
                                      hg + t + pair == 0, hg == 3 and pair == 1)
                    last.then_inc(x_o, 1)

                for j in range(3):
                    latent_queries(0, j)
                for w in range(UNITS):
                    more = w + 1 < UNITS
                    query_side(w)
                    if more:
                        latent_queries(w + 1, 0)
                    max_scores(w, 0)
                    max_scores(w, 1)
                    if more:
                        latent_queries(w + 1, 1)
                    max_scores(w, 2)
                    max_scores(w, 3)
                    if more:
                        latent_queries(w + 1, 2)
                    transposed_maxima(w)
                    if w >= 1:
                        output(w - 1)
                    scores(w)
                    weighted_contexts(w)
                output(UNITS - 1)

            attention0()
            if stages >= 2:
                pe.wait_ge(xb_loaded, 16 * 3)
                for t in range(TILES):
                    b = t // 2
                    if t >= 4:
                        pe.wait_ge(xsig_ready, t - 3)
                    else:
                        pe.wait_ge(x_done, 8)
                    mm(ps[:, t % 4, 0:SEQ], xb_l[:, b, 128 * (t % 2):128 * (t % 2) + 128], xb_r[:, b, :], True, True).then_inc(pe_xb, 1)
            if stages >= 3:
                experts(0)
            if stages >= 4:
                attention1()
            if stages >= 5:
                cross()
            if stages >= 6:
                experts(1)


def constants():
    c = np.zeros((P, CONST_W), np.float32)
    p = np.arange(P)

    def put(name, a):
        lo, hi = CONST[name]
        c[:, lo:hi] = np.asarray(a, np.float32).reshape(P, hi - lo)

    put("ident", np.eye(P))
    q = np.arange(SEQ)
    put("dist", np.maximum(q[None] - p[:, None], 0))
    put("causal", q[None] >= p[:, None])
    put("neg_qs", np.where(p[None] > p[:, None], NEG, 0.0))
    put("even", (p // HD) % 2 == 0)
    put("odd", (p // HD) % 2 == 1)
    scale = 1.0 / HD ** 0.5
    put("even_s", ((p // HD) % 2 == 0) * scale)
    put("odd_s", ((p // HD) % 2 == 1) * scale)
    same = (p[:, None] // 32) == (p[None] // 32)
    put("block_ones", same & (p[:, None] % 32 < HD))
    put("pick16", same & (p[:, None] % 32 == HD))
    put("ones", np.ones((P, 128)))
    dd = p % HD
    inv = np.float32(10000.0) ** (-(np.arange(0, HD, 2, dtype=np.float32) / np.float32(HD)))
    ang = (q.astype(np.float32)[None] * inv[dd // 2][:, None]).astype(np.float32)
    put("cos", np.cos(ang))
    put("sin", np.where(dd[:, None] % 2 == 0, -1.0, 1.0) * np.sin(ang))
    return c


def cross_constants():
    c = np.zeros((P, CX_W), np.float32)
    p = np.arange(P)
    pos = np.arange(SEQ, dtype=np.float32)

    def put(name, a):
        lo, hi = CX[name]
        c[:, lo:hi] = np.asarray(a, np.float32).reshape(P, hi - lo)

    def angles(dim, feature):
        inv = np.float32(1.0) / np.float32(10000.0) ** (np.arange(0, dim, 2, dtype=np.float32) / np.float32(dim))
        return (pos * inv[feature // 2][..., None]).astype(np.float32)

    f = (np.arange(3)[None] * P + p[:, None]) % LO
    lo, hi = angles(XQ, f), angles(XQ, f + LO)
    put("cosq", np.stack([np.cos(lo), np.cos(hi)], axis=2))
    put("sinq", np.stack([np.sin(hi), -np.sin(lo)], axis=2))
    g = angles(XC, p % XC)
    put("coskv", np.cos(g))
    put("sinkv", np.where((p % XC < XC // 2)[:, None], -1.0, 1.0) * np.sin(g))
    head = (np.arange(3)[None] * P + p[:, None]) // LO
    put("gmask", head[:, :, None] == np.arange(3)[None, :, None] + np.arange(2)[None, None, :])
    put("slot2", (p % 64)[:, None] == np.arange(2)[None])
    return c


def cross_pack(i):
    o = np.zeros((GROUPS, P, XPACK), np.float32)

    def put(name, a):
        lo, hi = XP[name]
        o[:, 0:a.shape[1], lo:hi] = a.reshape(GROUPS, a.shape[1], hi - lo)

    def by_group(a, *axes):
        return a.reshape((GROUPS, 4) + a.shape[1:]).transpose(axes)

    put("wq", by_group(i["L1_xattn_Wq"].reshape(XH, XK, D), 0, 2, 1, 3))
    put("kcq", by_group(i["L1_xattn_w_kc_q"], 0, 2, 1, 3))
    put("qrT", by_group(i["L1_xattn_W_qr"].reshape(XH, 2, LO, XR), 0, 4, 2, 1, 3))
    put("krT", by_group(i["L1_xattn_W_kr"], 0, 3, 1, 2))
    put("kckv", by_group(i["L1_xattn_w_kc_kv"], 0, 2, 1, 3))
    put("woT", by_group(i["L1_xattn_Wo"].T.reshape(XH, XK, D), 0, 2, 1, 3))
    return o


def rows_to_lhs(w):
    return w.reshape(KD, P, -1).transpose(1, 0, 2)


def gap_rows(w):
    n = w.shape[1]
    o = np.zeros((4, 32, 4, n), w.dtype)
    w = w.reshape(2, 4, 2, HD, n)
    for m in range(2):
        for e in range(2):
            o[:, 0:HD, 2 * m + e] = w[m, :, e]
    return o.reshape(P, 4, n)


def expert_pack(w13, w2, s13, s2):
    total = CHUNKS * P
    flat = E * INNER

    def rows(experts, shared):
        o = np.zeros((total, D), np.float32)
        o[:flat] = experts.reshape(flat, D)
        o[flat:flat + SHARED] = shared
        return o

    g = rows(w13[:, :INNER], s13[:SHARED]).reshape(CHUNKS, P, KD, P)
    u = rows(w13[:, INNER:], s13[SHARED:]).reshape(CHUNKS, P, KD, P)
    dn = rows(w2.transpose(0, 2, 1), s2.T).reshape(CHUNKS, P, D)
    sel = np.zeros((total, P), np.float32)
    r = np.arange(total)
    e = np.where(r < flat, r // INNER, E)
    sel[r, e] = 1
    sel[r, 32 + e] = 1
    sel = sel.reshape(CHUNKS, P, P).transpose(0, 2, 1)
    g = g.transpose(0, 3, 2, 1).reshape(CHUNKS, P, 2 * P)
    u = u.transpose(0, 3, 2, 1).reshape(CHUNKS, P, 2 * P)
    return np.concatenate([g, u, dn, sel], axis=2)


def lay_out(i):
    i = {k: np.asarray(v) for k, v in i.items()}
    ctxT = i["ctx_512"].transpose(2, 0, 1)
    xw = i["L0_xattn_W"][0]
    half = (64, NB, SEQ)
    swap = np.arange(D) ^ 1
    turn = np.arange(XC) ^ (XC // 2)
    wq, wk, wv = (i[f"L1_attn_w{c}"] for c in "qkv")
    return {
        "x": i["x"],
        "const": constants(),
        "ld": np.broadcast_to(i["L0_attn_log_decay"], (P, HEADS)),
        "wqkv0": np.stack([rows_to_lhs(i[f"L0_attn_W{c}"]) for c in "qkv"], axis=1),
        "wg1": rows_to_lhs(i["L0_attn_Wg1"]),
        "wg2": gap_rows(i["L0_attn_Wg2"].T).transpose(2, 1, 0),
        "wo_gap": np.stack([gap_rows(i["L0_attn_Wo"]), gap_rows(i["L1_attn_wo"].T)], axis=1),
        "normw": gap_rows(i["L0_attn_norm_w"].reshape(D, 1))[:, :, 0],
        "xb_l": np.concatenate([ctxT, np.broadcast_to(xw[64:, None, None], half)]),
        "xb_r": np.concatenate([np.broadcast_to(xw[:64, None, None], half), ctxT]),
        "xb_b": np.broadcast_to(i["L0_xattn_b"].reshape(1, 1), (P, 1)),
        "wqkv1": np.stack([rows_to_lhs(w.T) for w in (wq, wq[swap], wk, wk[swap], wv)], axis=1),
        "gate0": rows_to_lhs(i["L0_ffn_gate_w"].T),
        "gate1": rows_to_lhs(i["L1_ffn_gate_w"].T),
        "wx": cross_pack(i),
        "cx": cross_constants(),
        "kvc": np.stack([np.concatenate([ctxT, ctxT]), np.concatenate([ctxT[turn], ctxT[turn]])], axis=1),
        "ffn0": expert_pack(i["L0_ffn_w1"], i["L0_ffn_w2"], i["L0_ffn_shared_w1"], i["L0_ffn_shared_w2"]),
        "ffn1": expert_pack(i["L1_ffn_w13"], i["L1_ffn_w2"], i["L1_ffn_sw13"], i["L1_ffn_sw2"]),
    }


def kernel(**inputs):
    import numpy as _np
    import concourse.bacc as _bacc
    from concourse import mybir as _mybir
    from concourse.bass_utils import run_bass_kernel_spmd as _run

    nc = _bacc.Bacc("TRN2", target_bir_lowering=False, num_devices=1)
    arrays, aps = {}, {}
    for name, a in lay_out(inputs).items():
        a = _np.ascontiguousarray(a)
        arrays[f"in_{name}"] = a
        aps[name] = nc.dram_tensor(f"in_{name}", a.shape, _mybir.dt.from_np(a.dtype), kind="ExternalInput").ap()
    out = nc.dram_tensor("out", (NB, SEQ, D), F32, kind="ExternalOutput").ap()
    build(nc, aps, out, STAGES)
    r = _run(nc, [arrays], core_ids=[0])
    return r.results[0]["out"]
```

```python
from contextlib import ExitStack

import numpy as np

import concourse.bass as bass
from concourse import mybir

F32 = mybir.dt.float32
F32R = mybir.dt.float32r
BF16 = mybir.dt.bfloat16
ALU = mybir.AluOpType
ACT = mybir.ActivationFunctionType
AX = mybir.AxisListType.X

P = 128
D = 256
NB, SEQ = 4, 256
TILES = NB * SEQ // P
KD = D // P
HEADS, HD = 16, 16
EPS = 1e-5
NEG = -1e30
HALF = 512

E, TOP_K, INNER, SHARED = 16, 6, 176, 352
CHUNKS = -(-(E * INNER + SHARED) // P)
SHARED_CHUNKS = SHARED // P
PACK = 4 * 128 + 256 + 128
RING = 5

XH, XK, XQ, XR, XC = 16, 128, 192, 64, 64
GROUPS = XH // 4
LO = XQ // 2

def pack_layout():
    at, n = {}, 0
    for name, width in (("wq", 4 * D), ("kcq", 4 * XQ), ("qrT", 2 * 4 * LO), ("krT", 4 * XC), ("kckv", 4 * XC), ("woT", 4 * D)):
        at[name] = (n, n + width)
        n += width
    return at, n


XP, XPACK = pack_layout()


def cx_layout():
    at, n = {}, 0
    for name, width in (("cosq", 3 * 2 * SEQ), ("sinq", 3 * 2 * SEQ), ("coskv", SEQ), ("sinkv", SEQ)):
        at[name] = (n, n + width)
        n += width
    return at, n


CX, CX_W = cx_layout()

def const_layout():
    at, n = {}, 0
    for name, width in (("ident", 128), ("dist", SEQ), ("causal", SEQ), ("neg_qs", 128),
                        ("gmask", 6), ("even", 1), ("odd", 1), ("even_s", 1), ("odd_s", 1), ("block_ones", 128),
                        ("cos", SEQ), ("sin", SEQ)):
        at[name] = (n, n + width)
        n += width
    return at, n


CONST, CONST_W = const_layout()


def build(nc, d, out):
    with ExitStack() as ctx:
        def sb(name, shape, dt=F32, c=ctx):
            return c.enter_context(nc.sbuf_tensor(name, shape, dt))

        def sem(name):
            return ctx.enter_context(nc.semaphore(name))

        ps = ctx.enter_context(nc.psum_tensor("ps", [P, 8, 512], F32))

        X = sb("X", [P, TILES, D])
        xn = sb("xn", [P, TILES, D])
        cst = sb("cst", [P, CONST_W])
        stats = sb("stats", [P, TILES, 6])
        mv = sb("mv", [P, TILES, 2])
        sd = sb("sd", [P, TILES])
        rstd = sb("rstd", [P, TILES])
        epsc = sb("epsc", [P, 1])
        identb = sb("identb", [P, 128], BF16)
        negqs = sb("negqs", [P, 128], BF16)

        def k(name):
            a, b = CONST[name]
            return cst[:, a:b]

        ident = k("ident")

        a_ctx = ctx.enter_context(ExitStack())
        wqkv0 = sb("wqkv0", [P, 3, KD, D])
        wg1 = sb("wg1", [P, KD, HD])
        wg2 = sb("wg2", [HD, 4, 128])
        wo_gap = sb("wo_gap", [P, 2, 4, D])
        normw = sb("normw", [P, 4])
        ld_bc = sb("ld_bc", [P, HEADS])
        xT4 = sb("xT4", [P, KD, NB, SEQ])
        xb_b = sb("xb_b", [P, 1])
        kT = sb("kT", [P, 2, SEQ])
        wqkv1 = sb("wqkv1", [P, 5, KD, D])

        phase = ExitStack()
        with phase:
            qT = sb("qT", [P, NB, 2, SEQ], c=phase)
            kE = sb("kE", [P, NB, 2, SEQ], c=phase)
            kO = sb("kO", [P, NB, 2, SEQ], c=phase)
            vpad = sb("vpad", [P, TILES, HEADS, 32], c=phase)
            P0 = sb("P0", [P, 2, 4, 2, 256], c=phase)
            P1 = sb("P1", [P, 2, 4, 2, 128], c=phase)
            sg = sb("sg", [P, 4, 512], c=phase)
            og = sb("og", [P, 2, 512], c=phase)
            on = sb("on", [P, 4, SEQ], c=phase)
            with ExitStack() as layer0:
                DT = sb("DT", [P, HEADS, SEQ], c=layer0)
                g1S = sb("g1S", [HD, NB, SEQ], c=layer0)
                sgate = sb("sgate", [P, NB, 2, 512], c=layer0)
                sq = sb("sq", [P, 2, 512], c=layer0)
                rms = sb("rms", [P, 2, 512], c=layer0)
                xb_l = sb("xb_l", [P, NB, SEQ], c=layer0)
                xb_r = sb("xb_r", [P, NB, SEQ], c=layer0)
                xsig = sb("xsig", [P, TILES, SEQ], c=layer0)
                rrec = sb("rrec", [P, 2, 512], c=layer0)
            with ExitStack() as layer1:
                nm = sb("nm", [P, 2, 2, 4, 2], c=layer1)
                psum_q = sb("psum_q", [P, 2, 32], c=layer1)
                prec_q = sb("prec_q", [P, 32], c=layer1)
                prec_r = sb("prec_r", [P, 32, 32], c=layer1)
                Q0 = sb("Q0", [P, 2, 4, 2, 128], c=layer1)
                Q1 = sb("Q1", [P, 2, 4, 2, 256], c=layer1)
        phase = ExitStack()
        with phase:
            xTh = sb("xTh", [P, KD, 2, HALF], F32R, c=phase)
            xTl = sb("xTl", [P, KD, 2, HALF], F32R, c=phase)
            raw = sb("raw", [P, RING, PACK], c=phase)
            whi = sb("whi", [P, RING, PACK], F32R, c=phase)
            wlo = sb("wlo", [P, RING, PACK - 128], F32R, c=phase)
            silu_g = sb("silu_g", [P, 2, HALF], c=phase)
            gate_times_up = sb("gate_times_up", [P, 2, HALF], c=phase)
            weighted_h = sb("weighted_h", [P, 2, HALF], c=phase)
            h_hi = sb("h_hi", [P, 2, HALF], F32R, c=phase)
            h_lo = sb("h_lo", [P, 2, HALF], F32R, c=phase)
            shares = sb("shares", [64, 2, HALF], F32R, c=phase)
            half_shares = sb("half_shares", [64, HALF], F32R, c=phase)
            router_w = sb("router_w", [P, KD, E], c=phase)
            router_wh = sb("router_wh", [P, KD, E], F32R, c=phase)
            router_wl = sb("router_wl", [P, KD, E], F32R, c=phase)
            logits_t = sb("logits_t", [E, 2, HALF], c=phase)
            nmx = sb("nmx", [P, TILES], c=phase)
            logits_s = sb("logits_s", [P, TILES, E], c=phase)
            exp_logits = sb("exp_logits", [P, TILES, E], c=phase)
            softmax_den = sb("softmax_den", [P, 2, TILES], c=phase)
            prob = sb("prob", [P, TILES, 18], c=phase)
            v8 = sb("v8", [P, TILES, 8], c=phase)
            left = sb("left", [P, TILES, 18], c=phase)
            comb = sb("comb", [P, TILES, 17], c=phase)
            zeros = sb("zeros", [P, HALF], F32R, c=phase)
            y_sb = sb("y_sb", [P, 2, 2, HALF], c=phase)

        phase = ExitStack()
        with phase:
            merged_q = sb("merged_q", [P, GROUPS, KD, 2, 4 * LO], c=phase)
            merged_s = sb("merged_s", [P, GROUPS, 2, 4, 128], c=phase)
            merged_o = sb("merged_o", [P, GROUPS, 2, D], c=phase)
            cx = sb("cx", [P, CX_W], c=phase)
            rope_buf = sb("rope_buf", [P, 2 * 3 * 512], c=phase)
            kvT = sb("kvT", [P, NB, SEQ], c=phase)
            kv_tok_ab = sb("kv_tok_ab", [P, TILES, 2, 128], c=phase)
            r1, r2 = (rope_buf[:, 1536 * n:1536 * n + 1536].rearrange("p (j s) -> p j s", j=3) for n in range(2))
            kvc = rope_buf[:, 0:2 * NB * SEQ].rearrange("p (a b s) -> p a b s", a=2, b=NB)
            latent_rot = sb("latent_rot", [P, 3, 2, SEQ], c=phase)
            tSh = sb("tSh", [P, 2, SEQ], F32R, c=phase)
            neg_max = sb("neg_max", [P, 2, 2, 2], c=phase)
            sums = sb("sums", [P, 2, 2, 2], c=phase)
            rsum = sb("rsum", [P, 2, 2, 2], c=phase)
            rsumr = sb("rsumr", [P, 2, 2, 2, 64], c=phase)
            probs_q = sb("probs_q", [P, 2, 2, 2, SEQ], c=phase)
            probs_t = sb("probs_t", [P, 2, 2, 512], c=phase)
            recips_t = sb("recips_t", [P, 512], c=phase)
            contexts_sb = sb("contexts_sb", [P, 2, SEQ], c=phase)
            with ExitStack() as weights:
                wx = sb("wx", [P, 2, XPACK], c=weights)
            kvh = sb("kvh", [P, NB, 2, SEQ], F32R, c=phase)
            kvl = sb("kvl", [P, NB, 2, SEQ], F32R, c=phase)
            tSl = sb("tSl", [P, 2, SEQ], F32R, c=phase)

        def kx(name):
            a, b = CX[name]
            return cx[:, a:b]

        x_loaded = [sem(f"x_loaded{b}") for b in range(NB)]
        const_loaded = sem("const_loaded")
        w0_loaded, w1_loaded, xb_loaded = map(sem, ("w0_loaded", "w1_loaded", "xb_loaded"))
        x_done, x_part = sem("x_done"), sem("x_part")
        norm_stats, norm_var, norm_sd, norm_rstd, norm_done = map(sem, ("norm_stats", "norm_var", "norm_sd", "norm_rstd", "norm_done"))
        eps_ready = sem("eps_ready")
        setup_v = sem("setup_v")
        dt_exp = sem("dt_exp")
        dt_ready = sem("dt_ready")
        pe_xt, xt_ready, pe_q, pe_k, pe_v, pe_g1, pe_gate, pe_f = map(sem, ("pe_xt", "xt_ready", "pe_q", "pe_k", "pe_v", "pe_g1", "pe_gate", "pe_f"))
        sig_done, g1_ready, gate_ready, q_ready, k_ready, v_ready = map(sem, ("sig_done", "g1_ready", "gate_ready", "q_ready", "k_ready", "v_ready"))
        spread_ready = sem("spread_ready")
        rope_done, k_sum = map(sem, ("rope_done", "k_sum"))
        pe_s, p_done, max_done, pe_ta, ta_copied, pe_tb, tb_copied = map(
            sem, ("pe_s", "p_done", "max_done", "pe_ta", "ta_copied", "pe_tb", "tb_copied"))
        pe_o, og_ready, sq_ready, pe_ss, rms_ready, rec_ready, on_ready, pe_out = map(
            sem, ("pe_o", "og_ready", "sq_ready", "pe_ss", "rms_ready", "rec_ready", "on_ready", "pe_out"))
        pe_xb, xsig_ready, xb_part = map(sem, ("pe_xb", "xsig_ready", "xb_part"))
        out_done = sem("out_done")
        wx_in = [sem(f"wx_in{u}") for u in range(2)]
        cx_in, kvc_in = sem("cx_in"), sem("kvc_in")
        (x_zeroed, kv_products, kv_rotated, pe_kv_tokens, kv_tokens_copied, pe_merged_q, merged_q_copied, pe_merged_s, merged_s_copied, pe_merged_o, merged_o_copied, pe_latent, rope_products, latent_rotated, pe_operand, operand_hi, pe_xscores, xmax_done, 
         recips_spread, pe_recips_t, pe_probs_t, probs_t_by_vector, probs_t_by_scalar, recips_copied, operand_lo, kv_halves_zeroed, kv_hi, kv_lo, xprobs_done, pe_contexts, sums_inverted, contexts_scaled, pe_xout) = map(sem, (
            "x_zeroed", "kv_products", "kv_rotated", "pe_kv_tokens", "kv_tokens_copied", "pe_merged_q", "merged_q_copied", "pe_merged_s", "merged_s_copied", "pe_merged_o", "merged_o_copied", "pe_latent", "rope_products", "latent_rotated", "pe_operand",
            "operand_hi", "pe_xscores", "xmax_done", "recips_spread", "pe_recips_t", "pe_probs_t", "probs_t_by_vector", "probs_t_by_scalar", "recips_copied", "operand_lo", "kv_halves_zeroed", "kv_hi", "kv_lo", "xprobs_done", "pe_contexts", "sums_inverted", "contexts_scaled", "pe_xout"))
        ld_loaded = sem("ld_loaded")
        pad_ready = sem("pad_ready")
        pe_ffn_xt, xt_hi, xt_lo, pe_logits, logits_copied, pe_logits_tok, logits_shifted, logits_exp, router_steps, pe_combine_t, combine_hi, combine_lo = map(
            sem, ("pe_ffn_xt", "xt_hi", "xt_lo", "pe_logits", "logits_copied", "pe_logits_tok", "logits_shifted", "logits_exp", "router_steps", "pe_combine_t", "combine_hi", "combine_lo"))
        router_w_in, router_w_hi, router_w_lo = map(sem, ("router_w_in", "router_w_hi", "router_w_lo"))
        ffn_filled = sem("ffn_filled")
        raw_in = [[sem(f"raw_in{l}_{u}") for u in range(RING)] for l in range(2)]
        w_hi, w_lo = [[sem(f"{n}{l}") for l in range(2)] for n in ("w_hi", "w_lo")]
        pe_gate_part, pe_up_part, pe_share, silu_done, gated, weighted, act_hi, act_lo, pe_down = [
            [sem(f"{n}{l}") for l in range(2)] for n in ("pe_gate_part", "pe_up_part", "pe_share", "silu_done", "gated", "weighted", "act_hi", "act_lo", "pe_down")]
        y_copied, pe_y_tokens = sem("y_copied"), sem("pe_y_tokens")

        block = ctx.enter_context(nc.Block())

        ROUTER_STEPS = 24
        HALVES = 2 * NB
        SLOTS = 6
        FIRST = (4, 4)
        TURN = (4, 3)

        def score_bank(l, n):
            return FIRST[l] + n % TURN[l]

        def value_bank(l, b, m):
            return m if l else 2 * (b % 2) + m

        def norm_seq(n, b):
            return (b, NB + 2 * b, NB + 2 * b + 1)[n] if n < 3 else NB * n + b

        def out_bank(l, b):
            return 7 if l else 2 * (b % 2) + 1
        UNITS = NB * GROUPS

        def blocks(eng):
            yield 0, False
            with eng.Fori(1, CHUNKS // RING - 1) as i:
                yield i, False
            yield CHUNKS // RING - 1, True

        @block.sync
        def _(sp):
            xf = d["x"].rearrange("b n d -> (b n) d").rearrange("(t p) d -> p t d", p=P)
            for b in range(NB):
                sp.dma_start(X[:, 2 * b:2 * b + 2, :], xf[:, 2 * b:2 * b + 2, :]).then_inc(x_loaded[b], 16)
            sp.dma_start(xb_l[:, :, :], d["xb_l"]).then_inc(xb_loaded, 16)
            sp.dma_start(xb_r[:, :, :], d["xb_r"]).then_inc(xb_loaded, 16)
            sp.dma_start(xb_b[:, :], d["xb_b"]).then_inc(xb_loaded, 16)
            sp.dma_start(cst[:, :], d["const"]).then_inc(const_loaded, 16)
            sp.dma_start(wqkv0[:, :, :, :], d["wqkv0"]).then_inc(w0_loaded, 16)
            sp.dma_start(wg1[:, :, :], d["wg1"]).then_inc(w0_loaded, 16)
            sp.dma_start(wg2[:, :, :], d["wg2"]).then_inc(w0_loaded, 16)
            sp.dma_start(wo_gap[:, :, :, :], d["wo_gap"]).then_inc(w0_loaded, 16)
            sp.dma_start(normw[:, :], d["normw"]).then_inc(w0_loaded, 16)
            sp.dma_start(wqkv1[:, :, :, :], d["wqkv1"]).then_inc(w1_loaded, 16)
            for l in range(2):
                stage = 2 + 3 * l
                W = d[f"ffn{l}"]
                sp.wait_ge(x_done, 8 * stage)
                sp.dma_start(router_w[:, :, :], d[f"gate{l}"]).then_inc(router_w_in, 16)
                for c in range(RING):
                    sp.dma_start(raw[:, c, :], W[c, :, :]).then_inc(raw_in[l][c], 16)
                with sp.Fori(0, CHUNKS // RING - 1) as i:
                    for u in range(RING):
                        c = i * RING + u
                        sp.wait_ge(w_lo[l], c + 1)
                        sp.dma_start(raw[:, u, :], W[bass.ds(c + RING, 1), :, :].rearrange("a p n -> p (a n)")).then_inc(raw_in[l][u], 16)
                if l == 0:
                    sp.wait_ge(x_done, 8 * 3)
                    for hg in range(2):
                        sp.dma_start(wx[:, hg, :], d["wx"][hg, :, :]).then_inc(wx_in[hg], 16)
                    sp.wait_ge(x_done, 8 * 4)
                    sp.dma_start(kvc[:, :, :, :], d["kvc"]).then_inc(kvc_in, 16)
                    kv_tables = CX["coskv"][0]
                    sp.dma_start(cx[:, kv_tables:], d["cx"][:, kv_tables:]).then_inc(kvc_in, 16)
                    sp.dma_start(cx[:, 0:kv_tables], d["cx"][:, 0:kv_tables]).then_inc(cx_in, 16)
                    for hg in range(2, GROUPS):
                        sp.wait_ge(merged_o_copied, hg - 1)
                        sp.dma_start(wx[:, hg % 2, :], d["wx"][hg, :, :]).then_inc(wx_in[hg % 2], 16)
            of = out.rearrange("b n d -> (b n) d").rearrange("(t p) d -> p t d", p=P)
            for b in range(NB):
                sp.wait_ge(x_done, 8 * 5 + 2 * b + 2)
                sp.dma_start(of[:, 2 * b:2 * b + 2, :], X[:, 2 * b:2 * b + 2, :]).then_inc(out_done, 16)
            sp.wait_ge(out_done, 16 * NB)

        @block.vector
        def _(v):
            def norm(n, b):
                norm_statistics(n, b)
                normalise(n, b)

            def norm_statistics(n, b):
                for t in (2 * b, 2 * b + 1):
                    if n == 0:
                        v.wait_ge(x_loaded[b], 16)
                    elif n == 1:
                        v.wait_ge(x_part, t + 1)
                    elif n == 2:
                        v.wait_ge(x_done, 2 * t + 2)
                    else:
                        v.wait_ge(x_done, 8 * (n - 1) + t + 1)
                    v.bn_stats(stats[:, t, :], X[:, t, :]).then_inc(norm_stats, 1)
                for t in (2 * b, 2 * b + 1):
                    v.wait_ge(norm_stats, 2 * norm_seq(n, b) + t % 2 + 1)
                    v.bn_aggr(mv[:, t, :], stats[:, t, :]).then_inc(norm_var, 1)

            def normalise(n, b):
                two = slice(2 * b, 2 * b + 2)
                v.wait_ge(norm_sd, norm_seq(n, b) + 1)
                v.reciprocal(rstd[:, two], sd[:, two]).then_inc(norm_rstd, 1)
                v.wait_ge(norm_rstd, norm_seq(n, b) + 1)
                for t in (2 * b, 2 * b + 1):
                    v.tensor_scalar(xn[:, t, :], X[:, t, :], mv[:, t, 0:1], rstd[:, t:t + 1],
                                    ALU.subtract, ALU.mult).then_inc(norm_done, 1)

            def flat(x):
                return x.rearrange("p m s -> p (m s)")

            def project0(b):
                v.wait_ge(sig_done, 3 * b + 1)
                v.tensor_tensor(flat(qT[:, b]), ps[:, 0, :], sg[:, 0, :], ALU.mult).then_inc(q_ready, 1)
                v.wait_ge(sig_done, 3 * b + 2)
                v.scalar_tensor_tensor(flat(kE[:, b]), ps[:, 1, :], k("even"), sg[:, 1, :], ALU.mult, ALU.mult).then_inc(k_ready, 1)
                v.scalar_tensor_tensor(flat(kO[:, b]), ps[:, 1, :], k("odd"), sg[:, 1, :], ALU.mult, ALU.mult).then_inc(k_ready, 1)
                v.wait_ge(sig_done, 3 * b + 3)
                if b == 0:
                    v.wait_ge(pad_ready, 1)
                for st in range(2):
                    v.tensor_tensor(vpad[:, 2 * b + st, :, 0:HD], ps[:, 2, 256 * st:256 * st + 256].rearrange("p (h e) -> p h e", h=HEADS),
                                    sg[:, 2, 256 * st:256 * st + 256].rearrange("p (h e) -> p h e", h=HEADS), ALU.mult).then_inc(v_ready, 1)

            def project1(b):
                for j, tab in enumerate(("cos", "sin", "cos", "sin")):
                    v.wait_ge(pe_f, 4 * b + j + 1)
                    if b >= 1:
                        v.wait_ge(q_ready if j < 2 else k_sum, 4 + b if j < 2 else b)
                    v.tensor_tensor(sg[:, j, :].rearrange("p (m s) -> p m s", m=2), ps[:, j, :].rearrange("p (m s) -> p m s", m=2),
                                    k(tab).unsqueeze(1).to_broadcast([P, 2, SEQ]), ALU.mult).then_inc(rope_done, 1)

            def reciprocals(b):
                v.wait_ge(p_done, SLOTS * (HALVES + 2 * b + 2))
                v.reciprocal(prec_q[:, :], psum_q[:, b % 2, :]).then_inc(rec_ready, 1)

            def spread_reciprocals(b):
                v.wait_ge(rec_ready, 2 * NB + b + 1)
                if b >= 1:
                    v.wait_ge(pe_ss, HALVES + 2 * b)
                v.tensor_copy(prec_r[:, :, :], prec_q[:, :].unsqueeze(2).to_broadcast([P, 32, 32])).then_inc(spread_ready, 1)

            def scaled(l, b, m):
                if b >= 1:
                    v.wait_ge(pe_out, NB * l + b)
                if l == 0:
                    v.wait_ge(rec_ready, 2 * b + m + 1)
                    for e in range(2):
                        c = slice(256 * e, 256 * e + 256)
                        v.scalar_tensor_tensor(on[:, 2 * m + e, :], og[:, m, c], normw[:, 2 * m + e:2 * m + e + 1], rrec[:, m, c],
                                               ALU.mult, ALU.mult).then_inc(on_ready, 1)
                else:
                    v.wait_ge(pe_ss, HALVES + 2 * b + m + 1)
                    v.tensor_tensor(on[:, 2 * m:2 * m + 2, :].rearrange("p e q -> p (e q)"), og[:, m, :], ps[:, m, :], ALU.mult).then_inc(on_ready, 2)

            def add_out(l, b):
                v.wait_ge(pe_out, NB * l + b + 1)
                for t in range(2):
                    v.tensor_tensor(X[:, 2 * b + t, :], X[:, 2 * b + t, :], ps[:, out_bank(l, b), 256 * t:256 * t + 256], ALU.add).then_inc(
                        x_done if l else x_part, 1)

            def bilinear(b):
                if b == 0:
                    v.wait_ge(xsig_ready, NB)
                for t in (2 * b, 2 * b + 1):
                    v.scalar_tensor_tensor(X[:, t, :], xsig[:, t, :], 0.6, X[:, t, :], ALU.mult, ALU.add).then_inc(xb_part, 1)
                for t in (2 * b, 2 * b + 1):
                    v.wait_ge(xb_part, t + 1)
                    v.wait_ge(norm_done, 2 * norm_seq(1, b) + t % 2 + 1)
                    v.scalar_tensor_tensor(X[:, t, :], xn[:, t, :], 1.0 - 0.6, X[:, t, :], ALU.mult, ALU.add).then_inc(x_done, 2)

            def decayed(u, j):
                n = SLOTS * u + j
                v.wait_ge(pe_s, n + 1)
                bank = ps[:, score_bank(0, n), :]
                if j < 4:
                    h = 8 * (j // 2) + 2 * (2 * (u % 2) + j % 2)
                    v.tensor_tensor(P0[:, u % 2, j, :, :], bank.rearrange("p (e q) -> p e q", e=2), DT[:, h:h + 2, :], ALU.mult).then_inc(p_done, 1)
                else:
                    h = 2 * (2 * (u % 2) + j - 4)
                    v.tensor_tensor(P1[:, u % 2, j - 4::2, :, :], bank.rearrange("p (m e q) -> p m e q", m=2, e=2),
                                    DT[:, :, 0:128].rearrange("p (m h) q -> p m h q", m=2)[:, :, h:h + 2, :], ALU.mult).then_inc(p_done, 1)

            def row_max(u, j):
                n = SLOTS * u + j
                v.wait_ge(pe_s, SLOTS * HALVES + n + 1)
                bank = ps[:, score_bank(1, n), :]
                if j < 2:
                    v.tensor_reduce(nm[:, u % 2, 0, j::2, :], bank.rearrange("p (m e s) -> p m e s", m=2, e=2), AX, ALU.max, negate=True).then_inc(max_done, 1)
                else:
                    v.tensor_reduce(nm[:, u % 2, 1, j - 2, :], bank.rearrange("p (e s) -> p e s", e=2), AX, ALU.max, negate=True).then_inc(max_done, 1)

            def copy_transposed(u, g):
                n = 4 * u + g
                v.wait_ge(pe_ta, n + 1)
                v.tensor_copy(P0[:, u % 2, g, :, :].rearrange("p e q -> p (e q)"), ps[:, 2 + n % 2, :]).then_inc(ta_copied, 1)

            def attention0():
                for b in range(NB):
                    project0(b)
                v.wait_ge(dt_ready, 1)
                for u in range(HALVES + 2):
                    b = u // 2 - 1
                    for j in range(SLOTS):
                        if u < HALVES:
                            decayed(u, j)
                        if b < 0:
                            continue
                        if u % 2 == 0 and j in (2, 3):
                            m = j - 2
                            v.wait_ge(pe_o, 2 * b + 2)
                            v.wait_ge(gate_ready, NB)
                            v.tensor_tensor(og[:, m, :], ps[:, value_bank(0, b, m), :], sgate[:, b, m, :], ALU.mult).then_inc(og_ready, 1)
                        if (u % 2, j) == (1, 0):
                            scaled(0, b, 0)
                        if (u % 2, j) == (1, 2):
                            scaled(0, b, 1)
                        if (u % 2, j) == (1, 5):
                            add_out(0, b)
                            norm_statistics(1, b)
                        if b >= 1 and (u % 2, j) == (0, 1):
                            normalise(1, b - 1)
                        if b >= 1 and (u % 2, j) == (0, 4):
                            bilinear(b - 1)
                            norm_statistics(2, b - 1)
                        if b >= 1 and (u % 2, j) == (1, 3):
                            normalise(2, b - 1)
                normalise(1, NB - 1)
                bilinear(NB - 1)
                norm_statistics(2, NB - 1)
                normalise(2, NB - 1)

            def attention1():
                for b in range(NB):
                    project1(b)
                for u in range(HALVES + 3):
                    for j in range(SLOTS):
                        if u < HALVES:
                            row_max(u, j)
                        if j < 4 and 1 <= u <= HALVES:
                            copy_transposed(u - 1, j)
                        if u >= 2 and u % 2 == 0:
                            b = u // 2 - 1
                            if b < NB and j == 1:
                                reciprocals(b)
                            if b < NB and j == 2:
                                spread_reciprocals(b)
                            if b >= 1 and j == 3:
                                normalise(4, b - 1)
                        if u >= 3 and u % 2 and u // 2 - 1 < NB:
                            b = u // 2 - 1
                            if j in (2, 3):
                                scaled(1, b, j - 2)
                            if j == 5:
                                add_out(1, b)
                                norm_statistics(4, b)

            def experts(l):
                for kk in range(KD):
                    for hf in range(2):
                        n = 2 * kk + hf
                        v.wait_ge(xt_hi, 4 * l + n + 1)
                        v.tensor_tensor(xTl[:, kk, hf, :], ps[:, n, :], xTh[:, kk, hf, :].bitcast(F32), ALU.subtract).then_inc(xt_lo, 1)
                v.wait_ge(router_w_hi, l + 1)
                v.tensor_tensor(router_wl[:, :, :], router_w[:, :, :], router_wh[:, :, :].bitcast(F32), ALU.subtract).then_inc(router_w_lo, 1)
                for c in range(2):
                    split_lo(l, c, c)
                v.wait_ge(pe_logits_tok, l + 1)
                lg = ps[:, 7, 0:TILES * E].rearrange("p (t e) -> p t e", t=TILES)
                v.tensor_reduce(nmx[:, :], lg, AX, ALU.max, negate=True).then_inc(router_steps, 1)
                base = ROUTER_STEPS * l
                v.wait_ge(router_steps, base + 1)
                v.tensor_tensor(logits_s[:, :, :], lg, nmx[:, :].unsqueeze(2).to_broadcast([P, TILES, E]), ALU.add).then_inc(logits_shifted, 1)
                v.wait_ge(logits_exp, l + 1)
                v.tensor_reduce(softmax_den[:, 0, :], exp_logits[:, :, :], AX, ALU.add).then_inc(router_steps, 1)
                v.memset(prob[:, :, E:18], -1.0).then_inc(router_steps, 1)
                v.memset(comb[:, :, E:17], 1.0).then_inc(router_steps, 1)
                v.wait_ge(router_steps, base + 4)
                v.reciprocal(softmax_den[:, 1, :], softmax_den[:, 0, :]).then_inc(router_steps, 1)
                v.wait_ge(router_steps, base + 5)
                v.tensor_tensor(prob[:, :, 0:E], exp_logits[:, :, :], softmax_den[:, 1, :].unsqueeze(2).to_broadcast([P, TILES, E]), ALU.mult).then_inc(router_steps, 1)
                v.wait_ge(router_steps, base + 6)
                for t in range(TILES):
                    v.max(v8[:, t, :], prob[:, t, 0:E]).then_inc(router_steps, 1)
                v.wait_ge(router_steps, base + 14)
                v.memset(v8[:, :, TOP_K:8], -1.0).then_inc(router_steps, 1)
                v.wait_ge(router_steps, base + 15)
                for t in range(TILES):
                    v.match_replace(left[:, t, :], v8[:, t, :], prob[:, t, :], 0.0).then_inc(router_steps, 1)
                v.wait_ge(router_steps, base + 23)
                v.tensor_tensor(comb[:, :, 0:E], prob[:, :, 0:E], left[:, :, 0:E], ALU.subtract).then_inc(router_steps, 1)
                v.wait_ge(router_steps, base + 24)
                if l == 1:
                    v.tensor_reduce(softmax_den[:, 0, :], comb[:, :, 0:E], AX, ALU.add).then_inc(router_steps, 1)
                    v.wait_ge(router_steps, base + 25)
                    v.tensor_scalar(softmax_den[:, 0, :], softmax_den[:, 0, :], 1e-20, None, ALU.add).then_inc(router_steps, 1)
                    v.wait_ge(router_steps, base + 26)
                    v.reciprocal(softmax_den[:, 1, :], softmax_den[:, 0, :]).then_inc(router_steps, 1)
                    v.wait_ge(router_steps, base + 27)
                    v.tensor_tensor(comb[:, :, 0:E], comb[:, :, 0:E], softmax_den[:, 1, :].unsqueeze(2).to_broadcast([P, TILES, E]), ALU.mult).then_inc(router_steps, 1)
                for i, last in blocks(v):
                    for u in range(2 * RING):
                        n = i * (2 * RING) + u
                        c = i * RING + u // 2
                        v.wait_ge(silu_done[l], n + 1)
                        v.wait_ge(pe_up_part[l], n + 1)
                        v.tensor_tensor(gate_times_up[:, u % 2, :], ps[:, 5, :], silu_g[:, u % 2, :], ALU.mult).then_inc(gated[l], 1)
                        v.wait_ge(pe_share[l], n + 1)
                        v.wait_ge(gated[l], n + 1)
                        v.tensor_tensor(weighted_h[:, u % 2, :], ps[:, 6, :], gate_times_up[:, u % 2, :], ALU.mult).then_inc(weighted[l], 1)
                        v.wait_ge(act_hi[l], n + 1)
                        v.tensor_tensor(h_lo[:, u % 2, :], weighted_h[:, u % 2, :], h_hi[:, u % 2, :].bitcast(F32), ALU.subtract).then_inc(act_lo[l], 1)
                        if isinstance(n, int) and n < 2:
                            v.wait_ge(combine_hi, 2 * l + n + 1)
                            v.tensor_tensor(shares[32:49, n, :], ps[0:17, 7, :], shares[0:17, n, :].bitcast(F32), ALU.subtract).then_inc(combine_lo, 1)
                        if u % 2 == 0 and not (last and u // 2 + 2 >= RING):
                            split_lo(l, c + 2, (u // 2 + 2) % RING)
                for t in range(TILES):
                    v.wait_ge(pe_y_tokens, 4 * l + t // 2 + 1)
                    v.tensor_tensor(X[:, t, :], X[:, t, :], ps[:, 7 - t // 2, 256 * (t % 2):256 * (t % 2) + 256], ALU.add).then_inc(x_done, 1)
                    if l == 0 and t % 2:
                        norm_statistics(3, t // 2)
                    if l == 0 and t % 2 and t > 2:
                        normalise(3, t // 2 - 1)
                if l == 0:
                    normalise(3, NB - 1)

            def split_lo(l, c, slot):
                v.wait_ge(w_hi[l], c + 1)
                v.tensor_tensor(wlo[:, slot, :], raw[:, slot, 0:PACK - 128], whi[:, slot, 0:PACK - 128].bitcast(F32), ALU.subtract).then_inc(w_lo[l], 1)

            def cross():
                v.wait_ge(x_done, 8 * 4)
                def rope(w, j):
                    n = 3 * w + j
                    v.wait_ge(pe_latent, n + 1)
                    if w >= 1:
                        v.wait_ge(latent_rotated, 2 * (n - 3) + 2)
                    v.tensor_tensor(r1[:, j, :], ps[:, n % 2, :], kx("cosq")[:, 512 * j:512 * j + 512], ALU.mult).then_inc(rope_products, 1)
                    v.tensor_tensor(r2[:, j, :], ps[:, n % 2, :], kx("sinq")[:, 512 * j:512 * j + 512], ALU.mult).then_inc(rope_products, 1)

                gm = k("gmask").rearrange("p (j e) -> p j e", j=3)
                for hg in range(GROUPS):
                    if hg == 2:
                        v.wait_ge(kvc_in, 32)
                        for j, tab in enumerate(("coskv", "sinkv")):
                            v.tensor_tensor(kvc[:, j, :, :], kvc[:, j, :, :], kx(tab).unsqueeze(1).to_broadcast([P, NB, SEQ]), ALU.mult).then_inc(kv_products, 1)
                        v.wait_ge(kv_products, 2)
                        v.tensor_tensor(kvT[:, :, :], kvc[:, 0, :, :], kvc[:, 1, :, :], ALU.add).then_inc(kv_rotated, 1)
                        v.wait_ge(kv_rotated, 1)
                        v.wait_ge(cx_in, 16)
                        for j in range(3):
                            rope(0, j)
                    v.wait_ge(x_zeroed, hg + 1)
                    for part in range(2):
                        v.wait_ge(pe_merged_s, 2 * hg + part + 1)
                        for piece, j, e in ((0, 0, 0), (0, 0, 1), (1, 1, 0), (2, 1, 1), (3, 2, 0), (3, 2, 1)):
                            col = XC * ((j + e) % 2)
                            v.tensor_scalar(merged_s[:, hg, part, piece, col:col + XC], ps[:, 4 + part, 128 * j + XC * e:128 * j + XC * e + XC],
                                            gm[:, j, e:e + 1], None, ALU.mult).then_inc(merged_s_copied, 1)
                v.wait_ge(x_zeroed, GROUPS + 1)
                v.wait_ge(pe_kv_tokens, 1)
                kv_tok = ps[:, 7, :].rearrange("p (t c) -> p t c", t=TILES)
                v.tensor_copy(kv_tok_ab[:, :, 0, 0:XC], kv_tok).then_inc(kv_tokens_copied, 1)
                v.tensor_copy(kv_tok_ab[:, :, 1, XC:128], kv_tok).then_inc(kv_tokens_copied, 1)

                def row_max(w, n):
                    v.wait_ge(pe_xscores, 4 * w + n + 1)
                    v.tensor_reduce(neg_max[:, n // 2, :, n % 2], ps[:, 3 + n % 2, :].rearrange("p (e s) -> p e s", e=2),
                                    AX, ALU.max, negate=True).then_inc(xmax_done, 1)

                def reciprocals(w):
                    v.wait_ge(xprobs_done, 4 * w + 4)
                    v.reciprocal(rsum[:, :, :, :], sums[:, :, :, :]).then_inc(sums_inverted, 1)
                    v.wait_ge(sums_inverted, w + 1)
                    if w >= 1:
                        v.wait_ge(pe_recips_t, w)
                    for st in range(2):
                        v.tensor_copy(rsumr[:, st, :, :, :], rsum[:, st, :, :].rearrange("p a e -> p e a").unsqueeze(3).to_broadcast([P, 2, 2, 64])).then_inc(recips_spread, 1)

                def copy_transposed(w, k):
                    v.wait_ge(pe_probs_t, 4 * w + k + 1)
                    v.tensor_copy(probs_t[:, k // 2, k % 2, :], ps[:, 5, :]).then_inc(probs_t_by_vector, 1)

                def contexts(w):
                    v.wait_ge(pe_contexts, w + 1)
                    v.wait_ge(recips_copied, w + 1)
                    if w >= 1:
                        v.wait_ge(pe_xout, w)
                    v.tensor_tensor(contexts_sb[:, :, :].rearrange("p e s -> p (e s)"), ps[:, 6, :], recips_t[:, :], ALU.mult).then_inc(contexts_scaled, 1)

                def add_output(b):
                    v.wait_ge(pe_xout, GROUPS * (b + 1))
                    for t in range(2):
                        v.tensor_tensor(X[:, 2 * b + t, :], X[:, 2 * b + t, :], ps[:, 7, 256 * t:256 * t + 256], ALU.add).then_inc(x_done, 1)
                    norm_statistics(5, b)

                for ab in range(2):
                    r = slice(64 * ab, 64 * ab + 64)
                    v.wait_ge(kv_hi, ab + 1)
                    v.tensor_tensor(kvl[r, :, ab, :], kvT[r, :, :], kvh[r, :, ab, :].bitcast(F32), ALU.subtract).then_inc(kv_lo, 1)
                for w in range(UNITS):
                    more = w + 1 < UNITS
                    if w >= 1:
                        contexts(w - 1)
                    v.wait_ge(operand_hi, w + 1)
                    v.tensor_tensor(tSl[:, :, :].rearrange("p e s -> p (e s)"), ps[:, 2, :], tSh[:, :, :].rearrange("p e s -> p (e s)").bitcast(F32),
                                    ALU.subtract).then_inc(operand_lo, 1)
                    row_max(w, 0)
                    row_max(w, 1)
                    if more:
                        rope(w + 1, 0)
                    row_max(w, 2)
                    row_max(w, 3)
                    reciprocals(w)
                    if more:
                        rope(w + 1, 1)
                    copy_transposed(w, 1)
                    if more:
                        rope(w + 1, 2)
                    copy_transposed(w, 3)
                    if w % GROUPS == 0 and w:
                        add_output(w // GROUPS - 1)
                    if w % GROUPS == 1 and w > 1:
                        normalise(5, w // GROUPS - 1)
                contexts(UNITS - 1)
                add_output(NB - 1)
                normalise(5, NB - 1)

            v.memset(epsc[:, :], EPS).then_inc(eps_ready, 1)
            for b in range(NB):
                norm(0, b)
            v.wait_ge(const_loaded, 16)
            v.tensor_copy(identb[:, :], ident).then_inc(setup_v, 1)
            v.tensor_copy(negqs[:, :], k("neg_qs")).then_inc(setup_v, 1)
            attention0()
            experts(0)
            attention1()
            cross()
            experts(1)

        @block.scalar
        def _(a):
            def norm(n, b):
                if n == 0 and b == 0:
                    a.wait_ge(eps_ready, 1)
                a.wait_ge(norm_var, 2 * norm_seq(n, b) + 2)
                a.activation(sd[:, 2 * b:2 * b + 2], mv[:, 2 * b:2 * b + 2, 1], ACT.Sqrt, bias=epsc[:, 0:1]).then_inc(norm_sd, 1)

            def decay(heads):
                for h in heads:
                    a.activation(DT[:, h, :], k("dist"), ACT.Exp, scale=ld_bc[:, h:h + 1]).then_inc(dt_exp, 1)

            def transposed_tokens(i, b):
                a.wait_ge(pe_xt, i + 1)
                a.activation(xT4[:, :, b, :], ps[:, 7, :].rearrange("p (k s) -> p k s", k=KD), ACT.Copy).then_inc(xt_ready, 1)

            def attention0():
                transposed_tokens(0, 0)
                for b in range(NB):
                    if b + 1 < NB:
                        transposed_tokens(b + 1, b + 1)
                    a.wait_ge(pe_q, b + 1)
                    a.activation(sg[:, 0, :], ps[:, 0, :], ACT.Sigmoid).then_inc(sig_done, 1)
                    if b >= 1:
                        gate(b - 1)
                    a.wait_ge(pe_k, b + 1)
                    a.activation(sg[:, 1, :], ps[:, 1, :], ACT.Sigmoid).then_inc(sig_done, 1)
                    a.wait_ge(pe_v, b + 1)
                    a.activation(sg[:, 2, :], ps[:, 2, :], ACT.Sigmoid).then_inc(sig_done, 1)
                    a.wait_ge(pe_g1, b + 1)
                    a.activation(g1S[:, b, :], ps[0:HD, 3, 0:SEQ], ACT.Copy).then_inc(g1_ready, 1)
                    if b < 2:
                        decay(range(8 * b, 8 * b + 8))
                gate(NB - 1)
                for b in range(NB):
                    for m in range(2):
                        a.wait_ge(og_ready, 2 * b + m + 1)
                        a.activation(sq[:, m, :], og[:, m, :], ACT.Square).then_inc(sq_ready, 1)
                    for m in range(2):
                        a.wait_ge(pe_ss, 2 * b + m + 1)
                        a.activation(rms[:, m, :], ps[:, value_bank(0, b, m), :], ACT.Ln, bias=epsc[:, 0:1], scale=1.0 / HD).then_inc(rms_ready, 1)
                    for m in range(2):
                        a.wait_ge(rms_ready, 2 * b + m + 1)
                        a.activation(rrec[:, m, :], rms[:, m, :], ACT.Exp, scale=-0.5).then_inc(rec_ready, 1)
                    if b >= 1:
                        norm(2, b - 1)
                    norm(1, b)
                norm(2, NB - 1)

            def gate(b):
                a.wait_ge(pe_gate, b + 1)
                a.activation(sgate[:, b, :, :], ps[:, 5:7, :], ACT.Sigmoid).then_inc(gate_ready, 1)

            def attention1():
                transposed_tokens(NB, 0)
                for b in range(NB):
                    if b + 1 < NB:
                        transposed_tokens(NB + b + 1, b + 1)
                    if b == 0:
                        a.wait_ge(pad_ready, 2)
                    a.wait_ge(pe_v, NB + b + 1)
                    for st in range(2):
                        a.activation(vpad[:, 2 * b + st, :, 0:HD], ps[:, 6, 256 * st:256 * st + 256].rearrange("p (h e) -> p h e", h=HEADS),
                                     ACT.Copy).then_inc(v_ready, 1)
                for u in range(HALVES + 3):
                    for j in range(SLOTS):
                        if u < HALVES:
                            probabilities(u, j)
                        if j == 0 and 3 <= u <= HALVES + 1 and u % 2:
                            for m in range(2):
                                a.wait_ge(pe_o, HALVES + u - 1)
                                a.activation(og[:, m, :], ps[:, value_bank(1, 0, m), :], ACT.Copy).then_inc(og_ready, 1)
                        if j in (1, 3) and 1 <= u <= HALVES:
                            n = 2 * (u - 1) + j // 2
                            a.wait_ge(pe_tb, n + 1)
                            g = 2 * (j // 2)
                            a.activation(P1[:, (u - 1) % 2, g:g + 2, :, :].rearrange("p g e q -> p (g e q)"), ps[:, 7, :], ACT.Copy).then_inc(tb_copied, 1)
                        if u >= 4 and (u % 2, j) == (0, 1):
                            norm(4, u // 2 - 2)

            def probabilities(u, j):
                n = SLOTS * u + j
                bank = ps[:, score_bank(1, n), :]
                a.wait_ge(max_done, n + 1)
                if j == 0 and u >= 4 and u % 2 == 0:
                    a.wait_ge(rec_ready, 2 * NB + u // 2 - 1)
                if j < 2:
                    heads = [(Q0[:, u % 2, 2 * m + j, e, :], bank[:, 256 * m + 128 * e:256 * m + 128 * e + 128], 0, m, e) for m in range(2) for e in range(2)]
                else:
                    heads = [(Q1[:, u % 2, j - 2, e, :], bank[:, 256 * e:256 * e + 256], 1, j // 2 - 1, e) for e in range(2)]
                for dst, src, qt, m, e in heads:
                    at = 16 * qt + 8 * m + 4 * e + 2 * (u % 2) + j % 2
                    last = a.activation(dst, src, ACT.Exp, bias=nm[:, u % 2, qt, 2 * m + j % 2, e:e + 1], accum_out=psum_q[:, u // 2 % 2, at:at + 1])
                last.then_inc(p_done, 1)

            def split_hi(l, c, slot, turn):
                a.wait_ge(raw_in[l][slot], 16 * (turn + 1))
                a.activation(whi[:, slot, :], raw[:, slot, :], ACT.Copy).then_inc(w_hi[l], 1)

            def experts(l):
                for kk in range(KD):
                    for hf in range(2):
                        n = 2 * kk + hf
                        a.wait_ge(pe_ffn_xt, 4 * l + n + 1)
                        a.activation(xTh[:, kk, hf, :], ps[:, n, :], ACT.Copy).then_inc(xt_hi, 1)
                a.wait_ge(router_w_in, 16 * (l + 1))
                a.activation(router_wh[:, :, :], router_w[:, :, :], ACT.Copy).then_inc(router_w_hi, 1)
                for c in range(2):
                    split_hi(l, c, c, 0)
                for hf in range(2):
                    a.wait_ge(pe_logits, 2 * l + hf + 1)
                    a.activation(logits_t[:, hf, :], ps[0:E, 4 + hf, :], ACT.Copy).then_inc(logits_copied, 1)
                a.wait_ge(logits_shifted, l + 1)
                a.activation(exp_logits[:, :, :], logits_s[:, :, :], ACT.Exp).then_inc(logits_exp, 1)
                for i, last in blocks(a):
                    for u in range(2 * RING):
                        n = i * (2 * RING) + u
                        c = i * RING + u // 2
                        a.wait_ge(pe_gate_part[l], n + 1)
                        a.activation(silu_g[:, u % 2, :], ps[:, 4, :], ACT.Silu).then_inc(silu_done[l], 1)
                        a.wait_ge(weighted[l], n + 1)
                        a.activation(h_hi[:, u % 2, :], weighted_h[:, u % 2, :], ACT.Copy).then_inc(act_hi[l], 1)
                        if isinstance(n, int) and n < 2:
                            a.wait_ge(pe_combine_t, 2 * l + n + 1)
                            a.wait_ge(ffn_filled, 3 * (l + 1))
                            a.activation(shares[0:17, n, :], ps[0:17, 7, :], ACT.Copy).then_inc(combine_hi, 1)
                        if u % 2 == 0 and not (last and u // 2 + 2 >= RING):
                            split_hi(l, c + 2, (u // 2 + 2) % RING, i + (u // 2 + 2) // RING)
                for hf in range(2):
                    a.wait_ge(pe_down[l], 2 * CHUNKS + hf)
                    for mt in range(2):
                        a.activation(y_sb[:, mt, hf, :], ps[:, 2 * mt + hf, :], ACT.Copy).then_inc(y_copied, 1)
                if l == 0:
                    for b in range(NB):
                        norm(3, b)

            def cross():
                a.wait_ge(x_done, 8 * 4)
                for hg in range(GROUPS):
                    for jj in range(4):
                        a.wait_ge(pe_merged_q, 4 * hg + jj + 1)
                        a.activation(merged_q[:, hg, :, :, LO * jj:LO * jj + LO], ps[:, jj, 0:2 * XQ].rearrange("p (k h f) -> p k h f", k=KD, h=2),
                                     ACT.Copy).then_inc(merged_q_copied, 1)
                    a.wait_ge(pe_merged_o, hg + 1)
                    a.activation(merged_o[:, hg, :, :].rearrange("p e n -> p (e n)"), ps[:, 6, :], ACT.Copy).then_inc(merged_o_copied, 1)
                    a.wait_ge(pe_xt, 8 + hg + 1)
                    a.activation(xT4[:, :, hg, :], ps[:, 7, :].rearrange("p (k s) -> p k s", k=KD), ACT.Copy).then_inc(xt_ready, 1)
                a.wait_ge(kv_halves_zeroed, 1)
                for ab in range(2):
                    r = slice(64 * ab, 64 * ab + 64)
                    a.activation(kvh[r, :, ab, :], kvT[r, :, :], ACT.Copy).then_inc(kv_hi, 1)
                for w in range(UNITS):
                    a.wait_ge(pe_operand, w + 1)
                    a.activation(tSh[:, :, :].rearrange("p e s -> p (e s)"), ps[:, 2, :], ACT.Copy).then_inc(operand_hi, 1)
                    for n in range(4):
                        a.wait_ge(xmax_done, 4 * w + n + 1)
                        if w >= 1 and n == 0:
                            a.wait_ge(sums_inverted, w)
                        st, pair = n // 2, n % 2
                        for ab in range(2):
                            last = a.activation(probs_q[:, st, ab, pair, :], ps[:, 3 + pair, 256 * ab:256 * ab + 256], ACT.Exp,
                                                bias=neg_max[:, st, ab, pair:pair + 1], accum_out=sums[:, st, ab, pair:pair + 1])
                        last.then_inc(xprobs_done, 1)
                    for k in (0, 2):
                        a.wait_ge(pe_probs_t, 4 * w + k + 1)
                        a.activation(probs_t[:, k // 2, k % 2, :], ps[:, 5, :], ACT.Copy).then_inc(probs_t_by_scalar, 1)
                    a.wait_ge(pe_recips_t, w + 1)
                    if w >= 1:
                        a.wait_ge(contexts_scaled, w)
                    a.activation(recips_t[:, :], ps[:, 2, :], ACT.Copy).then_inc(recips_copied, 1)
                    if w % GROUPS == 0 and w:
                        norm(5, w // GROUPS - 1)
                norm(5, NB - 1)

            for b in range(NB):
                norm(0, b)
            a.wait_ge(xb_loaded, 16 * 3)
            for b in range(NB):
                a.wait_ge(pe_xb, b + 1)
                a.activation(xsig[:, 2 * b:2 * b + 2, :].rearrange("p t s -> p (t s)"), ps[:, b, :], ACT.Sigmoid, bias=xb_b[:, 0:1]).then_inc(xsig_ready, 1)
            a.wait_ge(const_loaded, 16)
            a.wait_ge(ld_loaded, 16)
            attention0()
            experts(0)
            attention1()
            cross()
            experts(1)

        @block.gpsimd
        def _(g):
            g.dma_start(ld_bc[:, :], d["ld"]).then_inc(ld_loaded, 16)
            g.memset(vpad[:, :, :, :], 0.0).then_inc(pad_ready, 1)

            g.wait_ge(dt_exp, HEADS)
            g.tensor_tensor(DT[:, :, :], DT[:, :, :], k("causal").unsqueeze(1).to_broadcast([P, HEADS, SEQ]), ALU.mult).then_inc(dt_ready, 1)

            def zero_fill(l):
                g.wait_ge(x_done, 8 * (2 + 3 * l))
                g.memset(shares[:, :, :].bitcast(F32), 0.0).then_inc(ffn_filled, 1)
                g.memset(zeros[:, :].bitcast(F32), 0.0).then_inc(ffn_filled, 1)
                g.memset(half_shares[:, :].bitcast(F32), 0.5).then_inc(ffn_filled, 1)

            zero_fill(0)
            g.wait_ge(x_done, 8 * 3)
            g.memset(vpad[:, :, :, :], 0.0).then_inc(pad_ready, 1)
            for b in range(NB):
                g.wait_ge(rope_done, 4 * b + 2)
                g.tensor_tensor(qT[:, b].rearrange("p m s -> p (m s)"), sg[:, 0, :], sg[:, 1, :], ALU.add).then_inc(q_ready, 1)
                g.wait_ge(rope_done, 4 * b + 4)
                if b >= 1:
                    g.wait_ge(k_ready, 2 * (NB + b))
                g.tensor_tensor(kT[:, :, :].rearrange("p m s -> p (m s)"), sg[:, 2, :], sg[:, 3, :], ALU.add).then_inc(k_sum, 1)
                g.wait_ge(k_sum, b + 1)
                g.tensor_scalar(kE[:, b], kT[:, :, :], k("even_s"), None, ALU.mult).then_inc(k_ready, 1)
                g.tensor_scalar(kO[:, b], kT[:, :, :], k("odd_s"), None, ALU.mult).then_inc(k_ready, 1)
            g.wait_ge(x_done, 8 * 4)
            for hg in range(GROUPS):
                g.memset(merged_s[:, hg, :, :, :], 0.0).then_inc(x_zeroed, 1)
            g.memset(kv_tok_ab[:, :, :, :], 0.0).then_inc(x_zeroed, 1)
            for w in range(NB * GROUPS):
                for j in range(3):
                    g.wait_ge(rope_products, 6 * w + 2 * j + 2)
                    if w >= 1:
                        g.wait_ge(pe_operand, w)
                    for part in range(2):
                        g.tensor_tensor(latent_rot[:, j, part, :], r1[:, j, 256 * part:256 * part + 256], r2[:, j, 256 - 256 * part:512 - 256 * part],
                                        ALU.add).then_inc(latent_rotated, 1)
                if w == 0:
                    g.wait_ge(merged_o_copied, GROUPS)
                    g.memset(kvh[:, :, :, :].bitcast(F32), 0.0)
                    g.memset(kvl[:, :, :, :].bitcast(F32), 0.0).then_inc(kv_halves_zeroed, 1)
            zero_fill(1)

        @block.tensor
        def _(pe):
            def mm(o, l, r, start, stop):
                return pe.matmul(o, l, r, start=start, stop=stop, skip_group_check=True)

            def transposed_tokens(l, b):
                i = NB * l + b
                pe.wait_ge(norm_done, 8 * 3 * l + 2 * b + 2)
                if b >= 1:
                    pe.wait_ge(xt_ready, i)
                for kk in range(KD):
                    for t in range(2):
                        last = pe.transpose(ps[:, 7, 256 * kk + 128 * t:256 * kk + 128 * t + 128], xn[:, 2 * b + t, 128 * kk:128 * kk + 128], ident)
                last.then_inc(pe_xt, 1)

            def features(l, bank, j, b):
                w = (wqkv0, wqkv1)[l]
                for m in range(2):
                    for kk in range(KD):
                        last = mm(ps[:, bank, 256 * m:256 * m + 256], w[:, j, kk, 128 * m:128 * m + 128], xT4[:, kk, b, :], kk == 0, kk == KD - 1)
                return last

            def tokens(l, bank, j, b):
                w = (wqkv0, wqkv1)[l]
                for st in range(2):
                    for kk in range(KD):
                        last = mm(ps[:, bank, 256 * st:256 * st + 256], xT4[:, kk, b, 128 * st:128 * st + 128], w[:, j, kk, :], kk == 0, kk == KD - 1)
                return last

            def gate(b):
                pe.wait_ge(g1_ready, b + 1)
                if b >= 1:
                    pe.wait_ge(gate_ready, b)
                for grp in range(4):
                    last = mm(ps[:, 5 + grp // 2, 256 * (grp % 2):256 * (grp % 2) + 256], wg2[:, grp, :], g1S[:, b, :], True, True)
                last.then_inc(pe_gate, 1)

            def mixed_values(l, u):
                b = u // 2
                for st in range(2):
                    for m in range(2):
                        for e in range(2):
                            for gi in range(2):
                                g = 2 * (u % 2) + gi
                                last = mm(ps[32 * g:32 * g + 32, value_bank(l, b, m), 256 * e + 128 * st:256 * e + 256], vpad[:, 2 * b + st, 8 * m + 2 * g + e, :],
                                          (P0 if st == 0 else P1)[:, u % 2, 2 * m + gi, e, :], st == 0 and e == 0, st == 1)
                last.then_inc(pe_o, 1)

            def output(l, b):
                for grp in range(4):
                    if grp % 2 == 0:
                        pe.wait_ge(on_ready, 4 * (NB * l + b) + grp + 2)
                    for t in range(2):
                        last = mm(ps[:, out_bank(l, b), 256 * t:256 * t + 256], on[:, grp, 128 * t:128 * t + 128], wo_gap[:, l, grp, :],
                                  grp == 0 and t == 0, grp == 3)
                last.then_inc(pe_out, 1)

            def scores_by_key(u, j):
                n, b = SLOTS * u + j, u // 2
                if n >= TURN[0]:
                    pe.wait_ge(p_done, n - TURN[0] + 1)
                bank = ps[:, score_bank(0, n), :]
                g = 2 * (u % 2) + j % 2
                r = slice(32 * g, 32 * g + 32)
                for m in ((j // 2,) if j < 4 else (0, 1)):
                    for e, kk in enumerate((kE, kO)):
                        if j < 4:
                            last = mm(bank[:, 256 * e:256 * e + 256], kk[r, b, m, 0:128], qT[r, b, m, :], True, True)
                        else:
                            c = 256 * m + 128 * e
                            last = mm(bank[:, c:c + 128], kk[r, b, m, 128:256], qT[r, b, m, 128:256], True, True)
                last.then_inc(pe_s, 1)

            def scores_by_query(u, j):
                n, b = SLOTS * u + j, u // 2
                if n >= TURN[1]:
                    pe.wait_ge(p_done, SLOTS * HALVES + n - TURN[1] + 1)
                bank = ps[:, score_bank(1, n), :]
                if j < 2:
                    mm(bank.rearrange("p (e s) -> p e s", e=4), identb[:, :], negqs[:, :].unsqueeze(1).to_broadcast([P, 4, 128]), True, False)
                else:
                    mm(bank.rearrange("p (e s) -> p e s", e=2)[:, :, 128:256], identb[:, :], negqs[:, :].unsqueeze(1).to_broadcast([P, 2, 128]), True, False)
                g = 2 * (u % 2) + j % 2
                r = slice(32 * g, 32 * g + 32)
                for m in ((0, 1) if j < 2 else (j // 2 - 1,)):
                    for e, kk in enumerate((kE, kO)):
                        if j < 2:
                            c = 256 * m + 128 * e
                            last = mm(bank[:, c:c + 128], qT[r, b, m, 0:128], kk[r, b, m, 0:128], False, True)
                        else:
                            last = mm(bank[:, 256 * e:256 * e + 256], qT[r, b, m, 128:256], kk[r, b, m, :], False, True)
                last.then_inc(pe_s, 1)

            def transpose_a(u, g):
                n, par = 4 * u + g, u % 2
                pe.wait_ge(p_done, SLOTS * (HALVES + u) + 3 + g)
                if n >= 2:
                    pe.wait_ge(ta_copied, n - 1)
                for e in range(2):
                    pe.transpose(ps[:, 2 + n % 2, 256 * e:256 * e + 128], Q0[:, par, g, e, :], ident)
                    last = pe.transpose(ps[:, 2 + n % 2, 256 * e + 128:256 * e + 256], Q1[:, par, g, e, 0:128], ident)
                last.then_inc(pe_ta, 1)

            def transpose_b(u, half):
                n, par = 2 * u + half, u % 2
                if n >= 1:
                    pe.wait_ge(tb_copied, n)
                if half == 0 and u >= 3 and u % 2:
                    pe.wait_ge(x_done, 8 * 3 + 2 * ((u - 3) // 2) + 2)
                for c in range(4):
                    last = pe.transpose(ps[:, 7, 128 * c:128 * c + 128], Q1[:, par, 2 * half + c // 2, c % 2, 128:256], ident)
                last.then_inc(pe_tb, 1)

            def attention0():
                pe.wait_ge(xb_loaded, 16 * 3)
                for b in range(NB):
                    for t in range(2):
                        last = mm(ps[:, b, 256 * t:256 * t + 256], xb_l[:, b, 128 * t:128 * t + 128], xb_r[:, b, :], True, True)
                    last.then_inc(pe_xb, 1)
                pe.wait_ge(const_loaded, 16)
                transposed_tokens(0, 0)
                pe.wait_ge(w0_loaded, 16 * 5)
                for b in range(NB):
                    if b + 1 < NB:
                        transposed_tokens(0, b + 1)
                    pe.wait_ge(xt_ready, b + 1)
                    if b == 0:
                        pe.wait_ge(xsig_ready, NB)
                    else:
                        pe.wait_ge(q_ready, b)
                    features(0, 0, 0, b).then_inc(pe_q, 1)
                    if b >= 1:
                        gate(b - 1)
                        pe.wait_ge(k_ready, 2 * b)
                    features(0, 1, 1, b).then_inc(pe_k, 1)
                    if b >= 1:
                        pe.wait_ge(v_ready, 2 * b)
                    tokens(0, 2, 2, b).then_inc(pe_v, 1)
                    for kk in range(KD):
                        last = mm(ps[0:HD, 3, 0:SEQ], wg1[:, kk, :], xT4[:, kk, b, :], kk == 0, kk == KD - 1)
                    last.then_inc(pe_g1, 1)
                gate(NB - 1)
                for u in range(HALVES + 2):
                    for j in range(SLOTS):
                        if u < HALVES:
                            if j == 0 and u % 2 == 0:
                                pe.wait_ge(q_ready, u // 2 + 1)
                                pe.wait_ge(k_ready, 2 * (u // 2) + 2)
                            if u == 0 and j == 1:
                                pe.wait_ge(gate_ready, NB)
                            scores_by_key(u, j)
                        if j == 1 and 1 <= u <= HALVES:
                            w = u - 1
                            pe.wait_ge(v_ready, 2 * (w // 2) + 2)
                            if w == 0:
                                pe.wait_ge(k_ready, 2 * NB)
                            if w == 4:
                                pe.wait_ge(x_part, 2)
                            if w == 6:
                                pe.wait_ge(x_part, 4)
                            pe.wait_ge(p_done, SLOTS * w + 6)
                            mixed_values(0, w)
                        b = u // 2 - 1
                        if b >= 0 and (u % 2, j) == (0, 4):
                            for m in range(2):
                                pe.wait_ge(sq_ready, 2 * b + m + 1)
                                mm(ps[:, value_bank(0, b, m), :], k("block_ones"), sq[:, m, :], True, True).then_inc(pe_ss, 1)
                        if b >= 0 and (u % 2, j) == (1, 4):
                            output(0, b)

            def attention1():
                pe.wait_ge(w1_loaded, 16)
                transposed_tokens(1, 0)
                for b in range(NB):
                    if b + 1 < NB:
                        transposed_tokens(1, b + 1)
                    pe.wait_ge(xt_ready, NB + b + 1)
                    if b == 0:
                        pe.wait_ge(x_done, 8 * 2 + 4)
                    else:
                        pe.wait_ge(v_ready, 2 * (NB + b))
                    tokens(1, 6, 4, b).then_inc(pe_v, 1)
                    for j in range(4):
                        if b >= 1:
                            pe.wait_ge(rope_done, 4 * (b - 1) + j + 1)
                        features(1, j, j, b).then_inc(pe_f, 1)
                pe.wait_ge(setup_v, 2)
                for u in range(HALVES + 2):
                    for j in range(SLOTS):
                        if u < HALVES:
                            if j == 0 and u % 2 == 0:
                                pe.wait_ge(q_ready, NB + u // 2 + 1)
                                pe.wait_ge(k_ready, 2 * (NB + u // 2) + 2)
                            if u == 0 and j == 2:
                                pe.wait_ge(v_ready, 4 * NB)
                            if u == 0 and j == 0:
                                pe.wait_ge(x_done, 8 * 3)
                            scores_by_query(u, j)
                        if j < 4 and 1 <= u <= HALVES:
                            if u == 1 and j == 0:
                                pe.wait_ge(rope_done, 4 * NB)
                            transpose_a(u - 1, j)
                            if j % 2:
                                transpose_b(u - 1, j // 2)
                        b = (u - 3) // 2
                        if 3 <= u <= HALVES + 1 and u % 2 and j == 1:
                            for m in range(2):
                                pe.wait_ge(og_ready, HALVES + 2 * b + m + 1)
                                pe.wait_ge(spread_ready, b + 1)
                                for e in range(2):
                                    for qt in range(2):
                                        at = 16 * qt + 8 * m + 4 * e
                                        last = pe.transpose(ps[:, m, 256 * e + 128 * qt:256 * e + 128 * qt + 128], prec_r[:, at:at + 4, :].rearrange("p g c -> p (g c)"), ident)
                                last.then_inc(pe_ss, 1)
                        if 3 <= u <= HALVES + 1 and u % 2 and j == 4:
                            pe.wait_ge(tb_copied, min(2 * u, 2 * HALVES))
                            output(1, b)
                        if j == 5 and 1 <= u <= HALVES:
                            w = u - 1
                            pe.wait_ge(ta_copied, 4 * w + 4)
                            pe.wait_ge(tb_copied, 2 * w + 2)
                            if w >= 2 and w % 2 == 0:
                                pe.wait_ge(on_ready, 4 * (NB + w // 2))
                            mixed_values(1, w)

            def experts(l):
                stage = 2 + 3 * l
                for kk in range(KD):
                    for hf in range(2):
                        for t in range(4):
                            pe.wait_ge(norm_done, 2 * norm_seq(stage, 2 * hf + t // 2) + t % 2 + 1)
                            last = pe.transpose(ps[:, 2 * kk + hf, 128 * t:128 * t + 128], xn[:, 4 * hf + t, 128 * kk:128 * kk + 128], ident)
                        last.then_inc(pe_ffn_xt, 1)
                pe.wait_ge(xt_lo, 4 * (l + 1))
                pe.wait_ge(router_w_lo, l + 1)
                for hf in range(2):
                    pairs = ((router_wh, xTh), (router_wl, xTh), (router_wh, xTl))
                    for j, (w, x) in enumerate(pairs):
                        for kk in range(KD):
                            last = mm(ps[0:E, 4 + hf, :], w[:, kk, :], x[:, kk, hf, :], j + kk == 0, j == 2 and kk == 1)
                    last.then_inc(pe_logits, 1)
                pe.wait_ge(logits_copied, 2 * (l + 1))
                for t in range(TILES):
                    last = pe.transpose(ps[:, 7, E * t:E * t + E], logits_t[:, t // 4, 128 * (t % 4):128 * (t % 4) + 128], ident[0:E, 0:E])
                last.then_inc(pe_logits_tok, 1)
                pe.wait_ge(ffn_filled, 3 * (l + 1))
                for bank in range(4):
                    last = mm(ps[:, bank, :], zeros[:, 0:128], zeros[:, :], True, False)
                last.then_inc(pe_down[l], 1)

                def after(semaphore, n):
                    if not isinstance(n, int) or n > 0:
                        pe.wait_ge(semaphore, n)

                def combine_transposed(hf):
                    pe.wait_ge(router_steps, 24 if l == 0 else 24 + 28)
                    if hf:
                        pe.wait_ge(combine_lo, 2 * l + 1)
                    for t in range(4):
                        last = pe.transpose(ps[0:17, 7, 128 * t:128 * t + 128], comb[:, 4 * hf + t, :], ident)
                    last.then_inc(pe_combine_t, 1)

                def gate_up(n, u):
                    slot, hf = u // 2 % RING, u % 2
                    pe.wait_ge(w_lo[l], nchunk(n, u) + 1)
                    after(silu_done[l], n)
                    three(4, whi, wlo, slot, 0, hf).then_inc(pe_gate_part[l], 1)
                    after(gated[l], n)
                    three(5, whi, wlo, slot, 256, hf).then_inc(pe_up_part[l], 1)

                def three(bank, hi, lo, slot, col, hf):
                    first = True
                    for w, x in ((hi, xTh), (lo, xTh), (hi, xTl)):
                        for kk in range(KD):
                            last = mm(ps[:, bank, :], w[:, slot, col + 128 * kk:col + 128 * kk + 128], x[:, kk, hf, :], first, False)
                            first = False
                    return last

                def weights_of_experts(n, u):
                    after(weighted[l], n)
                    if isinstance(n, int) and n == 2 * SHARED_CHUNKS:
                        pe.wait_ge(combine_lo, 2 * (l + 1))
                    share = half_shares[:, :] if isinstance(n, int) and n < 2 * SHARED_CHUNKS else shares[:, u % 2, :]
                    mm(ps[:, 6, :], whi[0:64, u // 2 % RING, PACK - 128:PACK], share, True, True).then_inc(pe_share[l], 1)

                def down(n, u):
                    slot, hf = u // 2 % RING, u % 2
                    pe.wait_ge(act_lo[l], n + 1)
                    for mt in range(2):
                        for w, x in ((whi, h_hi), (wlo, h_hi), (whi, h_lo)):
                            last = mm(ps[:, 2 * mt + hf, :], w[:, slot, 512 + 128 * mt:640 + 128 * mt], x[:, u % 2, :], False, False)
                    last.then_inc(pe_down[l], 1)

                def nchunk(n, u):
                    return cur[0] * RING + u // 2

                cur = [0]
                gate_up(0, 0)
                weights_of_experts(0, 0)
                for i, last in blocks(pe):
                    cur[0] = i
                    for u in range(2 * RING):
                        n = i * (2 * RING) + u
                        if not (last and u == 2 * RING - 1):
                            gate_up(n + 1, u + 1)
                            weights_of_experts(n + 1, u + 1)
                        if isinstance(n, int) and n < 2:
                            combine_transposed(n)
                        down(n, u)
                for t in range(TILES):
                    if t % 4 == 0:
                        pe.wait_ge(y_copied, 4 * l + 2 * (t // 4) + 2)
                    for mt in range(2):
                        last = pe.transpose(ps[:, 7 - t // 2, 256 * (t % 2) + 128 * mt:256 * (t % 2) + 128 * mt + 128],
                                            y_sb[:, mt, t // 4, 128 * (t % 4):128 * (t % 4) + 128], ident)
                    if t % 2:
                        last.then_inc(pe_y_tokens, 1)

            def cross():
                def part_of(slot, name, rows=P):
                    a, b = XP[name]
                    return wx[0:rows, slot, a:b]

                pe.wait_ge(on_ready, 8 * NB)
                def latent_queries(w, j):
                    b, hg, n = w // GROUPS, w % GROUPS, 3 * w + j
                    if n >= 2:
                        pe.wait_ge(rope_products, 2 * (n - 2) + 2)
                    for part in range(2):
                        for kk in range(KD):
                            last = mm(ps[:, n % 2, 256 * part:256 * part + 256], merged_q[:, hg, kk, part, 128 * j:128 * j + 128], xT4[:, kk, b, :], kk == 0, kk == 1)
                    last.then_inc(pe_latent, 1)

                for hg in range(GROUPS):
                    slot = hg % 2
                    pe.wait_ge(wx_in[slot], 16 * (hg // 2 + 1))
                    wq = part_of(slot, "wq").rearrange("p (h d) -> p h d", h=4)
                    kcq = part_of(slot, "kcq").rearrange("p (h q) -> p h q", h=4)
                    qrT = part_of(slot, "qrT", XR).rearrange("p (h f) -> p h f", h=2)
                    krT = part_of(slot, "krT", XR)
                    kckv = part_of(slot, "kckv").rearrange("p (h c) -> p h c", h=4)
                    woT = part_of(slot, "woT").rearrange("p (h n) -> p h n", h=4)
                    for jj in range(4):
                        if hg >= 1:
                            pe.wait_ge(merged_q_copied, 4 * (hg - 1) + jj + 1)
                        if hg == 2 and jj < 2:
                            pe.wait_ge(rope_products, 6 - 2 * jj)
                        for kk in range(KD):
                            last = mm(ps[:, jj, XQ * kk:XQ * kk + XQ], wq[:, jj, 128 * kk:128 * kk + 128], kcq[:, jj, :], True, True)
                        last.then_inc(pe_merged_q, 1)
                    for part in range(2):
                        if hg >= 1:
                            pe.wait_ge(merged_s_copied, 12 * (hg - 1) + 6 * part + 6)
                        for j in range(3):
                            last = mm(ps[:, 4 + part, 128 * j:128 * j + 128], qrT[:, part, 128 * j:128 * j + 128], krT[:, XC * j:XC * j + 2 * XC], True, True)
                        last.then_inc(pe_merged_s, 1)
                    if hg >= 1:
                        pe.wait_ge(merged_o_copied, hg)
                    for jj in range(4):
                        last = mm(ps[64 * (jj % 2):64 * (jj % 2) + 64, 6, 256 * (jj // 2):256 * (jj // 2) + 256], kckv[:, jj, :], woT[:, jj, :], True, True)
                    last.then_inc(pe_merged_o, 1)
                    b = hg
                    pe.wait_ge(*((xt_ready, 8 + b) if b else (x_done, 8 * 4)))
                    pe.wait_ge(norm_done, 8 * 4 + 2 * b + 2)
                    for kk in range(KD):
                        for t in range(2):
                            last = pe.transpose(ps[:, 7, 256 * kk + 128 * t:256 * kk + 128 * t + 128], xn[:, 2 * b + t, 128 * kk:128 * kk + 128], ident)
                    last.then_inc(pe_xt, 1)
                    if hg == 1:
                        pe.wait_ge(xt_ready, 8 + 1)
                        pe.wait_ge(merged_q_copied, 8)
                        for j in range(3):
                            latent_queries(0, j)
                pe.wait_ge(merged_q_copied, 4 * GROUPS)
                pe.wait_ge(merged_o_copied, GROUPS)
                pe.wait_ge(merged_s_copied, 12 * GROUPS)
                pe.wait_ge(xt_ready, 8 + NB)
                pe.wait_ge(kv_rotated, 1)
                for t in range(TILES):
                    last = pe.transpose(ps[:, 7, XC * t:XC * t + XC], kvT[0:XC, t // 2, 128 * (t % 2):128 * (t % 2) + 128], ident[0:XC, 0:XC])
                last.then_inc(pe_kv_tokens, 1)

                def query_side(w):
                    pe.wait_ge(latent_rotated, 6 * w + 6)
                    if w >= 1:
                        pe.wait_ge(recips_copied, w)
                    for pair in range(2):
                        n = 0
                        for piece in (2 * pair, 2 * pair + 1):
                            j = pair + piece % 2
                            for part in range(2):
                                last = mm(ps[:, 2, 256 * pair:256 * pair + 256], merged_s[:, w % GROUPS, part, piece, :], latent_rot[:, j, part, :], n == 0, n == 3)
                                n += 1
                    last.then_inc(pe_operand, 1)

                def max_scores(w, n):
                    st, pair, b = n // 2, n % 2, w // GROUPS
                    if w == 0 and n == 0:
                        pe.wait_ge(kv_lo, 2)
                    if n == 0:
                        pe.wait_ge(operand_lo, w + 1)
                    if 4 * w + n >= 2:
                        pe.wait_ge(xprobs_done, 4 * w + n - 1)
                    for i, (t, kv) in enumerate(((tSh, kvh), (tSh, kvl), (tSl, kvh))):
                        last = mm(ps[:, 3 + pair, :], t[:, pair, 128 * st:128 * st + 128], kv[:, b, :, :].rearrange("p a s -> p (a s)"), i == 0, i == 2)
                    last.then_inc(pe_xscores, 1)

                def transposed_probabilities(w, k):
                    ab, lt = k // 2, k % 2
                    if ab == 0 and lt == 0:
                        if w >= 1:
                            pe.wait_ge(probs_t_by_vector, 2 * w)
                    elif lt:
                        pe.wait_ge(probs_t_by_scalar, 2 * w + ab + 1)
                    else:
                        pe.wait_ge(probs_t_by_vector, 2 * w + 1)
                    pe.wait_ge(xprobs_done, 4 * w + 4)
                    for pair in range(2):
                        for st in range(2):
                            last = pe.transpose(ps[:, 5, 256 * pair + 128 * st:256 * pair + 128 * st + 128], probs_q[:, st, ab, pair, 128 * lt:128 * lt + 128], ident)
                    last.then_inc(pe_probs_t, 1)

                def transposed_reciprocals(w):
                    pe.wait_ge(recips_spread, 2 * w + 2)
                    for pair in range(2):
                        for st in range(2):
                            last = pe.transpose(ps[:, 2, 256 * pair + 128 * st:256 * pair + 128 * st + 128], rsumr[:, st, pair, :, :].rearrange("p a c -> p (a c)"), ident)
                    last.then_inc(pe_recips_t, 1)

                def weighted_contexts(w, k):
                    ab, lt = k // 2, k % 2
                    if k == 0 and w >= 1:
                        pe.wait_ge(contexts_scaled, w)
                    if lt:
                        pe.wait_ge(probs_t_by_vector, 2 * w + ab + 1)
                    else:
                        pe.wait_ge(probs_t_by_scalar, 2 * w + ab + 1)
                    last = mm(ps[:, 6, :], kv_tok_ab[:, 2 * (w // GROUPS) + lt, ab, :], probs_t[:, ab, lt, :], k == 0, k == 3)
                    if k == 3:
                        last.then_inc(pe_contexts, 1)

                def output(w):
                    b, hg = w // GROUPS, w % GROUPS
                    pe.wait_ge(contexts_scaled, w + 1)
                    if w == 0:
                        pe.wait_ge(kv_tokens_copied, 2)
                    elif hg == 0:
                        pe.wait_ge(x_done, 8 * 4 + 2 * b)
                    for t in range(2):
                        for pair in range(2):
                            last = mm(ps[:, 7, 256 * t:256 * t + 256], contexts_sb[:, pair, 128 * t:128 * t + 128], merged_o[:, hg, pair, :],
                                      hg + t + pair == 0, hg == 3 and pair == 1)
                    last.then_inc(pe_xout, 1)

                for w in range(UNITS):
                    more = w + 1 < UNITS
                    query_side(w)
                    if more:
                        latent_queries(w + 1, 0)
                    max_scores(w, 0)
                    max_scores(w, 1)
                    if w >= 1:
                        output(w - 1)
                    max_scores(w, 2)
                    max_scores(w, 3)
                    if more:
                        latent_queries(w + 1, 1)
                    transposed_probabilities(w, 0)
                    if more:
                        latent_queries(w + 1, 2)
                    transposed_probabilities(w, 1)
                    weighted_contexts(w, 0)
                    transposed_probabilities(w, 2)
                    weighted_contexts(w, 1)
                    transposed_probabilities(w, 3)
                    weighted_contexts(w, 2)
                    transposed_reciprocals(w)
                    weighted_contexts(w, 3)
                output(UNITS - 1)

            attention0()
            experts(0)
            attention1()
            cross()
            experts(1)


def constants():
    c = np.zeros((P, CONST_W), np.float32)
    p = np.arange(P)

    def put(name, a):
        lo, hi = CONST[name]
        c[:, lo:hi] = np.asarray(a, np.float32).reshape(P, hi - lo)

    put("ident", np.eye(P))
    q = np.arange(SEQ)
    put("dist", np.maximum(q[None] - p[:, None], 0))
    put("causal", q[None] >= p[:, None])
    put("neg_qs", np.where(p[None] > p[:, None], NEG, 0.0))
    head = (np.arange(3)[None] * P + p[:, None]) // LO
    put("gmask", head[:, :, None] == np.arange(3)[None, :, None] + np.arange(2)[None, None, :])
    put("even", (p // HD) % 2 == 0)
    put("odd", (p // HD) % 2 == 1)
    scale = 1.0 / HD ** 0.5
    put("even_s", ((p // HD) % 2 == 0) * scale)
    put("odd_s", ((p // HD) % 2 == 1) * scale)
    same = (p[:, None] // 32) == (p[None] // 32)
    put("block_ones", same & (p[:, None] % 32 < HD))
    dd = p % HD
    inv = np.float32(10000.0) ** (-(np.arange(0, HD, 2, dtype=np.float32) / np.float32(HD)))
    ang = (q.astype(np.float32)[None] * inv[dd // 2][:, None]).astype(np.float32)
    put("cos", np.cos(ang))
    put("sin", np.where(dd[:, None] % 2 == 0, -1.0, 1.0) * np.sin(ang))
    return c


def cross_constants():
    c = np.zeros((P, CX_W), np.float32)
    p = np.arange(P)
    pos = np.arange(SEQ, dtype=np.float32)

    def put(name, a):
        lo, hi = CX[name]
        c[:, lo:hi] = np.asarray(a, np.float32).reshape(P, hi - lo)

    def angles(dim, feature):
        inv = np.float32(1.0) / np.float32(10000.0) ** (np.arange(0, dim, 2, dtype=np.float32) / np.float32(dim))
        return (pos * inv[feature // 2][..., None]).astype(np.float32)

    f = (np.arange(3)[None] * P + p[:, None]) % LO
    lo, hi = angles(XQ, f), angles(XQ, f + LO)
    put("cosq", np.stack([np.cos(lo), np.cos(hi)], axis=2))
    put("sinq", np.stack([np.sin(hi), -np.sin(lo)], axis=2))
    g = angles(XC, p % XC)
    put("coskv", np.cos(g))
    put("sinkv", np.where((p % XC < XC // 2)[:, None], -1.0, 1.0) * np.sin(g))
    return c


def cross_pack(i):
    o = np.zeros((GROUPS, P, XPACK), np.float32)

    def put(name, a):
        lo, hi = XP[name]
        o[:, 0:a.shape[1], lo:hi] = a.reshape(GROUPS, a.shape[1], hi - lo)

    def by_group(a, *axes):
        return a.reshape((GROUPS, 4) + a.shape[1:]).transpose(axes)

    put("wq", by_group(i["L1_xattn_Wq"].reshape(XH, XK, D), 0, 2, 1, 3))
    put("kcq", by_group(i["L1_xattn_w_kc_q"], 0, 2, 1, 3))
    put("qrT", by_group(i["L1_xattn_W_qr"].reshape(XH, 2, LO, XR), 0, 4, 2, 1, 3))
    put("krT", by_group(i["L1_xattn_W_kr"], 0, 3, 1, 2))
    put("kckv", by_group(i["L1_xattn_w_kc_kv"], 0, 2, 1, 3))
    put("woT", by_group(i["L1_xattn_Wo"].T.reshape(XH, XK, D), 0, 2, 1, 3))
    return o


def rows_to_lhs(w):
    return w.reshape(KD, P, -1).transpose(1, 0, 2)


def gap_rows(w):
    n = w.shape[1]
    o = np.zeros((4, 32, 4, n), w.dtype)
    w = w.reshape(2, 4, 2, HD, n)
    for m in range(2):
        for e in range(2):
            o[:, 0:HD, 2 * m + e] = w[m, :, e]
    return o.reshape(P, 4, n)


def expert_pack(w13, w2, s13, s2):
    total = CHUNKS * P
    def rows(experts, shared):
        o = np.zeros((total, D), np.float32)
        o[:SHARED] = shared
        o[SHARED:SHARED + E * INNER] = experts.reshape(E * INNER, D)
        return o

    g = rows(w13[:, :INNER], s13[:SHARED]).reshape(CHUNKS, P, KD, P)
    u = rows(w13[:, INNER:], s13[SHARED:]).reshape(CHUNKS, P, KD, P)
    dn = rows(w2.transpose(0, 2, 1), s2.T).reshape(CHUNKS, P, D)
    sel = np.zeros((total, P), np.float32)
    r = np.arange(total)
    e = np.where(r < SHARED, E, np.minimum((r - SHARED) // INNER, E))
    sel[r, e] = 1
    sel[r, 32 + e] = 1
    sel = sel.reshape(CHUNKS, P, P).transpose(0, 2, 1)
    g = g.transpose(0, 3, 2, 1).reshape(CHUNKS, P, 2 * P)
    u = u.transpose(0, 3, 2, 1).reshape(CHUNKS, P, 2 * P)
    return np.concatenate([g, u, dn, sel], axis=2)


def lay_out(i):
    i = {k: np.asarray(v) for k, v in i.items()}
    ctxT = i["ctx_512"].transpose(2, 0, 1)
    xw = i["L0_xattn_W"][0]
    half = (64, NB, SEQ)
    swap = np.arange(D) ^ 1
    turn = np.arange(XC) ^ (XC // 2)
    wq, wk, wv = (i[f"L1_attn_w{c}"] for c in "qkv")
    return {
        "x": i["x"],
        "const": constants(),
        "ld": np.broadcast_to(i["L0_attn_log_decay"], (P, HEADS)),
        "wqkv0": np.stack([rows_to_lhs(i[f"L0_attn_W{c}"]) for c in "qkv"], axis=1),
        "wg1": rows_to_lhs(i["L0_attn_Wg1"]),
        "wg2": gap_rows(i["L0_attn_Wg2"].T).transpose(2, 1, 0),
        "wo_gap": np.stack([gap_rows(i["L0_attn_Wo"]), gap_rows(i["L1_attn_wo"].T)], axis=1),
        "normw": gap_rows(i["L0_attn_norm_w"].reshape(D, 1))[:, :, 0],
        "xb_l": np.concatenate([ctxT, np.broadcast_to(xw[64:, None, None], half)]),
        "xb_r": np.concatenate([np.broadcast_to(xw[:64, None, None], half), ctxT]),
        "xb_b": np.broadcast_to(i["L0_xattn_b"].reshape(1, 1), (P, 1)),
        "wqkv1": np.stack([rows_to_lhs(w.T) for w in (wq, wq[swap], wk, wk[swap], wv)], axis=1),
        "gate0": rows_to_lhs(i["L0_ffn_gate_w"].T),
        "gate1": rows_to_lhs(i["L1_ffn_gate_w"].T),
        "wx": cross_pack(i),
        "cx": cross_constants(),
        "kvc": np.stack([np.concatenate([ctxT, ctxT]), np.concatenate([ctxT[turn], ctxT[turn]])], axis=1),
        "ffn0": expert_pack(i["L0_ffn_w1"], i["L0_ffn_w2"], i["L0_ffn_shared_w1"], i["L0_ffn_shared_w2"]),
        "ffn1": expert_pack(i["L1_ffn_w13"], i["L1_ffn_w2"], i["L1_ffn_sw13"], i["L1_ffn_sw2"]),
    }


def kernel(**inputs):
    import numpy as _np
    import concourse.bacc as _bacc
    from concourse import mybir as _mybir
    from concourse.bass_utils import run_bass_kernel_spmd as _run

    nc = _bacc.Bacc("TRN2", target_bir_lowering=False, num_devices=1)
    arrays, aps = {}, {}
    for name, a in lay_out(inputs).items():
        a = _np.ascontiguousarray(a)
        arrays[f"in_{name}"] = a
        aps[name] = nc.dram_tensor(f"in_{name}", a.shape, _mybir.dt.from_np(a.dtype), kind="ExternalInput").ap()
    out = nc.dram_tensor("out", (NB, SEQ, D), F32, kind="ExternalOutput").ap()
    build(nc, aps, out)
    r = _run(nc, [arrays], core_ids=[0])
    return r.results[0]["out"]
```
